# Optimizing a Trainium2 kernel written in Bass

```python
import numpy as np
import jax
import jax.numpy as jnp

def _softmax(x, axis=-1):
    return jax.nn.softmax(x, axis=axis)

def _gelu(x):
    return jax.nn.gelu(x, approximate=True)

def _silu(x):
    return jax.nn.silu(x)

def _sigmoid(x):
    return jax.nn.sigmoid(x)

def _layernorm(x, axis=-1, eps=1e-05):
    m = jnp.mean(x, axis=axis, keepdims=True)
    v = jnp.var(x, axis=axis, keepdims=True)
    return (x - m) / jnp.sqrt(v + eps)

def _scatter_add(tgt, idx, src, axis=0):
    return tgt.at[idx].add(src)

def _segment_sum(src, seg, n):
    return jax.ops.segment_sum(src, seg, n)
kernel_name = 'mk_macaron_d4_jaxref_r8_f13947'

def setup_inputs(seed: int=0):
    np.random.seed(seed)
    _w = jnp.asarray

    def _L0_attn_setup():
        import jax, jax.numpy as jnp
        import numpy as np
        import math
        D_MODEL = 128
        NUM_HEADS = 16
        D_K = D_MODEL // NUM_HEADS
        MAX_LEN = 256
        B, S = (2, 128)
        key = jax.random.key(seed)
        ks = jax.random.split(key, 10)
        lin_scale = 1.0 / math.sqrt(D_MODEL)
        Wq = jax.random.uniform(ks[0], (D_MODEL, D_MODEL), jnp.float32, -lin_scale, lin_scale)
        Wk = jax.random.uniform(ks[1], (D_MODEL, D_MODEL), jnp.float32, -lin_scale, lin_scale)
        Wv = jax.random.uniform(ks[2], (D_MODEL, D_MODEL), jnp.float32, -lin_scale, lin_scale)
        Wo = jax.random.uniform(ks[3], (D_MODEL, D_MODEL), jnp.float32, -lin_scale, lin_scale)
        bq = jnp.zeros((D_MODEL,), jnp.float32)
        bk = jnp.zeros((D_MODEL,), jnp.float32)
        bv = jnp.zeros((D_MODEL,), jnp.float32)
        bo = jnp.zeros((D_MODEL,), jnp.float32)
        er_bound = math.sqrt(6.0 / (MAX_LEN + D_K))
        Er = jax.random.uniform(ks[4], (MAX_LEN, D_K), jnp.float32, -er_bound, er_bound)
        x = jax.random.normal(ks[5], (B, S, D_MODEL), jnp.float32)
        return {'x': x, 'Wq': Wq, 'bq': bq, 'Wk': Wk, 'bk': bk, 'Wv': Wv, 'bv': bv, 'Wo': Wo, 'bo': bo, 'Er': Er}
    _L0_attn_in = _L0_attn_setup()

    def _L0_ffn_setup():
        import jax, jax.numpy as jnp
        import numpy as np
        MAX_VAL = 100.0
        key = jax.random.key(seed)
        k1, k2, k3 = jax.random.split(key, 3)
        B, S, D_IN, D_OUT = (4, 1024, 128, 128)
        x = jax.random.normal(k1, (B, S, D_IN), dtype=jnp.float32)
        weights = jax.random.normal(k2, (D_OUT, D_IN), dtype=jnp.float32)
        scale = jnp.ones((D_OUT,), dtype=jnp.float32)
        bias = jax.random.normal(k3, (D_OUT,), dtype=jnp.float32)
        return {'x': x, 'weights': weights, 'scale': scale, 'bias': bias}
    _L0_ffn_in = _L0_ffn_setup()

    def _L1_attn_setup():
        import jax, jax.numpy as jnp
        import numpy as np
        HEADS = 16
        DIM_HEAD = 64
        HEIGHT = 16
        KERNEL = 5
        DILATION = 1
        ALPHA = 32 ** 2

        def stable_softmax(t, axis=-1, alpha=ALPHA):
            t = t / alpha
            t = t - jax.lax.stop_gradient(jnp.max(t, axis=axis, keepdims=True))
            return jax.nn.softmax(t * alpha, axis=axis)
        key = jax.random.key(seed)
        ks = jax.random.split(key, 5)
        b, n, dim = (4, 4097, 128)
        inner = HEADS * DIM_HEAD
        x = jax.random.normal(ks[0], (b, n, dim), dtype=jnp.float32)
        w_qkv = jax.random.normal(ks[1], (dim, 3 * inner), dtype=jnp.float32) * dim ** (-0.5)
        w_out = jax.random.normal(ks[2], (inner, dim), dtype=jnp.float32) * inner ** (-0.5)
        b_out = jax.random.normal(ks[3], (dim,), dtype=jnp.float32) * 0.02
        w_th = jax.random.normal(ks[4], (HEADS, HEADS), dtype=jnp.float32) * HEADS ** (-0.5)
        return {'x': x, 'w_qkv': w_qkv, 'w_out': w_out, 'b_out': b_out, 'w_th': w_th}
    _L1_attn_in = _L1_attn_setup()

    def _L1_ffn_setup():
        import jax, jax.numpy as jnp
        import numpy as np
        B, S, H, E = (2, 1024, 128, 8)
        SCALE = 0.5
        key = jax.random.key(seed)
        k1, k2 = jax.random.split(key)
        x = jax.random.normal(k1, (B, S, H), dtype=jnp.float32)
        gate_w = jax.random.normal(k2, (E, H), dtype=jnp.float32) * 0.02
        coeff = SCALE * (1.0 + 0.05 * jnp.arange(E, dtype=jnp.float32))
        expert_w = coeff[:, None, None] * jnp.eye(H, dtype=jnp.float32)
        return {'x': x, 'gate_w': gate_w, 'expert_w': expert_w}
    _L1_ffn_in = _L1_ffn_setup()

    def _L2_attn_setup():
        import jax, jax.numpy as jnp
        import numpy as np
        DIM = 128
        key = jax.random.key(seed)
        kx, kw = jax.random.split(key)
        x = jax.random.normal(kx, (4, 256, DIM), dtype=jnp.float32)
        W_qkv = jax.random.normal(kw, (3 * DIM, DIM), dtype=jnp.float32) * DIM ** (-0.5)
        return {'x': x, 'W_qkv': W_qkv}
    _L2_attn_in = _L2_attn_setup()

    def _L2_ffn_setup():
        import jax, jax.numpy as jnp
        import numpy as np
        B, S, D = (2, 256, 128)
        E, K, F = (16, 2, 64)
        FS = 128
        key = jax.random.key(seed)
        ks = jax.random.split(key, 8)

        def w(k, shape, fan_in):
            return jax.random.normal(k, shape, jnp.float32) / np.sqrt(fan_in).astype(np.float32)
        return {'x': jax.random.normal(ks[0], (B, S, D), jnp.float32), 'Wr': w(ks[1], (D, E), D), 'Wg': w(ks[2], (E, D, F), D), 'Wu': w(ks[3], (E, D, F), D), 'Wd': w(ks[4], (E, F, D), F), 'Sg': w(ks[5], (D, FS), D), 'Su': w(ks[6], (D, FS), D), 'Sd': w(ks[7], (FS, D), FS)}
    _L2_ffn_in = _L2_ffn_setup()

    def _L3_attn_setup():
        import jax, jax.numpy as jnp
        import numpy as np

        def apply_rope(x):
            b, h, n, d = x.shape
            half = d // 2
            freqs = jnp.arange(0, half, dtype=x.dtype) / half
            theta = 1.0 / 1250 ** freqs
            positions = jnp.arange(n, dtype=x.dtype)
            angles = positions[:, None] * theta[None, :]
            cos = jnp.cos(angles)[None, None, :, :]
            sin = jnp.sin(angles)[None, None, :, :]
            x1 = x[..., ::2]
            x2 = x[..., 1::2]
            r1 = x1 * cos - x2 * sin
            r2 = x1 * sin + x2 * cos
            return jnp.stack([r1, r2], axis=-1).reshape(b, h, n, d)
        key = jax.random.key(seed)
        ks = jax.random.split(key, 4)
        B, N, D = (2, 256, 128)
        x = jax.random.normal(ks[0], (B, N, D), dtype=jnp.float32)
        w_qkv = jax.random.normal(ks[1], (D, 3 * D), dtype=jnp.float32) * (1.0 / np.sqrt(D))
        b_qkv = jnp.zeros((3 * D,), dtype=jnp.float32)
        w_out = jax.random.normal(ks[2], (D, D), dtype=jnp.float32) * (1.0 / np.sqrt(D))
        b_out = jnp.zeros((D,), dtype=jnp.float32)
        return {'x': x, 'w_qkv': w_qkv, 'b_qkv': b_qkv, 'w_out': w_out, 'b_out': b_out}
    _L3_attn_in = _L3_attn_setup()

    def _L3_ffn_setup():
        import jax, jax.numpy as jnp
        import numpy as np
        DIM = 128
        HIDDEN = 384
        SCALE = 1.0 / 127.0

        def _dequant(w_int, dtype):
            return w_int.astype(dtype) * jnp.asarray(SCALE, dtype)
        key = jax.random.key(seed)
        k_x, k_g, k_u, k_d = jax.random.split(key, 4)
        x = jax.random.normal(k_x, (4, 256, DIM), dtype=jnp.float32)
        w_gate = jax.random.randint(k_g, (HIDDEN, DIM), -127, 128, dtype=jnp.int32)
        w_up = jax.random.randint(k_u, (HIDDEN, DIM), -127, 128, dtype=jnp.int32)
        w_down = jax.random.randint(k_d, (DIM, HIDDEN), -127, 128, dtype=jnp.int32)
        return {'x': x, 'w_gate': w_gate, 'w_up': w_up, 'w_down': w_down}
    _L3_ffn_in = _L3_ffn_setup()
    _d = {'L0_attn_x': _L0_attn_in['x'], 'L0_attn_Wq': _L0_attn_in['Wq'], 'L0_attn_bq': _L0_attn_in['bq'], 'L0_attn_Wk': _L0_attn_in['Wk'], 'L0_attn_bk': _L0_attn_in['bk'], 'L0_attn_Wv': _L0_attn_in['Wv'], 'L0_attn_bv': _L0_attn_in['bv'], 'L0_attn_Wo': _L0_attn_in['Wo'], 'L0_attn_bo': _L0_attn_in['bo'], 'L0_attn_Er': _L0_attn_in['Er'], 'L0_ffn_weights': _L0_ffn_in['weights'], 'L0_ffn_scale': _L0_ffn_in['scale'], 'L0_ffn_bias': _L0_ffn_in['bias'], 'L1_attn_w_qkv': _L1_attn_in['w_qkv'], 'L1_attn_w_out': _L1_attn_in['w_out'], 'L1_attn_b_out': _L1_attn_in['b_out'], 'L1_attn_w_th': _L1_attn_in['w_th'], 'L1_ffn_gate_w': _L1_ffn_in['gate_w'], 'L1_ffn_expert_w': _L1_ffn_in['expert_w'], 'L2_attn_W_qkv': _L2_attn_in['W_qkv'], 'L2_ffn_Wr': _L2_ffn_in['Wr'], 'L2_ffn_Wg': _L2_ffn_in['Wg'], 'L2_ffn_Wu': _L2_ffn_in['Wu'], 'L2_ffn_Wd': _L2_ffn_in['Wd'], 'L2_ffn_Sg': _L2_ffn_in['Sg'], 'L2_ffn_Su': _L2_ffn_in['Su'], 'L2_ffn_Sd': _L2_ffn_in['Sd'], 'L3_attn_w_qkv': _L3_attn_in['w_qkv'], 'L3_attn_b_qkv': _L3_attn_in['b_qkv'], 'L3_attn_w_out': _L3_attn_in['w_out'], 'L3_attn_b_out': _L3_attn_in['b_out'], 'L3_ffn_w_gate': _L3_ffn_in['w_gate'], 'L3_ffn_w_up': _L3_ffn_in['w_up'], 'L3_ffn_w_down': _L3_ffn_in['w_down']}
    _x0 = _d['L0_attn_x']
    _d['L0_attn_x'] = jax.random.normal(jax.random.fold_in(jax.random.key(seed), 1), (32, 256, 128), dtype=_x0.dtype)
    del _x0
    return _d

def reference(L0_attn_x, L0_attn_Wq, L0_attn_bq, L0_attn_Wk, L0_attn_bk, L0_attn_Wv, L0_attn_bv, L0_attn_Wo, L0_attn_bo, L0_attn_Er, L0_ffn_weights, L0_ffn_scale, L0_ffn_bias, L1_attn_w_qkv, L1_attn_w_out, L1_attn_b_out, L1_attn_w_th, L1_ffn_gate_w, L1_ffn_expert_w, L2_attn_W_qkv, L2_ffn_Wr, L2_ffn_Wg, L2_ffn_Wu, L2_ffn_Wd, L2_ffn_Sg, L2_ffn_Su, L2_ffn_Sd, L3_attn_w_qkv, L3_attn_b_qkv, L3_attn_w_out, L3_attn_b_out, L3_ffn_w_gate, L3_ffn_w_up, L3_ffn_w_down):

    def _L0_attn_ref(x, Wq, bq, Wk, bk, Wv, bv, Wo, bo, Er):
        import jax, jax.numpy as jnp
        import numpy as np
        import math
        D_MODEL = 128
        NUM_HEADS = 16
        D_K = D_MODEL // NUM_HEADS
        MAX_LEN = 256
        B, S = (2, 128)
        Bsz, Slen, Dm = x.shape
        H, dk = (NUM_HEADS, D_K)

        def proj(W, b):
            y = jnp.einsum('bsd,ed->bse', x, W) + b
            return y.reshape(Bsz, Slen, H, dk).transpose(0, 2, 1, 3)
        Q = proj(Wq, bq)
        K = proj(Wk, bk)
        V = proj(Wv, bv)
        AC = jnp.einsum('bhid,bhjd->bhij', Q, K)
        rel_pos = jnp.arange(Slen - 1, -Slen, -1)
        idx = rel_pos + (Slen - 1)
        Er_emb = Er[idx]
        BD_full = jnp.einsum('bhid,md->bhim', Q, Er_emb)
        i_idx = jnp.arange(Slen)[:, None]
        m_idx = Slen - 1 - i_idx + jnp.arange(Slen)[None, :]
        BD = BD_full[:, :, i_idx, m_idx]
        scores = (AC + BD) / math.sqrt(dk)
        attn = jax.nn.softmax(scores, axis=-1)
        out = jnp.einsum('bhij,bhjd->bhid', attn, V)
        out = out.transpose(0, 2, 1, 3).reshape(Bsz, Slen, Dm)
        return jnp.einsum('bsd,ed->bse', out, Wo) + bo

    def _L0_ffn_ref(x, weights, scale, bias):
        import jax, jax.numpy as jnp
        import numpy as np
        MAX_VAL = 100.0
        w = (weights >= 0.0).astype(x.dtype) * 2.0 - 1.0
        y = jnp.einsum('bsi,oi->bso', x, w)
        y = y * scale + bias
        y = jnp.clip(y, -MAX_VAL, MAX_VAL)
        return y

    def _L1_attn_ref(x, w_qkv, w_out, b_out, w_th):
        import jax, jax.numpy as jnp
        import numpy as np
        HEADS = 16
        DIM_HEAD = 64
        HEIGHT = 16
        KERNEL = 5
        DILATION = 1
        ALPHA = 32 ** 2

        def stable_softmax(t, axis=-1, alpha=ALPHA):
            t = t / alpha
            t = t - jax.lax.stop_gradient(jnp.max(t, axis=axis, keepdims=True))
            return jax.nn.softmax(t * alpha, axis=axis)
        b, n, dim = x.shape
        h, d = (HEADS, DIM_HEAD)
        height, K, dil = (HEIGHT, KERNEL, DILATION)
        pad = dil * (K - 1) // 2
        scale = d ** (-0.5)
        kernel_numel = K * height
        seq_pad = -(n - 1) % height
        xp = jnp.pad(x, ((0, 0), (0, seq_pad), (0, 0))) if seq_pad > 0 else x
        qkv = xp @ w_qkv
        q, k, v = jnp.split(qkv, 3, axis=-1)
        if n == 1:
            return v @ w_out + b_out
        out_bos = v[:, :1]

        def to_heads(t):
            return t.reshape(b, -1, h, d).transpose(0, 2, 1, 3)
        q, k, v = map(to_heads, (q, k, v))
        q = q * scale
        k_bos, k = (k[:, :, 0], k[:, :, 1:])
        v_bos, v = (v[:, :, 0], v[:, :, 1:])
        q = q[:, :, 1:]
        X = q.shape[2] // height
        k = k.reshape(b, h, X, height, d)
        v = v.reshape(b, h, X, height, d)
        kp = jnp.pad(k, ((0, 0), (0, 0), (pad, pad), (0, 0), (0, 0)))
        vp = jnp.pad(v, ((0, 0), (0, 0), (pad, pad), (0, 0), (0, 0)))
        idx = jnp.arange(X)[:, None] + jnp.arange(K)[None, :] * dil
        kw = kp[:, :, idx].reshape(b, h, X, kernel_numel, d)
        vw = vp[:, :, idx].reshape(b, h, X, kernel_numel, d)
        kb = jnp.broadcast_to(k_bos[:, :, None, None, :], (b, h, X, 1, d))
        vb = jnp.broadcast_to(v_bos[:, :, None, None, :], (b, h, X, 1, d))
        kw = jnp.concatenate([kb, kw], axis=3)
        vw = jnp.concatenate([vb, vw], axis=3)
        qw = q.reshape(b, h, X, height, d)
        sim = jnp.einsum('bhnid,bhnjd->bhnij', qw, kw)
        seq_len = X * height
        q_range = jnp.arange(seq_len).reshape(X, height)
        k_range = jnp.pad(jnp.arange(seq_len).reshape(X, height), ((pad, pad), (0, 0)), constant_values=seq_len)
        kr = k_range[idx].reshape(X, kernel_numel)
        mask = q_range[:, :, None] < kr[:, None, :]
        mask = jnp.pad(mask, ((0, 0), (0, 0), (1, 0)), constant_values=False)
        mask_value = -jnp.finfo(sim.dtype).max
        sim = jnp.where(mask[None, None], mask_value, sim)
        attn = stable_softmax(sim, axis=-1)
        attn = jnp.einsum('gh,bhnij->bgnij', w_th, attn)
        out = jnp.einsum('bhnij,bhnjd->bhnid', attn, vw)
        out = out.transpose(0, 2, 3, 1, 4).reshape(b, X * height, h * d)
        out = jnp.concatenate([out_bos, out], axis=1)
        return (out @ w_out + b_out)[:, :n]

    def _L1_ffn_ref(x, gate_w, expert_w):
        import jax, jax.numpy as jnp
        import numpy as np
        B, S, H, E = (2, 1024, 128, 8)
        SCALE = 0.5
        scores = jnp.einsum('bsh,eh->bse', x, gate_w)
        chosen = jnp.argmax(scores, axis=-1)
        onehot = jax.nn.one_hot(chosen, gate_w.shape[0], dtype=x.dtype)
        expert_out = jnp.einsum('bsh,efh->bsef', x, expert_w)
        return x + jnp.einsum('bsef,bse->bsf', expert_out, onehot)

    def _L2_attn_ref(x, W_qkv):
        import jax, jax.numpy as jnp
        import numpy as np
        DIM = 128
        qkv = jnp.einsum('bnd,ed->bne', x, W_qkv)
        B, N, _ = qkv.shape
        qkv = qkv.reshape(B, N, 3, DIM).transpose(2, 0, 1, 3)
        q, k, v = (qkv[0], qkv[1], qkv[2])
        scale = DIM ** (-0.5)
        attn = jnp.einsum('bnd,bmd->bnm', q * scale, k)
        attn = jax.nn.softmax(attn, axis=-1)
        out = jnp.einsum('bnm,bmd->bnd', attn, v)
        return out

    def _L2_ffn_ref(x, Wr, Wg, Wu, Wd, Sg, Su, Sd):
        import jax, jax.numpy as jnp
        import numpy as np
        B, S, D = (2, 256, 128)
        E, K, F = (16, 2, 64)
        FS = 128
        b, s, d = x.shape
        T = b * s
        xf = x.reshape(T, d)
        shared = jax.nn.silu(xf @ Sg) * (xf @ Su) @ Sd
        probs = jax.nn.softmax(xf @ Wr, axis=-1)
        topk_p, topk_i = jax.lax.top_k(probs, K)
        n_exp = Wr.shape[1]
        cw = jnp.zeros((T, n_exp), x.dtype).at[jnp.arange(T)[:, None], topk_i].add(topk_p)

        def step(acc, ew):
            wg, wu, wd, c = ew
            y = jax.nn.silu(xf @ wg) * (xf @ wu) @ wd
            return (acc + y * c[:, None], None)
        routed, _ = jax.lax.scan(step, jnp.zeros_like(xf), (Wg, Wu, Wd, cw.T))
        return (routed + shared).reshape(b, s, d)

    def _L3_attn_ref(x, w_qkv, b_qkv, w_out, b_out):
        import jax, jax.numpy as jnp
        import numpy as np

        def apply_rope(x):
            b, h, n, d = x.shape
            half = d // 2
            freqs = jnp.arange(0, half, dtype=x.dtype) / half
            theta = 1.0 / 1250 ** freqs
            positions = jnp.arange(n, dtype=x.dtype)
            angles = positions[:, None] * theta[None, :]
            cos = jnp.cos(angles)[None, None, :, :]
            sin = jnp.sin(angles)[None, None, :, :]
            x1 = x[..., ::2]
            x2 = x[..., 1::2]
            r1 = x1 * cos - x2 * sin
            r2 = x1 * sin + x2 * cos
            return jnp.stack([r1, r2], axis=-1).reshape(b, h, n, d)
        B, N, D = x.shape
        H = 16
        hd = D // H
        qkv = x @ w_qkv + b_qkv
        q, k, v = jnp.split(qkv, 3, axis=-1)
        to_heads = lambda t: t.reshape(B, N, H, hd).transpose(0, 2, 1, 3)
        q, k, v = (to_heads(q), to_heads(k), to_heads(v))
        q = jax.nn.elu(q) + 1
        k = jax.nn.elu(k) + 1
        rot_q = apply_rope(q)
        rot_k = apply_rope(k)
        attn_num = jnp.einsum('bhid,bhjd->bhij', rot_q, rot_k)
        attn_denom = jnp.einsum('bhid,bhjd->bhij', q, k)
        attn_weights = attn_num / attn_denom
        out = jnp.einsum('bhij,bhjd->bhid', attn_weights, v)
        out = out.transpose(0, 2, 1, 3).reshape(B, N, D)
        return out @ w_out + b_out

    def _L3_ffn_ref(x, w_gate, w_up, w_down):
        import jax, jax.numpy as jnp
        import numpy as np
        DIM = 128
        HIDDEN = 384
        SCALE = 1.0 / 127.0

        def _dequant(w_int, dtype):
            return w_int.astype(dtype) * jnp.asarray(SCALE, dtype)
        wg = _dequant(w_gate, x.dtype)
        wu = _dequant(w_up, x.dtype)
        wd = _dequant(w_down, x.dtype)
        gate = jnp.einsum('bsd,hd->bsh', x, wg)
        up = jnp.einsum('bsd,hd->bsh', x, wu)
        h = jax.nn.silu(gate) * up
        return jnp.einsum('bsh,dh->bsd', h, wd)
    x = L0_attn_x
    x = x + 0.5 * _L0_ffn_ref(_layernorm(x, axis=-1), L0_ffn_weights, L0_ffn_scale, L0_ffn_bias)
    x = x + _L0_attn_ref(_layernorm(x, axis=-1), L0_attn_Wq, L0_attn_bq, L0_attn_Wk, L0_attn_bk, L0_attn_Wv, L0_attn_bv, L0_attn_Wo, L0_attn_bo, L0_attn_Er)
    x = x + 0.5 * _L0_ffn_ref(_layernorm(x, axis=-1), L0_ffn_weights, L0_ffn_scale, L0_ffn_bias)
    x = x + 0.5 * _L1_ffn_ref(_layernorm(x, axis=-1), L1_ffn_gate_w, L1_ffn_expert_w)
    x = x + _L1_attn_ref(_layernorm(x, axis=-1), L1_attn_w_qkv, L1_attn_w_out, L1_attn_b_out, L1_attn_w_th)
    x = x + 0.5 * _L1_ffn_ref(_layernorm(x, axis=-1), L1_ffn_gate_w, L1_ffn_expert_w)
    x = x + 0.5 * _L2_ffn_ref(_layernorm(x, axis=-1), L2_ffn_Wr, L2_ffn_Wg, L2_ffn_Wu, L2_ffn_Wd, L2_ffn_Sg, L2_ffn_Su, L2_ffn_Sd)
    x = x + _L2_attn_ref(_layernorm(x, axis=-1), L2_attn_W_qkv)
    x = x + 0.5 * _L2_ffn_ref(_layernorm(x, axis=-1), L2_ffn_Wr, L2_ffn_Wg, L2_ffn_Wu, L2_ffn_Wd, L2_ffn_Sg, L2_ffn_Su, L2_ffn_Sd)
    x = x + 0.5 * _L3_ffn_ref(_layernorm(x, axis=-1), L3_ffn_w_gate, L3_ffn_w_up, L3_ffn_w_down)
    x = x + _L3_attn_ref(_layernorm(x, axis=-1), L3_attn_w_qkv, L3_attn_b_qkv, L3_attn_w_out, L3_attn_b_out)
    x = x + 0.5 * _L3_ffn_ref(_layernorm(x, axis=-1), L3_ffn_w_gate, L3_ffn_w_up, L3_ffn_w_down)
    return x

_drawn_inputs = setup_inputs


def setup_inputs(seed=0):
    import zlib

    import numpy as np

    out = dict(_drawn_inputs(seed))
    spreads = {'L0_attn_bq': (0.0, 0.8),
     'L0_attn_bk': (0.0, 0.8),
     'L0_attn_bv': (0.0, 0.496),
     'L0_attn_bo': (0.0, 0.295),
     'L0_ffn_scale': (1.0, 0.2),
     'L3_attn_b_qkv': (0.0, 0.1),
     'L3_attn_b_out': (0.0, 0.8)}
    factors = {'L0_attn_Wq': 8.0,
     'L0_attn_Wk': 8.0,
     'L0_attn_Wv': 4.479,
     'L0_attn_Wo': 2.733,
     'L0_attn_Er': 8.0,
     'L1_attn_b_out': 8.0,
     'L1_ffn_gate_w': 8.0}
    for name, (base, spread) in spreads.items():
        noise = np.random.default_rng([zlib.crc32(name.encode()), seed]).standard_normal(out[name].shape)
        drawn = base * np.exp(spread * noise) if base else spread * noise
        out[name] = jnp.asarray(drawn.astype(out[name].dtype))
    for name, factor in factors.items():
        out[name] = (out[name] * factor).astype(out[name].dtype)
    return out
```

```python
from contextlib import ExitStack

import numpy as np
import concourse.bass as bass
from concourse import mybir

F32 = mybir.dt.float32
I32 = mybir.dt.int32
ALU = mybir.AluOpType
ACT = mybir.ActivationFunctionType
AX = mybir.AxisListType

P = 128
S = 256
HEADS = 16
DK = P // HEADS
EPS = 1e-5
NEG = -1e30
WIN = 17
ROWS = S // 16 + 2
STAGES = list(range(12))

WQ0, WK0, WV0, WO0, WF0, WE1, WQ2, WK2, WV2, WG3, WU3, WD3, GW1, NWT = 0, 1, 2, 3, 4, 5, 13, 14, 15, 16, 19, 22, 25, 26
B_F0, B_V0, B_O0, B_O1, B_V3, B_O3, NBIAS = 0, 1, 2, 3, 4, 5, 6


def constants():
    part = np.arange(P)
    out = {}
    out["ident"] = np.eye(P)
    i = np.arange(S)
    out["head_of"] = (part[:, None] // DK == np.arange(HEADS)[None, :])
    out["step_of"] = (i[None, :] % 8 == (part[:, None] // DK) % 8)
    out["step8"] = (part[:, None] % 8 == np.arange(8)[None, :])
    out["spread_heads"] = (np.arange(HEADS)[:, None] == part[None, :] // 8)
    out["quad"] = ((part[:, None] // DK) % 4 == np.arange(4)[None, :])
    theta = 1.0 / 1250.0 ** ((part % DK) // 2 / (DK // 2))
    ang = (np.arange(S, dtype=np.float32)[None, :] * theta.astype(np.float32)[:, None]).astype(np.float32)
    out["cos"] = np.tile(np.cos(ang), (1, 2))
    out["sin"] = np.tile(np.sin(ang), (1, 2))
    swap = np.zeros((P, P))
    for m in range(P):
        swap[m + 1 if m % 2 == 0 else m - 1, m] = -1.0 if m % 2 == 0 else 1.0
    out["swap"] = swap
    out["rank8"] = np.tile(8.0 - np.arange(8), (P, 1))
    out["rank16"] = np.tile(16.0 - np.arange(16), (P, 1))
    sel = np.zeros((P, 8, P))
    for e in range(16):
        sel[e, e // 2, 64 * (e % 2):64 * (e % 2) + 64] = 1
    out["pick_expert"] = sel.reshape(P, -1)
    mask = np.zeros((P, 2, 8, 3, WIN))
    for first in range(2):
        for u in range(8):
            x = u // 2 if first == 0 else 4 + u // 2
            for p in range(P):
                n = 8 * (u % 2) + p % 8
                mask[p, first, u, :2, 0] = NEG
                for slot in range(3):
                    if x - 2 + slot < 0:
                        mask[p, first, u, slot, 1:] = NEG
                mask[p, first, u, 2, 2 + n:] = NEG
    out["window"] = mask.reshape(P, -1)
    back = np.zeros((2, P, 2 * S))
    for c in range(2 * S - 1):
        r = min(S - 1, 2 * S - 2 - c)
        back[r // P, r % P, c] = 1
    out["back0"], out["back1"] = back[0], back[1]
    at, cols, parts = {}, 0, []
    for name, a in out.items():
        a = np.asarray(a, np.float32)
        if a.shape[0] < P:
            a = np.concatenate([a, np.zeros((P - a.shape[0], a.shape[1]), np.float32)])
        at[name] = (cols, a.shape[1])
        cols += a.shape[1]
        parts.append(a)
    return np.ascontiguousarray(np.concatenate(parts, 1)), at


CONST, CONST_AT = constants()


class Signal:

    def __init__(self, nc, name, per=1):
        self.sem, self.per = nc.alloc_semaphore(name=name), per

    def at(self, t, k):
        return t * self.per + k


class Chain:

    def __init__(self, eng, steps, t):
        self.eng, self.steps, self.t, self.n = eng, steps, t, 0

    def did(self, ins):
        self.n += 1
        ins.then_inc(self.steps.sem, 1)

    def settle(self):
        self.eng.wait_ge(self.steps.sem, self.steps.at(self.t, self.n))

    def end(self):
        assert self.n == self.steps.per, (self.n, self.steps.per)


def network(nc, ins, out):
    NB = ins["L0_attn_x"].shape[0]
    x_dram = ins["L0_attn_x"].rearrange("b (h p) d -> p (b h) d", p=P)
    out_dram = out.rearrange("b (h p) d -> p (b h) d", p=P)
    ctx = ExitStack()
    with ctx:
        def sb(name, shape, dt=F32):
            return ctx.enter_context(nc.sbuf_tensor(name, shape, dt))

        bank = [ctx.enter_context(nc.psum_tensor(f"bank{i}", [P, 512], F32)) for i in range(8)]
        x_all = sb("x_all", [P, NB * 2 * P])
        wt = sb("wt", [P, NWT, P])
        small = {n: CONST_AT[n] for n in CONST_AT if n not in ("back0", "back1")}
        const_cols = CONST_AT["back0"][0]
        const = sb("const", [P, const_cols])
        bias_row = sb("bias_row", [1, NBIAS * P])
        ones_row = sb("ones_row", [1, P])
        col = sb("col", [P, 16])
        wqx = sb("wqx", [P, 8, P])
        er_win = sb("er_win", [P, 2 * S - 8])
        mix = sb("mix", [P, HEADS, 8])
        wqkv1 = sb("wqkv1", [P, 3 * 1024])
        wout1 = sb("wout1", [P, 8, P])
        wg2 = sb("wg2", [P, 16, 64])
        wu2 = sb("wu2", [P, 16, 64])
        wd2 = sb("wd2", [P, 9, P])
        sgu2 = sb("sgu2", [P, 2, P])
        wr2 = sb("wr2", [P, 16])
        wqkv3 = sb("wqkv3", [P, 3 * P])
        wout3 = sb("wout3", [P, P])
        g = dict(locals())

        def c(name):
            a, n = small[name]
            return const[:, a:a + n]

        g["c"] = c
        with nc.cleanup_on_exit():
            setup(nc, ins, g)
        stages = [("ffn0",), ("att0",), ("ffn0",), ("ffn1",), ("att1",), ("ffn1",),
                  ("ffn2",), ("att2",), ("ffn2",), ("ffn3",), ("att3",), ("ffn3",)]
        build = {"ffn0": ffn0, "att0": att0, "ffn1": ffn1, "att1": att1, "ffn2": ffn2, "att2": att2,
                 "ffn3": ffn3, "att3": att3}
        for n in STAGES:
            with nc.cleanup_on_exit():
                build[stages[n][0]](nc, g, NB, f"{stages[n][0]}_{n}_")
        with nc.cleanup_on_exit():
            stored = Signal(nc, "stored")
            with nc.Block() as block:
                @block.sync
                def _(sp):
                    xv = x_all[:, :].rearrange("p (t d) -> p t d", d=P)
                    half = NB
                    sp.dma_start(out_dram[:, 0:half, :], xv[:, 0:half, :]).then_inc(stored.sem, 16)
                    sp.dma_start(out_dram[:, half:, :], xv[:, half:, :]).then_inc(stored.sem, 16)
                    sp.wait_ge(stored.sem, 32)


def setup(nc, ins, g):
    wt, const, bias_row, ones_row, col, c = (g[k] for k in ("wt", "const", "bias_row", "ones_row", "col", "c"))
    bank, wqx, er_win, mix, wd2, x_all = (g[k] for k in ("bank", "wqx", "er_win", "mix", "wd2", "x_all"))
    with ExitStack() as ctx:
        def sb(name, shape, dt=F32):
            return ctx.enter_context(nc.sbuf_tensor(name, shape, dt))

        raw = sb("raw", [P, NWT, P])
        raw_int = sb("raw_int", [P, 9, P], I32)
        scale0 = sb("scale0", [P, 1])
        er = sb("er", [P, 2, DK])
        er_rep = sb("er_rep", [P, 2, HEADS, DK])
        back = sb("back", [P, 2, 2 * S])
        er_rev = sb("er_rev", [P, 2 * S])
        thT = sb("thT", [HEADS, HEADS])
        th_rep = sb("th_rep", [P, HEADS])
        half_ident = sb("half_ident", [P, P])
        loaded, x_in, prepared, turned, moved, chain = (Signal(nc, n) for n in (
            "loaded", "x_in", "prepared", "turned", "moved", "chain"))
        small_ps, er_ready, shifted = (Signal(nc, n) for n in ("small_ps", "er_ready", "shifted"))
        loads = []

        def blocks(name):
            return ins[name].rearrange("(t p) d -> p t d", p=P)

        loads.append((const[:, :], ins["const"][:, 0:g["const_cols"]]))
        loads.append((back[:, :, :], ins["const"][:, g["const_cols"]:].rearrange("p (t c) -> p t c", t=2)))
        for n, name in ((WQ0, "L0_attn_Wq"), (WK0, "L0_attn_Wk"), (WV0, "L0_attn_Wv"), (WO0, "L0_attn_Wo"), (WF0, "L0_ffn_weights")):
            loads.append((raw[:, n, :], ins[name]))
        loads.append((raw[:, WE1:WE1 + 8, :], ins["L1_ffn_expert_w"].rearrange("e f h -> f e h")))
        loads.append((raw[:, WQ2:WQ2 + 3, :], blocks("L2_attn_W_qkv")))
        loads.append((raw[0:8, GW1, :], ins["L1_ffn_gate_w"]))
        loads.append((raw_int[:, 0:3, :], blocks("L3_ffn_w_gate")))
        loads.append((raw_int[:, 3:6, :], blocks("L3_ffn_w_up")))
        loads.append((raw_int[:, 6:9, :], ins["L3_ffn_w_down"].rearrange("d (t h) -> d t h", t=3)))
        for n, name in ((B_F0, "L0_ffn_bias"), (B_V0, "L0_attn_bv"), (B_O0, "L0_attn_bo"), (B_O1, "L1_attn_b_out"), (B_O3, "L3_attn_b_out")):
            loads.append((bias_row[:, n * P:(n + 1) * P], ins[name].rearrange("(a d) -> a d", a=1)))
        loads.append((bias_row[:, B_V3 * P:(B_V3 + 1) * P], ins["L3_attn_b_qkv"][2 * P:3 * P].rearrange("(a d) -> a d", a=1)))
        loads.append((scale0[:, :], ins["L0_ffn_scale"].rearrange("(d a) -> d a", a=1)))
        loads.append((col[:, 8:9], ins["L0_attn_bq"].rearrange("(d a) -> d a", a=1)))
        loads.append((col[:, 9:10], ins["L0_attn_bk"].rearrange("(d a) -> d a", a=1)))
        loads.append((col[:, 10:12], ins["L3_attn_b_qkv"][0:2 * P].rearrange("(a d) -> d a", a=2)))
        for par in range(2):
            for i in range(8):
                loads.append((col[64 * par + 8 * i:64 * par + 8 * i + 8, 0:8],
                              ins["L0_attn_bq"][64 * par:64 * par + 64].rearrange("(h d) -> d h", d=DK)))
        loads.append((er[:, :, :], ins["L0_attn_Er"].rearrange("(t p) d -> p t d", p=P)))
        loads.append((thT[:, :], ins["L1_attn_w_th"].rearrange("g h -> h g")))
        loads.append((g["wqkv1"][:, :], ins["L1_attn_w_qkv"]))
        loads.append((g["wout1"][:, :, :], ins["L1_attn_w_out"].rearrange("(t p) d -> p t d", p=P)))
        loads.append((g["wg2"][:, :, :], ins["L2_ffn_Wg"].rearrange("e d f -> d e f")))
        loads.append((g["wu2"][:, :, :], ins["L2_ffn_Wu"].rearrange("e d f -> d e f")))
        loads.append((wd2[:, 0:8, :], ins["L2_ffn_Wd"].rearrange("(t e) f d -> (e f) t d", e=2)))
        loads.append((wd2[:, 8, :], ins["L2_ffn_Sd"]))
        loads.append((g["sgu2"][:, 0, :], ins["L2_ffn_Sg"]))
        loads.append((g["sgu2"][:, 1, :], ins["L2_ffn_Su"]))
        loads.append((g["wr2"][:, :], ins["L2_ffn_Wr"]))
        loads.append((g["wqkv3"][:, :], ins["L3_attn_w_qkv"]))
        loads.append((g["wout3"][:, :], ins["L3_attn_w_out"]))
        NL = len(loads)

        with nc.Block() as block:
            @block.sync
            def _(sp):
                for n, (dst, src) in enumerate(loads):
                    sp.dma_start(dst, src, allow_slow_non_contiguous=True).then_inc(loaded.sem, 16)
                sp.wait_ge(er_ready.sem, 1)
                for par in range(2):
                    for i in range(8):
                        rows = slice(64 * par + 8 * i, 64 * par + 8 * i + 8)
                        sp.dma_start(er_win[rows, :], er_rev[rows, 7 - i:7 - i + 2 * S - 8]).then_inc(shifted.sem, 16)
                sp.wait_ge(shifted.sem, 16 * 16)

            @block.scalar
            def _(act):
                act.dma_start(x_all[:, :].rearrange("p (t d) -> p t d", d=P), g["x_dram"]).then_inc(x_in.sem, 16)
                act.wait_ge(x_in.sem, 16)

            @block.vector
            def _(dve):
                n = [0]

                def did(ins_):
                    n[0] += 1
                    ins_.then_inc(chain.sem, 1)

                def settle():
                    dve.wait_ge(chain.sem, n[0])

                did(dve.memset(ones_row[:, :], 1.0))
                dve.wait_ge(loaded.sem, 16 * NL)
                did(dve.tensor_copy(raw[:, WG3:WG3 + 9, :], raw_int[:, :, :]))
                did(dve.tensor_scalar(raw[:, WF0, :], raw[:, WF0, :], 0.0, 2.0, ALU.is_ge, ALU.mult))
                did(dve.tensor_scalar(half_ident[:, :], c("ident"), 0.5, None, ALU.mult))
                did(dve.tensor_scalar(raw[:, WQ0, :], raw[:, WQ0, :], DK ** -0.5, None, ALU.mult))
                did(dve.tensor_scalar(col[:, 0:9], col[:, 0:9], DK ** -0.5, None, ALU.mult))
                did(dve.tensor_scalar(raw[:, WQ2, :], raw[:, WQ2, :], P ** -0.5, None, ALU.mult))
                did(dve.tensor_scalar(g["wqkv1"][:, 0:1024], g["wqkv1"][:, 0:1024], 64 ** -0.5, None, ALU.mult))
                did(dve.tensor_scalar(wd2[:, :, :], wd2[:, :, :], 0.25, None, ALU.mult))
                for t in range(2):
                    did(dve.tensor_copy(er_rep[:, t, :, :], er[:, t:t + 1, :].broadcast_to([P, HEADS, DK])))
                settle()
                did(dve.tensor_scalar(raw[:, WG3:WG3 + 9, :], raw[:, WG3:WG3 + 9, :], float(np.float32(1.0 / 127.0)), None, ALU.mult))
                did(dve.tensor_scalar(raw[:, WF0, :], raw[:, WF0, :], 1.0, scale0[:, 0:1], ALU.subtract, ALU.mult))
                for e in range(8):
                    did(dve.scalar_tensor_tensor(out=raw[:, WE1 + e, :], in0=raw[:, WE1 + e, :], scalar=0.5,
                                                 in1=half_ident[:, :], op0=ALU.mult, op1=ALU.add))
                settle()
                did(dve.tensor_scalar(raw[:, WD3:WD3 + 3, :], raw[:, WD3:WD3 + 3, :], 0.25, None, ALU.mult))
                settle()
                dve.memset(half_ident[0:1, 0:1], 0.5).then_inc(prepared.sem, 1)
                for b in range(7):
                    lo, hi = 4 * b, min(4 * b + 4, NWT)
                    dve.wait_ge(turned.sem, b + 1)
                    if hi == NWT:
                        did(dve.tensor_copy(wt[:, lo:lo + 1, :], bank[b][:, 0:P].rearrange("p (t d) -> p t d", d=P)))
                        did(dve.tensor_copy(wt[:, GW1, 0:8], bank[b][:, P:P + 8]))
                    else:
                        did(dve.tensor_copy(wt[:, lo:hi, :], bank[b][:, :].rearrange("p (t d) -> p t d", d=P)))
                dve.wait_ge(small_ps.sem, 1)
                did(dve.tensor_copy(th_rep[:, :], bank[7][:, 0:HEADS]))
                settle()
                did(dve.tensor_tensor(mix[:, :, :], th_rep[:, :].unsqueeze(2).broadcast_to([P, HEADS, 8]),
                                      c("step8").unsqueeze(1).broadcast_to([P, HEADS, 8]), ALU.mult))
                for hp in range(8):
                    for par in range(2):
                        h = par * 8 + hp
                        did(dve.tensor_copy(wqx[:, hp, 64 * par:64 * par + 64].rearrange("p (i d) -> p i d", d=DK),
                                            wt[:, WQ0:WQ0 + 1, DK * h:DK * h + DK].broadcast_to([P, 8, DK])))
                settle()
                dve.memset(half_ident[0:1, 0:1], 0.5).then_inc(moved.sem, 1)
                dve.wait_ge(small_ps.sem, 2)
                dve.tensor_copy(er_rev[:, :], bank[6][:, :]).then_inc(er_ready.sem, 1)

            @block.tensor
            def _(pe):
                pe.wait_ge(prepared.sem, 1)
                for b in range(7):
                    lo, hi = 4 * b, min(4 * b + 4, NWT)
                    for k in range(lo, hi):
                        rows = 8 if k == GW1 else P
                        last = pe.transpose(bank[b][:, (k - lo) * P:(k - lo) * P + rows], raw[0:rows, k, :],
                                            c("ident")[0:rows, 0:rows])
                    last.then_inc(turned.sem, 1)
                pe.matmul(bank[7][:, 0:HEADS], c("spread_heads")[0:HEADS, :], thT[:, :], start=True, stop=True).then_inc(small_ps.sem, 1)
                pe.wait_ge(moved.sem, 1)
                for t in range(2):
                    last = pe.matmul(bank[6][:, :], er_rep[:, t, :, :].rearrange("p h d -> p (h d)"), back[:, t, :],
                                     start=(t == 0), stop=(t == 1))
                last.then_inc(small_ps.sem, 1)


def x_tiles(g, t, n):
    return g["x_all"][:, bass.ds(t * (n * P), n * P)].rearrange("p (k d) -> p k d", d=P)


def norm_parts(nc, sb, pre, n):
    return {
        "n": n, "stats": sb(pre + "stats", [P, n, 6]), "mv": sb(pre + "mv", [P, n, 2]), "apart": sb(pre + "apart", [P, n]), "mean": sb(pre + "mean", [P, n]), "var": sb(pre + "var", [P, n]),
        "power": sb(pre + "power", [P, n]), "rstd": sb(pre + "rstd", [P, n]), "xn": sb(pre + "xn", [P, n, P]),
        "var_ready": Signal(nc, pre + "var_ready"), "rstd_ready": Signal(nc, pre + "rstd_ready"),
        "xn_ready": Signal(nc, pre + "xn_ready", n), "steps": Signal(nc, pre + "norm_steps", n + 5), "power_set": Signal(nc, pre + "power_set"),
    }


def norm_vector(dve, g, ln, t):
    n, x = ln["n"], x_tiles(g, t, ln["n"])
    ch = Chain(dve, ln["steps"], t)
    for k in range(n):
        ch.did(dve.bn_stats(ln["stats"][:, k, :], x[:, k, :]))
    ch.settle()
    ch.did(dve.tensor_tensor(ln["mv"][:, :, 0:2], ln["stats"][:, :, 1:3], ln["stats"][:, :, 4:6], ALU.add))
    ch.did(dve.tensor_tensor(ln["apart"][:, :], ln["stats"][:, :, 1], ln["stats"][:, :, 4], ALU.subtract))
    ch.settle()
    ch.did(dve.tensor_scalar(ln["mean"][:, :], ln["mv"][:, :, 0], 0.5, None, ALU.mult))
    ch.did(dve.tensor_tensor(ln["apart"][:, :], ln["apart"][:, :], ln["apart"][:, :], ALU.mult))
    ch.settle()
    ch.did(dve.scalar_tensor_tensor(out=ln["var"][:, :], in0=ln["apart"][:, :], scalar=P / 4, in1=ln["mv"][:, :, 1], op0=ALU.mult, op1=ALU.add))
    ch.settle()
    ch.end()
    dve.tensor_scalar(ln["var"][:, :], ln["var"][:, :], 1.0 / P, EPS, ALU.mult, ALU.add).then_inc(ln["var_ready"].sem, 1)
    dve.wait_ge(ln["rstd_ready"].sem, ln["rstd_ready"].at(t, 1))
    for k in range(n):
        dve.tensor_scalar(ln["xn"][:, k, :], x[:, k, :], ln["mean"][:, k:k + 1], ln["rstd"][:, k:k + 1],
                          ALU.subtract, ALU.mult).then_inc(ln["xn_ready"].sem, 1)


def norm_pool(pool, ln, t):
    pool.wait_ge(ln["var_ready"].sem, ln["var_ready"].at(t, 1))
    pool.tensor_tensor(ln["rstd"][:, :], ln["var"][:, :], ln["power"][:, :], ALU.pow).then_inc(ln["rstd_ready"].sem, 1)


def norm_pool_setup(pool, ln):
    pool.memset(ln["power"][:, :], -0.5).then_inc(ln["power_set"].sem, 1)
    pool.wait_ge(ln["power_set"].sem, 1)


def turn_tokens(pe, g, ln, ps, signal, t):
    for k in range(ln["n"]):
        pe.wait_ge(ln["xn_ready"].sem, ln["xn_ready"].at(t, k + 1))
        last = pe.transpose(ps[:, k * P:(k + 1) * P], ln["xn"][:, k, :], g["c"]("ident"))
    last.then_inc(signal.sem, 1)


def add_bias(pe, g, out, row, stop):
    return pe.matmul(out, g["ones_row"][:, :], g["bias_row"][:, row * P:(row + 1) * P], start=False, stop=stop)


def ffn0(nc, g, NB, pre):
    N = 4
    with ExitStack() as ctx:
        sb = lambda name, shape, dt=F32: ctx.enter_context(nc.sbuf_tensor(name, shape, dt))
        ln = norm_parts(nc, sb, pre, N)
        xT = sb(pre + "xT", [P, N * P])
        y = sb(pre + "y", [P, N, P])
        xT_ps, xT_ready, y_ps, chain = Signal(nc, pre + "xT_ps"), Signal(nc, pre + "xT_ready"), Signal(nc, pre + "y_ps"), Signal(nc, pre + "chain", 2)
        turned, prod = g["bank"][0], g["bank"][1]
        turns = NB * 2 // N
        with nc.Block() as block:
            @block.vector
            def _(dve):
                with dve.Fori(0, turns) as t:
                    ch = Chain(dve, chain, t)
                    norm_vector(dve, g, ln, t)
                    dve.wait_ge(y_ps.sem, y_ps.at(t, 1))
                    ch.did(dve.tensor_scalar(y[:, :, :], prod[:, :].rearrange("p (k d) -> p k d", d=P), 100.0, -100.0, ALU.min, ALU.max))
                    ch.settle()
                    x = x_tiles(g, t, N)
                    ch.did(dve.scalar_tensor_tensor(out=x, in0=y[:, :, :], scalar=0.5, in1=x, op0=ALU.mult, op1=ALU.add))
                    ch.settle()
                    ch.end()

            @block.gpsimd
            def _(pool):
                norm_pool_setup(pool, ln)
                with pool.Fori(0, turns) as t:
                    norm_pool(pool, ln, t)

            @block.scalar
            def _(act):
                with act.Fori(0, turns) as t:
                    act.wait_ge(xT_ps.sem, xT_ps.at(t, 1))
                    act.copy(xT[:, :], turned[:, :]).then_inc(xT_ready.sem, 1)

            @block.tensor
            def _(pe):
                with pe.Fori(0, turns) as t:
                    turn_tokens(pe, g, ln, turned, xT_ps, t)
                    pe.wait_ge(xT_ready.sem, xT_ready.at(t, 1))
                    for k in range(N):
                        pe.matmul(prod[:, k * P:(k + 1) * P], xT[:, k * P:(k + 1) * P], g["wt"][:, WF0, :], start=True, stop=False)
                        last = add_bias(pe, g, prod[:, k * P:(k + 1) * P], B_F0, True)
                    last.then_inc(y_ps.sem, 1)


def ffn1(nc, g, NB, pre):
    N, E = 4, 8
    with ExitStack() as ctx:
        sb = lambda name, shape, dt=F32: ctx.enter_context(nc.sbuf_tensor(name, shape, dt))
        ln = norm_parts(nc, sb, pre, N)
        xT = sb(pre + "xT", [P, N * P])
        score = sb(pre + "score", [P, N, E])
        key = sb(pre + "key", [P, N, E])
        chosen = sb(pre + "chosen", [P, N, E])
        best = sb(pre + "best", [P, N])
        xT_ps, xT_ready, gate_ps = Signal(nc, pre + "xT_ps"), Signal(nc, pre + "xT_ready"), Signal(nc, pre + "gate_ps")
        y_ps, y_used = Signal(nc, pre + "y_ps", N), Signal(nc, pre + "y_used", N)
        chain = Signal(nc, pre + "chain", 6 + E * N)
        turned, gate = g["bank"][0], g["bank"][1]
        y_banks = [g["bank"][2:4], g["bank"][4:6]]
        turns = NB * 2 // N
        c = g["c"]
        with nc.Block() as block:
            @block.vector
            def _(dve):
                with dve.Fori(0, turns) as t:
                    ch = Chain(dve, chain, t)
                    norm_vector(dve, g, ln, t)
                    dve.wait_ge(gate_ps.sem, gate_ps.at(t, 1))
                    ch.did(dve.tensor_copy(score[:, :, :], gate[:, 0:N * E].rearrange("p (k e) -> p k e", e=E)))
                    ch.settle()
                    first_largest(dve, ch, score, best, key, chosen, c("rank8"), N, E)
                    for k in range(N):
                        x = x_tiles(g, t, N)[:, k, :]
                        dve.wait_ge(y_ps.sem, y_ps.at(t, k + 1))
                        for e in range(E):
                            y = y_banks[k % 2][e // 4][:, (e % 4) * P:(e % 4 + 1) * P]
                            ins = dve.scalar_tensor_tensor(out=x, in0=y, scalar=chosen[:, k, e:e + 1], in1=x, op0=ALU.mult, op1=ALU.add)
                            ch.did(ins)
                            ch.settle()
                        dve.nop().then_inc(y_used.sem, 1)
                    ch.end()

            @block.gpsimd
            def _(pool):
                norm_pool_setup(pool, ln)
                with pool.Fori(0, turns) as t:
                    norm_pool(pool, ln, t)

            @block.scalar
            def _(act):
                with act.Fori(0, turns) as t:
                    act.wait_ge(xT_ps.sem, xT_ps.at(t, 1))
                    act.copy(xT[:, :], turned[:, :]).then_inc(xT_ready.sem, 1)

            @block.tensor
            def _(pe):
                with pe.Fori(0, turns) as t:
                    turn_tokens(pe, g, ln, turned, xT_ps, t)
                    pe.wait_ge(xT_ready.sem, xT_ready.at(t, 1))
                    for k in range(N):
                        last = pe.matmul(gate[:, k * E:(k + 1) * E], xT[:, k * P:(k + 1) * P], g["wt"][:, GW1, 0:E], start=True, stop=True)
                    last.then_inc(gate_ps.sem, 1)
                    for k in range(N):
                        if k >= 2:
                            pe.wait_ge(y_used.sem, y_used.at(t, k - 1))
                        for half in range(2):
                            last = pe.matmul(y_banks[k % 2][half][:, :], xT[:, k * P:(k + 1) * P],
                                             g["wt"][:, WE1 + 4 * half:WE1 + 4 * half + 4, :].rearrange("p e d -> p (e d)"), start=True, stop=True)
                        last.then_inc(y_ps.sem, 1)


def first_largest(dve, ch, value, best, key, chosen, rank, n, m):
    def over(v):
        return v[:, :].unsqueeze(2).broadcast_to([P, n, m])

    ch.did(dve.tensor_reduce(best[:, :], value[:, :, :], AX.X, ALU.max))
    ch.settle()
    ch.did(dve.tensor_tensor(key[:, :, :], value[:, :, :], over(best), ALU.is_equal))
    ch.settle()
    ch.did(dve.tensor_tensor(key[:, :, :], key[:, :, :], rank.unsqueeze(1).broadcast_to([P, n, m]), ALU.mult))
    ch.settle()
    ch.did(dve.tensor_reduce(best[:, :], key[:, :, :], AX.X, ALU.max))
    ch.settle()
    ch.did(dve.tensor_tensor(chosen[:, :, :], key[:, :, :], over(best), ALU.is_equal))
    ch.settle()


def ffn2(nc, g, NB, pre):
    N, E = 4, 16
    NP = E // 2 + 1
    with ExitStack() as ctx:
        sb = lambda name, shape, dt=F32: ctx.enter_context(nc.sbuf_tensor(name, shape, dt))
        ln = norm_parts(nc, sb, pre, N)
        xT = sb(pre + "xT", [P, N * P])
        prob = sb(pre + "prob", [P, N, E])
        rest = sb(pre + "rest", [P, N, E])
        key = sb(pre + "key", [P, N, E])
        one1 = sb(pre + "one1", [P, N, E])
        one2 = sb(pre + "one2", [P, N, E])
        weight = sb(pre + "weight", [P, N, E])
        top = sb(pre + "top", [P, N])
        best = sb(pre + "best", [P, N])
        total = sb(pre + "total", [P, N])
        wT = sb(pre + "wT", [E, N * P])
        th = sb(pre + "th", [P, 2, N * P])
        hid = sb(pre + "hid", [P, 2, N * P])
        names = ("xT_ps", "xT_ready", "logit_ps", "shifted", "exped", "weight_ready", "wT_ps", "wT_ready", "out_ps")
        s = {n: Signal(nc, pre + n) for n in names}
        pair_ps, tanhed, hid_ready, hid_used = (Signal(nc, pre + n, NP) for n in ("pair_ps", "tanhed", "hid_ready", "hid_used"))
        chain = Signal(nc, pre + "chain", 1 + 3 + 5 + 1 + 5 + 1 + 2 * NP - 1 + 1)
        misc, acc = g["bank"][0], g["bank"][1]
        gb, ub, cb = g["bank"][2:4], g["bank"][4:6], g["bank"][6:8]
        turns = NB * 2 // N
        c = g["c"]
        with nc.Block() as block:
            @block.vector
            def _(dve):
                with dve.Fori(0, turns) as t:
                    ch = Chain(dve, chain, t)
                    norm_vector(dve, g, ln, t)
                    over = lambda v: v[:, :].unsqueeze(2).broadcast_to([P, N, E])
                    dve.wait_ge(s["logit_ps"].sem, s["logit_ps"].at(t, 1))
                    logit = misc[:, 0:N * E].rearrange("p (k e) -> p k e", e=E)
                    ch.did(dve.tensor_reduce(top[:, :], logit, AX.X, ALU.max))
                    ch.settle()
                    dve.tensor_tensor(rest[:, :, :], logit, over(top), ALU.subtract).then_inc(s["shifted"].sem, 1)
                    dve.wait_ge(s["exped"].sem, s["exped"].at(t, 1))
                    ch.did(dve.tensor_reduce(total[:, :], key[:, :, :], AX.X, ALU.add))
                    ch.settle()
                    ch.did(dve.reciprocal(total[:, :], total[:, :]))
                    ch.settle()
                    ch.did(dve.tensor_tensor(prob[:, :, :], key[:, :, :], over(total), ALU.mult))
                    ch.settle()
                    first_largest(dve, ch, prob, best, key, one1, c("rank16"), N, E)
                    ch.did(dve.scalar_tensor_tensor(out=rest[:, :, :], in0=one1[:, :, :], scalar=-2.0, in1=prob[:, :, :], op0=ALU.mult, op1=ALU.add))
                    ch.settle()
                    first_largest(dve, ch, rest, best, key, one2, c("rank16"), N, E)
                    ch.did(dve.tensor_tensor(one2[:, :, :], one2[:, :, :], one1[:, :, :], ALU.add))
                    ch.settle()
                    dve.tensor_tensor(weight[:, :, :], prob[:, :, :], one2[:, :, :], ALU.mult).then_inc(s["weight_ready"].sem, 1)
                    dve.wait_ge(s["wT_ps"].sem, s["wT_ps"].at(t, 1))
                    dve.tensor_copy(wT[:, :], misc[0:E, :]).then_inc(s["wT_ready"].sem, 1)
                    for j in range(NP):
                        dve.wait_ge(tanhed.sem, tanhed.at(t, j + 1))
                        if j >= 2:
                            dve.wait_ge(hid_used.sem, hid_used.at(t, j - 1))
                        h = hid[:, j % 2, :]
                        ch.did(dve.scalar_tensor_tensor(out=h, in0=th[:, j % 2, :], scalar=1.0, in1=gb[j % 2][:, :], op0=ALU.add, op1=ALU.mult))
                        ch.settle()
                        if j < NP - 1:
                            ch.did(dve.tensor_tensor(h, h, ub[j % 2][:, :], ALU.mult))
                            ch.settle()
                            dve.tensor_tensor(h, h, cb[j % 2][:, :], ALU.mult).then_inc(hid_ready.sem, 1)
                        else:
                            dve.tensor_tensor(h, h, ub[j % 2][:, :], ALU.mult).then_inc(hid_ready.sem, 1)
                    dve.wait_ge(s["out_ps"].sem, s["out_ps"].at(t, 1))
                    x = x_tiles(g, t, N)
                    ch.did(dve.tensor_tensor(x, acc[:, :].rearrange("p (k d) -> p k d", d=P), x, ALU.add))
                    ch.settle()
                    ch.end()

            @block.gpsimd
            def _(pool):
                norm_pool_setup(pool, ln)
                with pool.Fori(0, turns) as t:
                    norm_pool(pool, ln, t)

            @block.scalar
            def _(act):
                with act.Fori(0, turns) as t:
                    act.wait_ge(s["xT_ps"].sem, s["xT_ps"].at(t, 1))
                    act.copy(xT[:, :], misc[:, :]).then_inc(s["xT_ready"].sem, 1)
                    act.wait_ge(s["shifted"].sem, s["shifted"].at(t, 1))
                    act.activation(key[:, :, :], rest[:, :, :], ACT.Exp).then_inc(s["exped"].sem, 1)
                    for j in range(NP):
                        act.wait_ge(pair_ps.sem, pair_ps.at(t, j + 1))
                        if j >= 2:
                            act.wait_ge(hid_ready.sem, hid_ready.at(t, j - 1))
                        act.activation(th[:, j % 2, :], gb[j % 2][:, :], ACT.Tanh, scale=0.5).then_inc(tanhed.sem, 1)

            @block.tensor
            def _(pe):
                def down(t, j):
                    pe.wait_ge(hid_ready.sem, hid_ready.at(t, j + 1))
                    for k in range(N):
                        last = pe.matmul(acc[:, k * P:(k + 1) * P], hid[:, j % 2, k * P:(k + 1) * P], g["wd2"][:, j, :],
                                         start=(j == 0 and k == 0), stop=(j == NP - 1), skip_group_check=True)
                    last.then_inc(hid_used.sem, 1)
                    return last

                with pe.Fori(0, turns) as t:
                    turn_tokens(pe, g, ln, misc, s["xT_ps"], t)
                    pe.wait_ge(s["xT_ready"].sem, s["xT_ready"].at(t, 1))
                    for k in range(N):
                        last = pe.matmul(misc[:, k * E:(k + 1) * E], xT[:, k * P:(k + 1) * P], g["wr2"][:, :], start=True, stop=True)
                    last.then_inc(s["logit_ps"].sem, 1)
                    pe.wait_ge(s["weight_ready"].sem, s["weight_ready"].at(t, 1))
                    for k in range(N):
                        last = pe.transpose(misc[0:E, k * P:(k + 1) * P], weight[:, k, :], c("ident"))
                    last.then_inc(s["wT_ps"].sem, 1)
                    pe.wait_ge(s["wT_ready"].sem, s["wT_ready"].at(t, 1))
                    for j in range(NP):
                        if j >= 2:
                            pe.wait_ge(hid_ready.sem, hid_ready.at(t, j - 1))
                        if j < NP - 1:
                            wg = g["wg2"][:, 2 * j:2 * j + 2, :].rearrange("p e f -> p (e f)")
                            wu = g["wu2"][:, 2 * j:2 * j + 2, :].rearrange("p e f -> p (e f)")
                            pe.matmul(cb[j % 2][:, :], c("pick_expert")[0:E, j * P:(j + 1) * P], wT[:, :], start=True, stop=True)
                        else:
                            wg, wu = g["sgu2"][:, 0, :], g["sgu2"][:, 1, :]
                        pe.matmul(gb[j % 2][:, :], wg, xT[:, :], start=True, stop=True)
                        pe.matmul(ub[j % 2][:, :], wu, xT[:, :], start=True, stop=True).then_inc(pair_ps.sem, 1)
                        if j >= 1:
                            down(t, j - 1)
                    down(t, NP - 1)
                    pe.wait_ge(hid_used.sem, hid_used.at(t, NP))
                    pe.nop().then_inc(s["out_ps"].sem, 1)


def ffn3(nc, g, NB, pre):
    N, NH = 4, 3
    with ExitStack() as ctx:
        sb = lambda name, shape, dt=F32: ctx.enter_context(nc.sbuf_tensor(name, shape, dt))
        ln = norm_parts(nc, sb, pre, N)
        xT = sb(pre + "xT", [P, N * P])
        th = sb(pre + "th", [P, NH, N * P])
        hid = sb(pre + "hid", [P, NH, N * P])
        xT_ps, xT_ready = Signal(nc, pre + "xT_ps"), Signal(nc, pre + "xT_ready")
        part_ps, tanhed, hid_ready, down_ps = (Signal(nc, pre + n, NH) for n in ("part_ps", "tanhed", "hid_ready", "down_ps"))
        chain = Signal(nc, pre + "chain", NH + 1)
        misc, acc = g["bank"][0], g["bank"][1]
        gb, ub = g["bank"][2:5], g["bank"][5:8]
        turns = NB * 2 // N
        with nc.Block() as block:
            @block.vector
            def _(dve):
                with dve.Fori(0, turns) as t:
                    ch = Chain(dve, chain, t)
                    norm_vector(dve, g, ln, t)
                    for j in range(NH):
                        dve.wait_ge(tanhed.sem, tanhed.at(t, j + 1))
                        ch.did(dve.scalar_tensor_tensor(out=hid[:, j, :], in0=th[:, j, :], scalar=1.0, in1=gb[j][:, :], op0=ALU.add, op1=ALU.mult))
                        ch.settle()
                        dve.tensor_tensor(hid[:, j, :], hid[:, j, :], ub[j][:, :], ALU.mult).then_inc(hid_ready.sem, 1)
                    dve.wait_ge(down_ps.sem, down_ps.at(t, NH))
                    x = x_tiles(g, t, N)
                    ch.did(dve.tensor_tensor(x, acc[:, :].rearrange("p (k d) -> p k d", d=P), x, ALU.add))
                    ch.settle()
                    ch.end()

            @block.gpsimd
            def _(pool):
                norm_pool_setup(pool, ln)
                with pool.Fori(0, turns) as t:
                    norm_pool(pool, ln, t)

            @block.scalar
            def _(act):
                with act.Fori(0, turns) as t:
                    act.wait_ge(xT_ps.sem, xT_ps.at(t, 1))
                    act.copy(xT[:, :], misc[:, :]).then_inc(xT_ready.sem, 1)
                    for j in range(NH):
                        act.wait_ge(part_ps.sem, part_ps.at(t, j + 1))
                        act.activation(th[:, j, :], gb[j][:, :], ACT.Tanh, scale=0.5).then_inc(tanhed.sem, 1)

            @block.tensor
            def _(pe):
                with pe.Fori(0, turns) as t:
                    turn_tokens(pe, g, ln, misc, xT_ps, t)
                    pe.wait_ge(xT_ready.sem, xT_ready.at(t, 1))
                    for j in range(NH):
                        pe.matmul(gb[j][:, :], g["wt"][:, WG3 + j, :], xT[:, :], start=True, stop=True)
                        pe.matmul(ub[j][:, :], g["wt"][:, WU3 + j, :], xT[:, :], start=True, stop=True).then_inc(part_ps.sem, 1)
                    for j in range(NH):
                        pe.wait_ge(hid_ready.sem, hid_ready.at(t, j + 1))
                        for k in range(N):
                            last = pe.matmul(acc[:, k * P:(k + 1) * P], hid[:, j, k * P:(k + 1) * P], g["wt"][:, WD3 + j, :],
                                             start=(j == 0 and k == 0), stop=(j == NH - 1), skip_group_check=True)
                        last.then_inc(down_ps.sem, 1)


def att2(nc, g, NB, pre):
    N = 2
    with ExitStack() as ctx:
        sb = lambda name, shape, dt=F32: ctx.enter_context(nc.sbuf_tensor(name, shape, dt))
        ln = norm_parts(nc, sb, pre, N)
        xT = sb(pre + "xT", [P, S])
        qk = sb(pre + "qk", [P, 2, S])
        v = sb(pre + "v", [P, N, P])
        low = sb(pre + "low", [P, N])
        prob = sb(pre + "prob", [P, N, S])
        total = sb(pre + "total", [P, N])
        probT = sb(pre + "probT", [P, N, S])
        names = ("xT_ps", "xT_ready", "qk_ps", "qk_ready", "v_ps", "v_ready", "score_ps", "low_ready", "exped", "probT_ps", "probT_ready", "out_ps")
        s = {n: Signal(nc, pre + n, 2 if n == "exped" else 1) for n in names}
        chain = Signal(nc, pre + "chain", 3)
        turned, qk_b, v_b, score_b, probT_b, out_b = g["bank"][0:6]
        with nc.Block() as block:
            @block.vector
            def _(dve):
                with dve.Fori(0, NB) as t:
                    ch = Chain(dve, chain, t)
                    norm_vector(dve, g, ln, t)
                    dve.wait_ge(s["v_ps"].sem, s["v_ps"].at(t, 1))
                    dve.tensor_copy(v[:, :, :], v_b[:, 0:N * P].rearrange("p (k d) -> p k d", d=P)).then_inc(s["v_ready"].sem, 1)
                    dve.wait_ge(s["score_ps"].sem, s["score_ps"].at(t, 1))
                    dve.tensor_reduce(low[:, :], score_b[:, :].rearrange("p (k j) -> p k j", j=S), AX.X, ALU.max, negate=True).then_inc(s["low_ready"].sem, 1)
                    dve.wait_ge(s["exped"].sem, s["exped"].at(t, 2))
                    ch.did(dve.reciprocal(total[:, :], total[:, :]))
                    ch.settle()
                    dve.wait_ge(s["out_ps"].sem, s["out_ps"].at(t, 1))
                    for k in range(N):
                        x = x_tiles(g, t, N)[:, k, :]
                        ch.did(dve.scalar_tensor_tensor(out=x, in0=out_b[:, k * P:(k + 1) * P], scalar=total[:, k:k + 1], in1=x, op0=ALU.mult, op1=ALU.add))
                    ch.settle()
                    ch.end()

            @block.gpsimd
            def _(pool):
                norm_pool_setup(pool, ln)
                with pool.Fori(0, NB) as t:
                    norm_pool(pool, ln, t)

            @block.scalar
            def _(act):
                with act.Fori(0, NB) as t:
                    act.wait_ge(s["xT_ps"].sem, s["xT_ps"].at(t, 1))
                    act.copy(xT[:, :], turned[:, 0:S]).then_inc(s["xT_ready"].sem, 1)
                    act.wait_ge(s["qk_ps"].sem, s["qk_ps"].at(t, 1))
                    act.copy(qk[:, :, :], qk_b[:, :].rearrange("p (a i) -> p a i", a=2)).then_inc(s["qk_ready"].sem, 1)
                    act.wait_ge(s["low_ready"].sem, s["low_ready"].at(t, 1))
                    for k in range(N):
                        act.activation(prob[:, k, :], score_b[:, k * S:(k + 1) * S], ACT.Exp, bias=low[:, k:k + 1],
                                       accum_out=total[:, k:k + 1]).then_inc(s["exped"].sem, 1)
                    act.wait_ge(s["probT_ps"].sem, s["probT_ps"].at(t, 1))
                    act.copy(probT[:, :, :], probT_b[:, :].rearrange("p (k i) -> p k i", k=N)).then_inc(s["probT_ready"].sem, 1)

            @block.tensor
            def _(pe):
                with pe.Fori(0, NB) as t:
                    turn_tokens(pe, g, ln, turned, s["xT_ps"], t)
                    pe.wait_ge(s["xT_ready"].sem, s["xT_ready"].at(t, 1))
                    for a in range(2):
                        last = pe.matmul(qk_b[:, a * S:(a + 1) * S], g["wt"][:, WQ2 + a, :], xT[:, :], start=True, stop=True)
                    last.then_inc(s["qk_ps"].sem, 1)
                    for k in range(N):
                        last = pe.matmul(v_b[:, k * P:(k + 1) * P], xT[:, k * P:(k + 1) * P], g["wt"][:, WV2, :], start=True, stop=True)
                    last.then_inc(s["v_ps"].sem, 1)
                    pe.wait_ge(s["qk_ready"].sem, s["qk_ready"].at(t, 1))
                    for k in range(N):
                        last = pe.matmul(score_b[:, k * S:(k + 1) * S], qk[:, 0, k * P:(k + 1) * P], qk[:, 1, :], start=True, stop=True)
                    last.then_inc(s["score_ps"].sem, 1)
                    for k in range(N):
                        pe.wait_ge(s["exped"].sem, s["exped"].at(t, k + 1))
                        for j in range(N):
                            last = pe.transpose(probT_b[:, j * S + k * P:j * S + (k + 1) * P], prob[:, k, j * P:(j + 1) * P], g["c"]("ident"))
                    last.then_inc(s["probT_ps"].sem, 1)
                    pe.wait_ge(s["probT_ready"].sem, s["probT_ready"].at(t, 1))
                    pe.wait_ge(s["v_ready"].sem, s["v_ready"].at(t, 1))
                    for k in range(N):
                        for j in range(N):
                            last = pe.matmul(out_b[:, k * P:(k + 1) * P], probT[:, j, k * P:(k + 1) * P], v[:, j, :], start=(j == 0), stop=(j == N - 1))
                    last.then_inc(s["out_ps"].sem, 1)


def att0(nc, g, NB, pre):
    N, U, R = 2, S // 8, S // 16
    with ExitStack() as ctx:
        sb = lambda name, shape, dt=F32: ctx.enter_context(nc.sbuf_tensor(name, shape, dt))
        ln = norm_parts(nc, sb, pre, N)
        xT = sb(pre + "xT", [P, S])
        q = sb(pre + "q", [P, S])
        k = sb(pre + "k", [P, S])
        v = sb(pre + "v", [P, N, HEADS, DK + 1])
        q_heads = sb(pre + "q_heads", [P, U, HEADS, 8])
        q_steps = sb(pre + "q_steps", [P, U, HEADS, 8])
        low = sb(pre + "low", [P, 2, 2])
        prob = sb(pre + "prob", [P, 2, 2, S])
        probT = sb(pre + "probT", [P, N, HEADS, S])
        total = sb(pre + "total", [P, N, HEADS])
        o = sb(pre + "o", [P, N, P])
        oT = sb(pre + "oT", [P, S])
        s = {n: Signal(nc, pre + n) for n in ("xT_ps", "xT_ready", "qk_ps", "q_ready", "k_ready", "v_ps", "v_ready",
                                              "o_ps", "o_ready", "oT_ps", "oT_ready", "out_ps", "cleared")}
        qx_ps, qx_read, heads_ready = Signal(nc, pre + "qx_ps", 4), Signal(nc, pre + "qx_read", 4), Signal(nc, pre + "heads_ready", 4)
        score_ps, low_ready, probT_ps, moved_act, moved_dve = (Signal(nc, pre + n, R) for n in (
            "score_ps", "low_ready", "probT_ps", "moved_act", "moved_dve"))
        exped = Signal(nc, pre + "exped", 2 * R)
        chain = Signal(nc, pre + "chain", 2)
        bank = g["bank"]
        turned, qk_b, score_b, flip_b, o_b, oT_b = bank[0], bank[1], bank[2:4], bank[4:6], bank[6], bank[7]
        c = g["c"]

        def flipped(r, j):
            src = flip_b[r % 2][:, :].rearrange("p (k j h i) -> p k j h i", k=2, j=N, i=8)[:, :, j, :, :]
            dst = probT[:, j, :, 16 * r:16 * r + 16].rearrange("p h (k i) -> p k h i", k=2)
            return dst, src

        with nc.Block() as block:
            @block.vector
            def _(dve):
                dve.memset(q_steps[:, :, :, :], 0.0).then_inc(s["cleared"].sem, 1)
                dve.memset(v[:, :, :, :], 1.0).then_inc(s["cleared"].sem, 1)
                dve.wait_ge(s["cleared"].sem, 2)
                with dve.Fori(0, NB) as t:
                    ch = Chain(dve, chain, t)
                    norm_vector(dve, g, ln, t)
                    for w in range(4):
                        dve.wait_ge(qx_ps.sem, qx_ps.at(t, w + 1))
                        for m in range(2):
                            hp = 2 * w + m
                            for par in range(2):
                                rows = slice(64 * par, 64 * par + 64)
                                last = dve.scalar_tensor_tensor(
                                    out=q_steps[rows, :, 8 * par + hp, :], in0=flip_b[w % 2][rows, m * S:(m + 1) * S].rearrange("p (u i) -> p u i", i=8),
                                    scalar=g["col"][rows, hp:hp + 1], in1=c("step_of")[rows, :].rearrange("p (u i) -> p u i", i=8),
                                    op0=ALU.add, op1=ALU.mult)
                        last.then_inc(qx_read.sem, 1)
                    dve.wait_ge(s["v_ps"].sem, s["v_ps"].at(t, 1))
                    dve.tensor_copy(v[:, :, :, 0:DK].rearrange("p n h d -> p (n h) d"),
                                    o_b[:, 0:N * P].rearrange("p (a d) -> p a d", d=DK)).then_inc(s["v_ready"].sem, 1)
                    for r in range(R + 1):
                        if r < R:
                            dve.wait_ge(score_ps.sem, score_ps.at(t, r + 1))
                            if r >= 2:
                                dve.wait_ge(exped.sem, exped.at(t, 2 * (r - 1)))
                            dve.tensor_reduce(low[:, r % 2, :], score_b[r % 2][:, :].rearrange("p (k j) -> p k j", j=S),
                                              AX.X, ALU.max, negate=True).then_inc(low_ready.sem, 1)
                        if r >= 1:
                            dve.wait_ge(probT_ps.sem, probT_ps.at(t, r))
                            dve.wait_ge(moved_act.sem, moved_act.at(t, r))
                            dve.tensor_copy(*flipped(r - 1, 1)).then_inc(moved_dve.sem, 1)
                    dve.wait_ge(s["o_ps"].sem, s["o_ps"].at(t, 1))
                    o_v = o_b[:, 0:N * HEADS * (DK + 1)].rearrange("p (n h d) -> p n h d", n=N, d=DK + 1)
                    ch.did(dve.reciprocal(total[:, :, :], o_v[:, :, :, DK]))
                    ch.settle()
                    for n in range(N):
                        last = dve.tensor_tensor(o[:, n, :].rearrange("p (h d) -> p h d", d=DK), o_v[:, n, :, 0:DK],
                                                 total[:, n, :].unsqueeze(2).broadcast_to([P, HEADS, DK]), ALU.mult)
                    last.then_inc(s["o_ready"].sem, 1)
                    dve.wait_ge(s["out_ps"].sem, s["out_ps"].at(t, 1))
                    x = x_tiles(g, t, N)
                    ch.did(dve.tensor_tensor(x, qk_b[:, 0:N * P].rearrange("p (k d) -> p k d", d=P), x, ALU.add))
                    ch.settle()
                    ch.end()

            @block.gpsimd
            def _(pool):
                norm_pool_setup(pool, ln)
                with pool.Fori(0, NB) as t:
                    norm_pool(pool, ln, t)
                    pool.wait_ge(s["q_ready"].sem, s["q_ready"].at(t, 1))
                    for w in range(4):
                        us = slice(8 * w, 8 * w + 8)
                        pool.tensor_tensor(q_heads[:, us, :, :],
                                           q[:, 64 * w:64 * w + 64].rearrange("p (u i) -> p u i", i=8).unsqueeze(2).broadcast_to([P, 8, HEADS, 8]),
                                           c("head_of").unsqueeze(1).unsqueeze(3).broadcast_to([P, 8, HEADS, 8]),
                                           ALU.mult).then_inc(heads_ready.sem, 1)

            @block.scalar
            def _(act):
                with act.Fori(0, NB) as t:
                    act.wait_ge(s["xT_ps"].sem, s["xT_ps"].at(t, 1))
                    act.copy(xT[:, :], turned[:, 0:S]).then_inc(s["xT_ready"].sem, 1)
                    act.wait_ge(s["qk_ps"].sem, s["qk_ps"].at(t, 1))
                    act.activation(q[:, :], qk_b[:, 0:S], ACT.Identity, bias=g["col"][:, 8:9]).then_inc(s["q_ready"].sem, 1)
                    act.activation(k[:, :], qk_b[:, S:2 * S], ACT.Identity, bias=g["col"][:, 9:10]).then_inc(s["k_ready"].sem, 1)
                    for r in range(R + 1):
                        if r < R:
                            act.wait_ge(low_ready.sem, low_ready.at(t, r + 1))
                            if r >= 2:
                                act.wait_ge(probT_ps.sem, probT_ps.at(t, r - 1))
                            for m in range(2):
                                act.activation(prob[:, r % 2, m, :], score_b[r % 2][:, m * S:(m + 1) * S], ACT.Exp,
                                               bias=low[:, r % 2, m:m + 1]).then_inc(exped.sem, 1)
                        if r >= 1:
                            act.wait_ge(probT_ps.sem, probT_ps.at(t, r))
                            act.copy(*flipped(r - 1, 0)).then_inc(moved_act.sem, 1)
                    act.wait_ge(s["oT_ps"].sem, s["oT_ps"].at(t, 1))
                    act.copy(oT[:, :], oT_b[:, 0:S]).then_inc(s["oT_ready"].sem, 1)

            @block.tensor
            def _(pe):
                def scores(t, r):
                    if r >= 2:
                        pe.wait_ge(exped.sem, exped.at(t, 2 * (r - 1)))
                    if r % 4 == 0:
                        pe.wait_ge(heads_ready.sem, heads_ready.at(t, r // 4 + 1))
                    for m in range(2):
                        u = 2 * r + m
                        dst = score_b[r % 2][:, m * S:(m + 1) * S]
                        pe.matmul(dst, q_heads[:, u, :, :].rearrange("p h i -> p (h i)"), k[:, :], start=True, stop=False)
                        last = pe.matmul(dst, q_steps[:, u, :, :].rearrange("p h i -> p (h i)"), g["er_win"][:, S - 8 - 8 * u:2 * S - 8 - 8 * u],
                                         start=False, stop=True)
                    last.then_inc(score_ps.sem, 1)

                def flips(t, r):
                    pe.wait_ge(exped.sem, exped.at(t, 2 * r + 2))
                    if r >= 2:
                        pe.wait_ge(moved_dve.sem, moved_dve.at(t, r - 1))
                    for m in range(2):
                        for j in range(N):
                            last = pe.transpose(flip_b[r % 2][:, (2 * m + j) * P:(2 * m + j + 1) * P], prob[:, r % 2, m, j * P:(j + 1) * P], c("ident"))
                    last.then_inc(probT_ps.sem, 1)

                pe.wait_ge(s["cleared"].sem, 2)
                with pe.Fori(0, NB) as t:
                    turn_tokens(pe, g, ln, turned, s["xT_ps"], t)
                    pe.wait_ge(s["xT_ready"].sem, s["xT_ready"].at(t, 1))
                    for a in range(2):
                        last = pe.matmul(qk_b[:, a * S:(a + 1) * S], g["wt"][:, WQ0 + a, :], xT[:, :], start=True, stop=True)
                    last.then_inc(s["qk_ps"].sem, 1)
                    for w in range(4):
                        if w >= 2:
                            pe.wait_ge(qx_read.sem, qx_read.at(t, w - 1))
                        for m in range(2):
                            last = pe.matmul(flip_b[w % 2][:, m * S:(m + 1) * S], g["wqx"][:, 2 * w + m, :], xT[:, :], start=True, stop=True)
                        last.then_inc(qx_ps.sem, 1)
                    for n in range(N):
                        pe.matmul(o_b[:, n * P:(n + 1) * P], xT[:, n * P:(n + 1) * P], g["wt"][:, WV0, :], start=True, stop=False)
                        last = add_bias(pe, g, o_b[:, n * P:(n + 1) * P], B_V0, True)
                    last.then_inc(s["v_ps"].sem, 1)
                    pe.wait_ge(s["k_ready"].sem, s["k_ready"].at(t, 1))
                    pe.wait_ge(qx_read.sem, qx_read.at(t, 4))
                    scores(t, 0)
                    for r in range(R):
                        if r + 1 < R:
                            scores(t, r + 1)
                        flips(t, r)
                    pe.wait_ge(s["v_ready"].sem, s["v_ready"].at(t, 1))
                    pe.wait_ge(moved_dve.sem, moved_dve.at(t, R))
                    for n in range(N):
                        for h in range(HEADS):
                            at = (n * HEADS + h) * (DK + 1)
                            for j in range(N):
                                last = pe.matmul(o_b[:, at:at + DK + 1], probT[:, j, h, n * P:(n + 1) * P], v[:, j, h, :], start=(j == 0), stop=(j == N - 1))
                    last.then_inc(s["o_ps"].sem, 1)
                    pe.wait_ge(s["o_ready"].sem, s["o_ready"].at(t, 1))
                    for n in range(N):
                        last = pe.transpose(oT_b[:, n * P:(n + 1) * P], o[:, n, :], c("ident"))
                    last.then_inc(s["oT_ps"].sem, 1)
                    pe.wait_ge(s["oT_ready"].sem, s["oT_ready"].at(t, 1))
                    for n in range(N):
                        pe.matmul(qk_b[:, n * P:(n + 1) * P], oT[:, n * P:(n + 1) * P], g["wt"][:, WO0, :], start=True, stop=False)
                        last = add_bias(pe, g, qk_b[:, n * P:(n + 1) * P], B_O0, True)
                    last.then_inc(s["out_ps"].sem, 1)


def att3(nc, g, NB, pre):
    N = 2
    with ExitStack() as ctx:
        sb = lambda name, shape, dt=F32: ctx.enter_context(nc.sbuf_tensor(name, shape, dt))
        ln = norm_parts(nc, sb, pre, N)
        xT = sb(pre + "xT", [P, S])
        lin = sb(pre + "lin", [P, 2, S])
        neg = sb(pre + "neg", [P, 2, S])
        feat = sb(pre + "feat", [P, 2, S])
        rot = sb(pre + "rot", [P, 2, S])
        part = sb(pre + "part", [P, 2, S])
        q = sb(pre + "q", [P, 2, S])
        k_pick = sb(pre + "k_pick", [P, 2, HEADS, S])
        v = sb(pre + "v", [P, N, HEADS * (P + DK)])
        log_den = sb(pre + "log_den", [P, 2, N * S])
        inv = sb(pre + "inv", [P, 2, N * S])
        miss = sb(pre + "miss", [P, 2, N * S])
        rough = sb(pre + "rough", [P, 2, N * S])
        w = sb(pre + "w", [P, 2, N, S])
        oT = sb(pre + "oT", [P, S])
        s = {n: Signal(nc, pre + n) for n in ("xT_ps", "xT_ready", "qk_ps", "neg_ready", "exped", "feat_ready", "swap_ps", "rot_ready",
                                              "v_ps", "v_ready", "oT_ready", "out_ps", "cleared")}
        lin_ready, pick_ready, q_ready = Signal(nc, pre + "lin_ready", 2), Signal(nc, pre + "pick_ready", 8), Signal(nc, pre + "q_ready", 2)
        den_ps, num_ps, logged, inverted, w_ready, w_used = (Signal(nc, pre + n, HEADS) for n in (
            "den_ps", "num_ps", "logged", "inverted", "w_ready", "w_used"))
        rotated = Signal(nc, pre + "rotated", 2)
        refined = Signal(nc, pre + "refined", 2 * HEADS)
        added = Signal(nc, pre + "added")
        bank = g["bank"]
        turned, qk_b, swap_b, o_b, num_b, den_b = bank[0], bank[1], bank[2], bank[3], bank[4:6], bank[6:8]
        v_b = turned[:, S:2 * S]
        c = g["c"]
        flat = lambda a: a[:, :, :].rearrange("p a i -> p (a i)")
        with nc.Block() as block:
            @block.vector
            def _(dve):
                def negatives(t):
                    dve.wait_ge(lin_ready.sem, lin_ready.at(t, 2))
                    dve.tensor_scalar(flat(neg), flat(lin), 0.0, None, ALU.min).then_inc(s["neg_ready"].sem, 1)

                def features(t):
                    dve.wait_ge(s["exped"].sem, s["exped"].at(t, 1))
                    dve.scalar_tensor_tensor(out=flat(feat), in0=flat(lin), scalar=0.0, in1=flat(neg), op0=ALU.max, op1=ALU.add).then_inc(s["feat_ready"].sem, 1)

                def turn_features(t):
                    dve.wait_ge(s["feat_ready"].sem, s["feat_ready"].at(t, 1))
                    dve.tensor_tensor(flat(part), flat(feat), c("cos"), ALU.mult).then_inc(rotated.sem, 1)
                    dve.wait_ge(s["swap_ps"].sem, s["swap_ps"].at(t, 1))
                    dve.tensor_tensor(flat(rot), swap_b[:, :], c("sin"), ALU.mult).then_inc(rotated.sem, 1)
                    dve.wait_ge(rotated.sem, rotated.at(t, 2))
                    dve.tensor_tensor(flat(rot), flat(rot), flat(part), ALU.add).then_inc(s["rot_ready"].sem, 1)

                def values_in(t):
                    dve.wait_ge(s["v_ps"].sem, s["v_ps"].at(t, 1))
                    for n in range(N):
                        last = dve.tensor_scalar(v[:, n, :].rearrange("p (h c) -> p h c", h=HEADS)[:, :, 0:DK],
                                                 v_b[:, n * P:(n + 1) * P].rearrange("p (h d) -> p h d", d=DK), -1.0, None, ALU.mult)
                    last.then_inc(s["v_ready"].sem, 1)

                def turn(t, nxt):
                    for h in range(HEADS):
                        if h >= 2:
                            dve.wait_ge(w_ready.sem, w_ready.at(t, h - 1))
                        dve.wait_ge(inverted.sem, inverted.at(t, h + 1))
                        dve.tensor_tensor(miss[:, h % 2, :], den_b[h % 2][:, :], inv[:, h % 2, :], ALU.mult).then_inc(refined.sem, 1)
                        dve.wait_ge(num_ps.sem, num_ps.at(t, h + 1))
                        dve.tensor_tensor(rough[:, h % 2, :], num_b[h % 2][:, :], inv[:, h % 2, :], ALU.mult).then_inc(refined.sem, 1)
                        dve.wait_ge(refined.sem, refined.at(t, 2 * h + 2))
                        if h >= 2:
                            dve.wait_ge(w_used.sem, w_used.at(t, h - 1))
                        dve.scalar_tensor_tensor(out=w[:, h % 2, :, :].rearrange("p n i -> p (n i)"), in0=miss[:, h % 2, :], scalar=2.0, in1=rough[:, h % 2, :],
                                                 op0=ALU.subtract, op1=ALU.mult).then_inc(w_ready.sem, 1)
                        if nxt is not None:
                            if h == 0:
                                norm_vector(dve, g, ln, nxt)
                            if h == 5:
                                negatives(nxt)
                            if h == 6:
                                dve.wait_ge(pick_ready.sem, pick_ready.at(t, 8))
                                dve.wait_ge(q_ready.sem, q_ready.at(t, 2))
                                features(nxt)
                            if h == 7:
                                turn_features(nxt)
                    if nxt is not None:
                        dve.wait_ge(w_used.sem, w_used.at(t, HEADS))
                        values_in(nxt)
                    dve.wait_ge(s["out_ps"].sem, s["out_ps"].at(t, 1))
                    x = x_tiles(g, t, N)
                    dve.tensor_tensor(x, swap_b[:, 0:N * P].rearrange("p (k d) -> p k d", d=P), x, ALU.add).then_inc(added.sem, 1)

                dve.memset(v[:, :, :], 0.0).then_inc(s["cleared"].sem, 1)
                dve.wait_ge(s["cleared"].sem, 1)
                norm_vector(dve, g, ln, 0)
                negatives(0)
                features(0)
                turn_features(0)
                values_in(0)
                each_turn(dve, NB, turn)

            @block.gpsimd
            def _(pool):
                def picks(t, before):
                    pool.wait_ge(s["rot_ready"].sem, s["rot_ready"].at(t, 1))
                    for b in range(4):
                        hs = slice(4 * b, 4 * b + 4)
                        pick = c("head_of")[:, hs].unsqueeze(2).broadcast_to([P, 4, S])
                        if before is not None:
                            pool.wait_ge(num_ps.sem, num_ps.at(before, 4 * b + 4))
                        for kind, src in ((0, feat), (1, rot)):
                            pool.tensor_tensor(k_pick[:, kind, hs, :], src[:, 1:2, :].broadcast_to([P, 4, S]), pick, ALU.mult).then_inc(pick_ready.sem, 1)

                def turn(t, nxt):
                    if nxt is not None:
                        norm_pool(pool, ln, nxt)
                        picks(nxt, t)

                norm_pool_setup(pool, ln)
                norm_pool(pool, ln, 0)
                picks(0, None)
                each_turn(pool, NB, turn)

            @block.scalar
            def _(act):
                def x_in(t):
                    act.wait_ge(s["xT_ps"].sem, s["xT_ps"].at(t, 1))
                    act.copy(xT[:, :], turned[:, 0:S]).then_inc(s["xT_ready"].sem, 1)

                def linear(t):
                    act.wait_ge(s["qk_ps"].sem, s["qk_ps"].at(t, 1))
                    for a in range(2):
                        act.activation(lin[:, a, :], qk_b[:, a * S:(a + 1) * S], ACT.Identity, bias=g["col"][:, 10 + a:11 + a]).then_inc(lin_ready.sem, 1)

                def exponentials(t):
                    act.wait_ge(s["neg_ready"].sem, s["neg_ready"].at(t, 1))
                    act.activation(flat(neg), flat(neg), ACT.Exp).then_inc(s["exped"].sem, 1)

                def queries(t):
                    act.wait_ge(s["feat_ready"].sem, s["feat_ready"].at(t, 1))
                    act.copy(q[:, 0, :], feat[:, 0, :]).then_inc(q_ready.sem, 1)
                    act.wait_ge(s["rot_ready"].sem, s["rot_ready"].at(t, 1))
                    act.copy(q[:, 1, :], rot[:, 0, :]).then_inc(q_ready.sem, 1)

                def turn(t, nxt):
                    for h in range(HEADS):
                        act.wait_ge(den_ps.sem, den_ps.at(t, h + 1))
                        if h >= 2:
                            act.wait_ge(inverted.sem, inverted.at(t, h - 1))
                        act.activation(log_den[:, h % 2, :], den_b[h % 2][:, :], ACT.Ln).then_inc(logged.sem, 1)
                        act.wait_ge(logged.sem, logged.at(t, h + 1))
                        if h >= 2:
                            act.wait_ge(w_ready.sem, w_ready.at(t, h - 1))
                        act.activation(inv[:, h % 2, :], log_den[:, h % 2, :], ACT.Exp, scale=-1.0).then_inc(inverted.sem, 1)
                        if nxt is not None:
                            if h == 3:
                                x_in(nxt)
                            if h == 4:
                                linear(nxt)
                            if h == 5:
                                exponentials(nxt)
                    if nxt is not None:
                        act.wait_ge(num_ps.sem, num_ps.at(t, HEADS))
                        queries(nxt)
                    act.wait_ge(w_used.sem, w_used.at(t, HEADS))
                    act.copy(oT[:, :], o_b[:, 0:S]).then_inc(s["oT_ready"].sem, 1)

                act.add_instruction(mybir.InstLoadActFuncSet(name=nc.get_next_instruction_name(), act_func_set_id=6))
                x_in(0)
                linear(0)
                exponentials(0)
                queries(0)
                each_turn(act, NB, turn)

            @block.tensor
            def _(pe):
                def project(t):
                    pe.wait_ge(s["xT_ready"].sem, s["xT_ready"].at(t, 1))
                    for a in range(2):
                        last = pe.matmul(qk_b[:, a * S:(a + 1) * S], g["wqkv3"][:, a * P:(a + 1) * P], xT[:, :], start=True, stop=True)
                    last.then_inc(s["qk_ps"].sem, 1)
                    for n in range(N):
                        pe.matmul(v_b[:, n * P:(n + 1) * P], xT[:, n * P:(n + 1) * P], g["wqkv3"][:, 2 * P:3 * P], start=True, stop=False)
                        last = add_bias(pe, g, v_b[:, n * P:(n + 1) * P], B_V3, True)
                    last.then_inc(s["v_ps"].sem, 1)

                def swap(t):
                    pe.wait_ge(s["feat_ready"].sem, s["feat_ready"].at(t, 1))
                    pe.matmul(swap_b[:, :], c("swap"), flat(feat), start=True, stop=True).then_inc(s["swap_ps"].sem, 1)

                def weights(t, h):
                    if h % 4 == 0:
                        pe.wait_ge(pick_ready.sem, pick_ready.at(t, 2 * (h // 4) + 2))
                    for kind, banks, done in ((0, den_b, den_ps), (1, num_b, num_ps)):
                        if h >= 2:
                            pe.wait_ge(w_ready.sem, w_ready.at(t, h - 1))
                        for j in range(N):
                            last = pe.matmul(banks[h % 2][:, j * S:(j + 1) * S], k_pick[:, kind, h, j * P:(j + 1) * P],
                                             q[:, kind, :], start=True, stop=True)
                        last.then_inc(done.sem, 1)

                def values(t, h):
                    pe.wait_ge(w_ready.sem, w_ready.at(t, h + 1))
                    for j in range(N):
                        last = pe.matmul(o_b[:, 0:S], v[:, j, h * P:(h + 1) * P], w[:, h % 2, j, :],
                                         start=(h == 0 and j == 0), stop=(h == HEADS - 1 and j == N - 1))
                    last.then_inc(w_used.sem, 1)

                def turn(t, nxt):
                    pe.wait_ge(q_ready.sem, q_ready.at(t, 2))
                    weights(t, 0)
                    pe.wait_ge(s["v_ready"].sem, s["v_ready"].at(t, 1))
                    for h in range(HEADS):
                        if h + 1 < HEADS:
                            weights(t, h + 1)
                        values(t, h)
                        if nxt is not None:
                            if h == 2:
                                turn_tokens(pe, g, ln, turned, s["xT_ps"], nxt)
                            if h == 3:
                                project(nxt)
                            if h == 7:
                                swap(nxt)
                    if nxt is not None:
                        pe.wait_ge(s["rot_ready"].sem, s["rot_ready"].at(nxt, 1))
                    pe.wait_ge(s["oT_ready"].sem, s["oT_ready"].at(t, 1))
                    for n in range(N):
                        pe.matmul(swap_b[:, n * P:(n + 1) * P], oT[:, n * P:(n + 1) * P], g["wout3"][:, :], start=True, stop=False)
                        last = add_bias(pe, g, swap_b[:, n * P:(n + 1) * P], B_O3, True)
                    last.then_inc(s["out_ps"].sem, 1)

                pe.wait_ge(s["cleared"].sem, 1)
                turn_tokens(pe, g, ln, turned, s["xT_ps"], 0)
                project(0)
                swap(0)
                each_turn(pe, NB, turn)


def each_turn(eng, n, turn):
    if n > 1:
        with eng.Fori(0, n - 1) as t:
            turn(t, t + 1)
    turn(n - 1, None)


def att1(nc, g, NB, pre):
    N, B, H, D = 2, 4, 16, 64
    U, KEYS, BK = 8, 3 * WIN, 6 * WIN
    G = H // 2
    with ExitStack() as ctx:
        sb = lambda name, shape, dt=F32: ctx.enter_context(nc.sbuf_tensor(name, shape, dt))
        ln = norm_parts(nc, sb, pre, N)
        xT = sb(pre + "xT", [P, ROWS, WIN])
        q = sb(pre + "q", [P, G, B * U, 4, 8])
        k = sb(pre + "k", [P, G, ROWS * WIN])
        v = sb(pre + "v", [BK, 2, H * D])
        masked = sb(pre + "masked", [P, 2, U, KEYS])
        moved = sb(pre + "moved", [P, U, KEYS])
        ex = sb(pre + "ex", [P, U, KEYS])
        low = sb(pre + "low", [P, U])
        total = sb(pre + "total", [P, U])
        prob = sb(pre + "prob", [P, 4 * (2 * BK + WIN)])
        mixed = sb(pre + "mixed", [BK, H, U, 8])
        oT = sb(pre + "oT", [P, G, S + 4])
        s = {n: Signal(nc, pre + n) for n in ("xT_ps", "xT_ready", "first_ps", "first_ready", "out_ps", "cleared", "out_read")}
        q_ps, q_act, q_dve = (Signal(nc, pre + n, G // 2) for n in ("q_ps", "q_act", "q_dve"))
        k_ps, k_ready = Signal(nc, pre + "k_ps", G), Signal(nc, pre + "k_ready", G)
        v_ps, v_act, v_dve, score_ps, masked_ready, low_ready, moved_ready, exped, prob_ready, pv_ps, oT_ready = (
            Signal(nc, pre + n, B) for n in ("v_ps", "v_act", "v_dve", "score_ps", "masked_ready", "low_ready", "moved_ready",
                                             "exped", "prob_ready", "pv_ps", "oT_ready"))
        mix_ps, mixed_ready = Signal(nc, pre + "mix_ps", 2 * B), Signal(nc, pre + "mixed_ready", 2 * B)
        chain = Signal(nc, pre + "chain", 2 * B + 1)
        bank = g["bank"]
        turned, qk_b, v_b, score_b, mix_b = bank[0], bank[1:3], bank[3:5], bank[5], bank[6:8]
        out_ps = turned[:, S:2 * S]
        c = g["c"]
        window = c("window").rearrange("p (f u k) -> p f u k", f=2, u=U)

        def query_block(gp, half):
            rows = slice(D * half, D * half + D)
            src = qk_b[(gp // 2) % 2][rows, (gp % 2) * S:(gp % 2 + 1) * S].rearrange("p (u i) -> p u i", i=8)
            return q[rows, gp, :, 2 * (gp % 2) + half, :], src

        with nc.Block() as block:
            @block.vector
            def _(dve):
                dve.memset(q[:, :, :, :, :].rearrange("p a b c d -> p (a b c d)"), 0.0).then_inc(s["cleared"].sem, 1)
                dve.memset(prob[:, :], 0.0).then_inc(s["cleared"].sem, 1)
                dve.memset(xT[:, :, :], 0.0).then_inc(s["cleared"].sem, 1)
                dve.wait_ge(s["cleared"].sem, 3)

                with dve.Fori(0, NB) as t:
                    ch = Chain(dve, chain, t)
                    norm_vector(dve, g, ln, t)
                    for w in range(G // 2):
                        dve.wait_ge(q_ps.sem, q_ps.at(t, w + 1))
                        dve.wait_ge(q_act.sem, q_act.at(t, w + 1))
                        dve.tensor_copy(*query_block(2 * w + 1, 0))
                        dve.tensor_copy(*query_block(2 * w + 1, 1)).then_inc(q_dve.sem, 1)
                    for b in range(B):
                        dve.wait_ge(v_ps.sem, v_ps.at(t, b + 1))
                        if b >= 2:
                            dve.wait_ge(pv_ps.sem, pv_ps.at(t, b - 1))
                        dve.tensor_copy(v[:, b % 2, 0:512], v_b[0][0:BK, :]).then_inc(v_dve.sem, 1)
                        dve.wait_ge(score_ps.sem, score_ps.at(t, b + 1))
                        dve.tensor_tensor(masked[:, b % 2, :, :], score_b[:, 0:U * KEYS].rearrange("p (u k) -> p u k", k=KEYS),
                                          window[:, min(b, 1), :, :], ALU.add).then_inc(masked_ready.sem, 1)
                        dve.wait_ge(masked_ready.sem, masked_ready.at(t, b + 1))
                        dve.tensor_reduce(low[:, :], masked[:, b % 2, :, :], AX.X, ALU.max, negate=True).then_inc(low_ready.sem, 1)
                        dve.wait_ge(exped.sem, exped.at(t, b + 1))
                        ch.did(dve.tensor_reduce(total[:, :], ex[:, :, :], AX.X, ALU.add))
                        ch.settle()
                        ch.did(dve.reciprocal(total[:, :], total[:, :]))
                        ch.settle()
                        if b >= 1:
                            dve.wait_ge(mix_ps.sem, mix_ps.at(t, 2 * b))
                        place = prob[:, :].rearrange("p (r c) -> p r c", r=4)[:, :, 0:2 * BK].rearrange("p r (u k) -> p r u k", u=2)[:, :, :, 0:KEYS]
                        dve.tensor_tensor(place, ex[:, :, :].rearrange("p (r u) k -> p r u k", u=2),
                                          total[:, :].rearrange("p (r u) -> p r u", u=2).unsqueeze(3).broadcast_to([P, 4, 2, KEYS]),
                                          ALU.mult).then_inc(prob_ready.sem, 1)
                    dve.wait_ge(s["out_ps"].sem, s["out_ps"].at(t, 1))
                    x = x_tiles(g, t, N)
                    ch.did(dve.tensor_tensor(x, out_ps.rearrange("p (k d) -> p k d", d=P), x, ALU.add))
                    ch.settle()
                    ch.end()

            @block.gpsimd
            def _(pool):
                norm_pool_setup(pool, ln)
                with pool.Fori(0, NB) as t:
                    norm_pool(pool, ln, t)
                    for b in range(B):
                        pool.wait_ge(low_ready.sem, low_ready.at(t, b + 1))
                        if b >= 1:
                            pool.wait_ge(exped.sem, exped.at(t, b))
                        pool.tensor_tensor(moved[:, :, :], masked[:, b % 2, :, :], low[:, :].unsqueeze(2).broadcast_to([P, U, KEYS]),
                                           ALU.add).then_inc(moved_ready.sem, 1)

            @block.scalar
            def _(act):
                act.wait_ge(s["cleared"].sem, 3)
                with act.Fori(0, NB) as t:
                    act.wait_ge(s["xT_ps"].sem, s["xT_ps"].at(t, 1))
                    act.copy(xT[:, 2:ROWS - 1, 1:WIN], turned[:, 1:1 + 16 * 15].rearrange("p (r k) -> p r k", k=16))
                    act.copy(xT[:, ROWS - 1, 1:WIN - 1], turned[:, 241:S])
                    act.copy(xT[:, :, 0], turned[:, 0:1].broadcast_to([P, ROWS])).then_inc(s["xT_ready"].sem, 1)
                    for w in range(G // 2):
                        act.wait_ge(q_ps.sem, q_ps.at(t, w + 1))
                        act.copy(*query_block(2 * w, 0))
                        act.copy(*query_block(2 * w, 1)).then_inc(q_act.sem, 1)
                    for gp in range(G):
                        act.wait_ge(k_ps.sem, k_ps.at(t, gp + 1))
                        act.copy(k[:, gp, :], qk_b[gp % 2][:, 0:ROWS * WIN]).then_inc(k_ready.sem, 1)
                    act.wait_ge(s["first_ps"].sem, s["first_ps"].at(t, 1))
                    act.copy(oT[:, :, 0], turned[:, 0:G]).then_inc(s["first_ready"].sem, 1)

                    def values_in(b):
                        act.wait_ge(v_ps.sem, v_ps.at(t, b + 1))
                        if b >= 2:
                            act.wait_ge(pv_ps.sem, pv_ps.at(t, b - 1))
                        act.copy(v[:, b % 2, 512:1024], v_b[1][0:BK, :]).then_inc(v_act.sem, 1)

                    values_in(0)
                    for b in range(B):
                        act.wait_ge(moved_ready.sem, moved_ready.at(t, b + 1))
                        if b >= 1:
                            act.wait_ge(prob_ready.sem, prob_ready.at(t, b))
                        act.activation(ex[:, :, :], moved[:, :, :], ACT.Exp).then_inc(exped.sem, 1)
                        if b + 1 < B:
                            values_in(b + 1)
                        for half in range(2):
                            act.wait_ge(mix_ps.sem, mix_ps.at(t, 2 * b + half + 1))
                            if b >= 1 and half == 0:
                                act.wait_ge(pv_ps.sem, pv_ps.at(t, b))
                            act.copy(mixed[:, :, 4 * half:4 * half + 4, :].rearrange("p g u i -> p u g i"),
                                     mix_b[half][0:BK, :].rearrange("p (u g i) -> p u g i", u=4, i=8)).then_inc(mixed_ready.sem, 1)
                        act.wait_ge(pv_ps.sem, pv_ps.at(t, b + 1))
                        act.copy(oT[:, :, 1 + 64 * b:65 + 64 * b], qk_b[b % 2][:, :].rearrange("p (g i) -> p g i", g=G)).then_inc(oT_ready.sem, 1)

            @block.tensor
            def _(pe):
                wq, wk, wv = (g["wqkv1"][:, a * H * D:(a + 1) * H * D] for a in range(3))

                def values_and_scores(t, b):
                    if b >= 1:
                        pe.wait_ge(v_act.sem, v_act.at(t, b))
                        pe.wait_ge(v_dve.sem, v_dve.at(t, b))
                    for half in range(2):
                        last = pe.matmul(v_b[half][0:BK, :], xT[:, 4 * b:4 * b + 6, :].rearrange("p r k -> p (r k)"),
                                         wv[:, 512 * half:512 * half + 512], start=True, stop=True)
                    last.then_inc(v_ps.sem, 1)
                    if b >= 1:
                        pe.wait_ge(masked_ready.sem, masked_ready.at(t, b))
                    for u in range(U):
                        row = 4 * b + u // 2
                        for gp in range(G):
                            four = gp // 2
                            last = pe.matmul(score_b[32 * four:32 * four + 32, u * KEYS:(u + 1) * KEYS],
                                             q[:, gp, U * b + u, :, :].rearrange("p h i -> p (h i)"), k[:, gp, WIN * row:WIN * row + KEYS],
                                             start=(gp % 2 == 0), stop=(gp % 2 == 1))
                    last.then_inc(score_ps.sem, 1)

                pe.wait_ge(s["cleared"].sem, 3)
                with pe.Fori(0, NB) as t:
                    turn_tokens(pe, g, ln, turned, s["xT_ps"], t)
                    pe.wait_ge(s["xT_ready"].sem, s["xT_ready"].at(t, 1))
                    for w in range(G // 2):
                        if w >= 2:
                            pe.wait_ge(q_dve.sem, q_dve.at(t, w - 1))
                        for m in range(2):
                            gp = 2 * w + m
                            last = pe.matmul(qk_b[w % 2][:, m * S:(m + 1) * S], wq[:, gp * P:(gp + 1) * P], xT[:, 2:ROWS, 1:WIN], start=True, stop=True)
                        last.then_inc(q_ps.sem, 1)
                    for gp in range(G):
                        if gp < 2:
                            pe.wait_ge(q_dve.sem, q_dve.at(t, G // 2 - 1 + gp))
                        else:
                            pe.wait_ge(k_ready.sem, k_ready.at(t, gp - 1))
                        pe.matmul(qk_b[gp % 2][:, 0:ROWS * WIN], wk[:, gp * P:(gp + 1) * P], xT[:, :, :].rearrange("p r k -> p (r k)"),
                                  start=True, stop=True).then_inc(k_ps.sem, 1)
                    for gp in range(G):
                        last = pe.matmul(turned[:, gp:gp + 1], wv[:, gp * P:(gp + 1) * P], xT[:, 0, 0:1], start=True, stop=True)
                    last.then_inc(s["first_ps"].sem, 1)
                    pe.wait_ge(k_ready.sem, k_ready.at(t, G))
                    values_and_scores(t, 0)
                    for b in range(B):
                        if b + 1 < B:
                            values_and_scores(t, b + 1)
                        pe.wait_ge(prob_ready.sem, prob_ready.at(t, b + 1))
                        for half in range(2):
                            if b >= 1:
                                pe.wait_ge(mixed_ready.sem, mixed_ready.at(t, 2 * b - 1 + half))
                            for u in range(4 * half, 4 * half + 4):
                                last = pe.matmul(mix_b[half][0:BK, (u % 4) * P:(u % 4 + 1) * P], prob[:, u * BK:(u + 1) * BK],
                                                 g["mix"][:, :, :].rearrange("p g i -> p (g i)"), start=True, stop=True)
                            last.then_inc(mix_ps.sem, 1)
                        pe.wait_ge(mixed_ready.sem, mixed_ready.at(t, 2 * b + 2))
                        pe.wait_ge(v_act.sem, v_act.at(t, b + 1))
                        pe.wait_ge(v_dve.sem, v_dve.at(t, b + 1))
                        if b >= 2:
                            pe.wait_ge(oT_ready.sem, oT_ready.at(t, b - 1))
                        for h in range(H):
                            last = pe.matmul(qk_b[b % 2][D * (h % 2):D * (h % 2) + D, (h // 2) * 64:(h // 2) * 64 + 64], v[:, b % 2, h * D:(h + 1) * D],
                                             mixed[:, h, :, :].rearrange("p u i -> p (u i)"), start=True, stop=True)
                        last.then_inc(pv_ps.sem, 1)
                    pe.wait_ge(oT_ready.sem, oT_ready.at(t, B))
                    pe.wait_ge(s["first_ready"].sem, s["first_ready"].at(t, 1))
                    for n in range(N):
                        dst = out_ps[:, n * P:(n + 1) * P]
                        for gp in range(G):
                            pe.matmul(dst, oT[:, gp, n * P:(n + 1) * P], g["wout1"][:, gp, :], start=(gp == 0), stop=False)
                        last = add_bias(pe, g, dst, B_O1, True)
                    last.then_inc(s["out_ps"].sem, 1)


_INS = ['L0_attn_x', 'L0_attn_Wq', 'L0_attn_bq', 'L0_attn_Wk', 'L0_attn_bk', 'L0_attn_Wv', 'L0_attn_bv', 'L0_attn_Wo',
        'L0_attn_bo', 'L0_attn_Er', 'L0_ffn_weights', 'L0_ffn_scale', 'L0_ffn_bias', 'L1_attn_w_qkv', 'L1_attn_w_out',
        'L1_attn_b_out', 'L1_attn_w_th', 'L1_ffn_gate_w', 'L1_ffn_expert_w', 'L2_attn_W_qkv', 'L2_ffn_Wr', 'L2_ffn_Wg',
        'L2_ffn_Wu', 'L2_ffn_Wd', 'L2_ffn_Sg', 'L2_ffn_Su', 'L2_ffn_Sd', 'L3_attn_w_qkv', 'L3_attn_b_qkv',
        'L3_attn_w_out', 'L3_attn_b_out', 'L3_ffn_w_gate', 'L3_ffn_w_up', 'L3_ffn_w_down']


def kernel(**inputs):
    import numpy as _np
    import concourse.bacc as _bacc
    from concourse import mybir as _mybir
    from concourse.bass_utils import run_bass_kernel_spmd as _run

    nc = _bacc.Bacc("TRN2", target_bir_lowering=False, num_devices=1)
    arrays, aps = {}, {}
    for name in _INS + ["const"]:
        a = CONST if name == "const" else _np.ascontiguousarray(inputs[name])
        arrays[f"in_{name}_dram"] = a
        aps[name] = nc.dram_tensor(f"in_{name}_dram", a.shape, _mybir.dt.from_np(a.dtype), kind="ExternalInput").ap()
    shape = tuple(inputs["L0_attn_x"].shape)
    out = nc.dram_tensor("out_0_dram", shape, F32, kind="ExternalOutput").ap()
    network(nc, aps, out)
    r = _run(nc, [arrays], core_ids=[0])
    return r.results[0]["out_0_dram"]
```

```python
from contextlib import ExitStack

import numpy as np
import concourse.bass as bass
from concourse import mybir

F32 = mybir.dt.float32
BF16 = mybir.dt.bfloat16
I32 = mybir.dt.int32
ALU = mybir.AluOpType
ACT = mybir.ActivationFunctionType
AX = mybir.AxisListType

P = 128
S = 256
HEADS = 16
DK = P // HEADS
EPS = 1e-5
NEG = -1e30
WIN = 17
ROWS = S // 16 + 2
STAGES = list(range(12))

WQ0, WK0, WV0, WO0, WF0, WE1, WQ2, WK2, WV2, WG3, WU3, WD3, GW1, NWT = 0, 1, 2, 3, 4, 5, 13, 14, 15, 16, 19, 22, 25, 26
B_F0, B_V0, B_O0, B_O1, B_V3, B_O3, NBIAS = 0, 1, 2, 3, 4, 5, 6


def constants():
    part = np.arange(P)
    out = {}
    out["ident"] = np.eye(P)
    i = np.arange(S)
    out["head_of"] = (part[:, None] // DK == np.arange(HEADS)[None, :])
    out["step_of"] = (i[None, :] % 8 == (part[:, None] // DK) % 8)
    out["step8"] = (part[:, None] % 8 == np.arange(8)[None, :])
    out["spread_heads"] = (np.arange(HEADS)[:, None] == part[None, :] // 8)
    out["quad"] = ((part[:, None] // DK) % 4 == np.arange(4)[None, :])
    theta = 1.0 / 1250.0 ** ((part % DK) // 2 / (DK // 2))
    ang = (np.arange(S, dtype=np.float32)[None, :] * theta.astype(np.float32)[:, None]).astype(np.float32)
    out["cos"] = np.tile(np.cos(ang), (1, 2))
    out["sin"] = np.tile(np.sin(ang), (1, 2))
    swap = np.zeros((P, P))
    for m in range(P):
        swap[m + 1 if m % 2 == 0 else m - 1, m] = -1.0 if m % 2 == 0 else 1.0
    out["swap"] = swap
    out["rank8"] = np.tile(8.0 - np.arange(8), (P, 1))
    out["rank16"] = np.tile(16.0 - np.arange(16), (P, 1))
    sel = np.zeros((P, 8, P))
    for e in range(16):
        sel[e:48:16, e // 2, 64 * (e % 2):64 * (e % 2) + 64] = 1
    out["pick_expert"] = sel.reshape(P, -1)
    mask = np.zeros((P, 2, 8, 3, WIN))
    for first in range(2):
        for u in range(8):
            x = u // 2 if first == 0 else 4 + u // 2
            for p in range(P):
                n = 8 * (u % 2) + p % 8
                mask[p, first, u, :2, 0] = NEG
                for slot in range(3):
                    if x - 2 + slot < 0:
                        mask[p, first, u, slot, 1:] = NEG
                mask[p, first, u, 2, 2 + n:] = NEG
    out["window"] = mask.reshape(P, -1)
    back = np.zeros((2, P, 2 * S))
    for c in range(2 * S - 1):
        r = min(S - 1, 2 * S - 2 - c)
        back[r // P, r % P, c] = 1
    out["back0"], out["back1"] = back[0], back[1]
    at, cols, parts = {}, 0, []
    for name, a in out.items():
        a = np.asarray(a, np.float32)
        if a.shape[0] < P:
            a = np.concatenate([a, np.zeros((P - a.shape[0], a.shape[1]), np.float32)])
        at[name] = (cols, a.shape[1])
        cols += a.shape[1]
        parts.append(a)
    return np.ascontiguousarray(np.concatenate(parts, 1)), at


CONST, CONST_AT = constants()


class Signal:

    def __init__(self, nc, name, per=1):
        self.sem, self.per = nc.alloc_semaphore(name=name), per

    def at(self, t, k):
        return t * self.per + k


class Chain:

    def __init__(self, eng, steps, t):
        self.eng, self.steps, self.t, self.n = eng, steps, t, 0

    def did(self, ins):
        self.n += 1
        ins.then_inc(self.steps.sem, 1)

    def settle(self):
        self.eng.wait_ge(self.steps.sem, self.steps.at(self.t, self.n))

    def end(self):
        assert self.n == self.steps.per, (self.n, self.steps.per)


def network(nc, ins, out):
    NB = ins["L0_attn_x"].shape[0]
    x_dram = ins["L0_attn_x"].rearrange("b (h p) d -> p (b h) d", p=P)
    out_dram = out.rearrange("b (h p) d -> p (b h) d", p=P)
    ctx = ExitStack()
    with ctx:
        def sb(name, shape, dt=F32):
            return ctx.enter_context(nc.sbuf_tensor(name, shape, dt))

        bank = [ctx.enter_context(nc.psum_tensor(f"bank{i}", [P, 512], F32)) for i in range(8)]
        x_all = sb("x_all", [P, NB * 2 * P])
        wt = sb("wt", [P, NWT, P])
        small = {n: CONST_AT[n] for n in CONST_AT if n not in ("back0", "back1")}
        const_cols = CONST_AT["back0"][0]
        const = sb("const", [P, const_cols])
        bias_row = sb("bias_row", [1, NBIAS * P])
        ones_row = sb("ones_row", [1, P])
        col = sb("col", [P, 16])
        wqx = sb("wqx", [P, 8, P])
        er_win = sb("er_win", [P, 2 * S - 8])
        mix = sb("mix", [P, HEADS, 8])
        wqkv1 = sb("wqkv1", [P, 3 * 1024])
        wout1 = sb("wout1", [P, 8, P])
        wg2 = sb("wg2", [P, 16, 64])
        wu2 = sb("wu2", [P, 16, 64])
        wd2 = sb("wd2", [P, 9, P])
        sgu2 = sb("sgu2", [P, 2, P])
        wr2 = sb("wr2", [P, 16])
        wqkv3 = sb("wqkv3", [P, 3 * P])
        wout3 = sb("wout3", [P, P])
        g = dict(locals())

        def c(name):
            a, n = small[name]
            return const[:, a:a + n]

        g["c"] = c
        with nc.cleanup_on_exit():
            setup(nc, ins, g)
        stages = [("ffn0",), ("att0",), ("ffn0",), ("ffn1",), ("att1",), ("ffn1",),
                  ("ffn2",), ("att2",), ("ffn2",), ("ffn3",), ("att3",), ("ffn3",)]
        build = {"ffn0": ffn0, "att0": att0, "ffn1": ffn1, "att1": att1, "ffn2": ffn2, "att2": att2,
                 "ffn3": ffn3, "att3": att3}
        for n in STAGES:
            with nc.cleanup_on_exit():
                build[stages[n][0]](nc, g, NB, f"{stages[n][0]}_{n}_")
        with nc.cleanup_on_exit():
            stored = Signal(nc, "stored")
            with nc.Block() as block:
                @block.sync
                def _(sp):
                    xv = x_all[:, :].rearrange("p (t d) -> p t d", d=P)
                    half = NB
                    sp.dma_start(out_dram[:, 0:half, :], xv[:, 0:half, :]).then_inc(stored.sem, 16)
                    sp.dma_start(out_dram[:, half:, :], xv[:, half:, :]).then_inc(stored.sem, 16)
                    sp.wait_ge(stored.sem, 32)


def setup(nc, ins, g):
    wt, const, bias_row, ones_row, col, c = (g[k] for k in ("wt", "const", "bias_row", "ones_row", "col", "c"))
    bank, wqx, er_win, mix, wd2, x_all = (g[k] for k in ("bank", "wqx", "er_win", "mix", "wd2", "x_all"))
    with ExitStack() as ctx:
        def sb(name, shape, dt=F32):
            return ctx.enter_context(nc.sbuf_tensor(name, shape, dt))

        raw = sb("raw", [P, NWT, P])
        raw_int = sb("raw_int", [P, 9, P], I32)
        scale0 = sb("scale0", [P, 1])
        er = sb("er", [P, 2, DK])
        er_rep = sb("er_rep", [P, 2, HEADS, DK])
        back = sb("back", [P, 2, 2 * S])
        er_rev = sb("er_rev", [P, 2 * S])
        thT = sb("thT", [HEADS, HEADS])
        th_rep = sb("th_rep", [P, HEADS])
        half_ident = sb("half_ident", [P, P])
        loaded, x_in, prepared, turned, moved, chain = (Signal(nc, n) for n in (
            "loaded", "x_in", "prepared", "turned", "moved", "chain"))
        small_ps, er_ready, shifted = (Signal(nc, n) for n in ("small_ps", "er_ready", "shifted"))
        loads = []

        def blocks(name):
            return ins[name].rearrange("(t p) d -> p t d", p=P)

        loads.append((const[:, :], ins["const"][:, 0:g["const_cols"]]))
        loads.append((back[:, :, :], ins["const"][:, g["const_cols"]:].rearrange("p (t c) -> p t c", t=2)))
        for n, name in ((WQ0, "L0_attn_Wq"), (WK0, "L0_attn_Wk"), (WV0, "L0_attn_Wv"), (WO0, "L0_attn_Wo"), (WF0, "L0_ffn_weights")):
            loads.append((raw[:, n, :], ins[name]))
        loads.append((raw[:, WE1:WE1 + 8, :], ins["L1_ffn_expert_w"].rearrange("e f h -> f e h")))
        loads.append((raw[:, WQ2:WQ2 + 3, :], blocks("L2_attn_W_qkv")))
        loads.append((raw[0:8, GW1, :], ins["L1_ffn_gate_w"]))
        loads.append((raw_int[:, 0:3, :], blocks("L3_ffn_w_gate")))
        loads.append((raw_int[:, 3:6, :], blocks("L3_ffn_w_up")))
        loads.append((raw_int[:, 6:9, :], ins["L3_ffn_w_down"].rearrange("d (t h) -> d t h", t=3)))
        for n, name in ((B_F0, "L0_ffn_bias"), (B_V0, "L0_attn_bv"), (B_O0, "L0_attn_bo"), (B_O1, "L1_attn_b_out"), (B_O3, "L3_attn_b_out")):
            loads.append((bias_row[:, n * P:(n + 1) * P], ins[name].rearrange("(a d) -> a d", a=1)))
        loads.append((bias_row[:, B_V3 * P:(B_V3 + 1) * P], ins["L3_attn_b_qkv"][2 * P:3 * P].rearrange("(a d) -> a d", a=1)))
        loads.append((scale0[:, :], ins["L0_ffn_scale"].rearrange("(d a) -> d a", a=1)))
        loads.append((col[:, 8:9], ins["L0_attn_bq"].rearrange("(d a) -> d a", a=1)))
        loads.append((col[:, 9:10], ins["L0_attn_bk"].rearrange("(d a) -> d a", a=1)))
        loads.append((col[:, 10:12], ins["L3_attn_b_qkv"][0:2 * P].rearrange("(a d) -> d a", a=2)))
        for par in range(2):
            for i in range(8):
                loads.append((col[64 * par + 8 * i:64 * par + 8 * i + 8, 0:8],
                              ins["L0_attn_bq"][64 * par:64 * par + 64].rearrange("(h d) -> d h", d=DK)))
        loads.append((er[:, :, :], ins["L0_attn_Er"].rearrange("(t p) d -> p t d", p=P)))
        loads.append((thT[:, :], ins["L1_attn_w_th"].rearrange("g h -> h g")))
        loads.append((g["wqkv1"][:, :], ins["L1_attn_w_qkv"]))
        loads.append((g["wout1"][:, :, :], ins["L1_attn_w_out"].rearrange("(t p) d -> p t d", p=P)))
        loads.append((g["wg2"][:, :, :], ins["L2_ffn_Wg"].rearrange("e d f -> d e f")))
        loads.append((g["wu2"][:, :, :], ins["L2_ffn_Wu"].rearrange("e d f -> d e f")))
        loads.append((wd2[:, 0:8, :], ins["L2_ffn_Wd"].rearrange("(t e) f d -> (e f) t d", e=2)))
        loads.append((wd2[:, 8, :], ins["L2_ffn_Sd"]))
        loads.append((g["sgu2"][:, 0, :], ins["L2_ffn_Sg"]))
        loads.append((g["sgu2"][:, 1, :], ins["L2_ffn_Su"]))
        loads.append((g["wr2"][:, :], ins["L2_ffn_Wr"]))
        loads.append((g["wqkv3"][:, :], ins["L3_attn_w_qkv"]))
        loads.append((g["wout3"][:, :], ins["L3_attn_w_out"]))
        NL = len(loads)

        with nc.Block() as block:
            @block.sync
            def _(sp):
                for n, (dst, src) in enumerate(loads):
                    sp.dma_start(dst, src, allow_slow_non_contiguous=True).then_inc(loaded.sem, 16)
                sp.wait_ge(er_ready.sem, 1)
                for par in range(2):
                    for i in range(8):
                        rows = slice(64 * par + 8 * i, 64 * par + 8 * i + 8)
                        sp.dma_start(er_win[rows, :], er_rev[rows, 7 - i:7 - i + 2 * S - 8]).then_inc(shifted.sem, 16)
                sp.wait_ge(shifted.sem, 16 * 16)

            @block.scalar
            def _(act):
                act.dma_start(x_all[:, :].rearrange("p (t d) -> p t d", d=P), g["x_dram"]).then_inc(x_in.sem, 16)
                act.wait_ge(x_in.sem, 16)

            @block.vector
            def _(dve):
                n = [0]

                def did(ins_):
                    n[0] += 1
                    ins_.then_inc(chain.sem, 1)

                def settle():
                    dve.wait_ge(chain.sem, n[0])

                did(dve.memset(ones_row[:, :], 1.0))
                dve.wait_ge(loaded.sem, 16 * NL)
                did(dve.tensor_copy(raw[:, WG3:WG3 + 9, :], raw_int[:, :, :]))
                did(dve.tensor_scalar(raw[:, WF0, :], raw[:, WF0, :], 0.0, 2.0, ALU.is_ge, ALU.mult))
                did(dve.tensor_scalar(half_ident[:, :], c("ident"), 0.5, None, ALU.mult))
                did(dve.tensor_scalar(raw[:, WQ0, :], raw[:, WQ0, :], DK ** -0.5, None, ALU.mult))
                did(dve.tensor_scalar(col[:, 0:9], col[:, 0:9], DK ** -0.5, None, ALU.mult))
                did(dve.tensor_scalar(raw[:, WQ2, :], raw[:, WQ2, :], P ** -0.5, None, ALU.mult))
                did(dve.tensor_scalar(g["wqkv1"][:, 0:1024], g["wqkv1"][:, 0:1024], 64 ** -0.5, None, ALU.mult))
                did(dve.tensor_scalar(wd2[:, :, :], wd2[:, :, :], 0.25, None, ALU.mult))
                for t in range(2):
                    did(dve.tensor_copy(er_rep[:, t, :, :], er[:, t:t + 1, :].broadcast_to([P, HEADS, DK])))
                settle()
                did(dve.tensor_scalar(raw[:, WG3:WG3 + 9, :], raw[:, WG3:WG3 + 9, :], float(np.float32(1.0 / 127.0)), None, ALU.mult))
                did(dve.tensor_scalar(raw[:, WF0, :], raw[:, WF0, :], 1.0, scale0[:, 0:1], ALU.subtract, ALU.mult))
                for e in range(8):
                    did(dve.scalar_tensor_tensor(out=raw[:, WE1 + e, :], in0=raw[:, WE1 + e, :], scalar=0.5,
                                                 in1=half_ident[:, :], op0=ALU.mult, op1=ALU.add))
                settle()
                did(dve.tensor_scalar(raw[:, WD3:WD3 + 3, :], raw[:, WD3:WD3 + 3, :], 0.25, None, ALU.mult))
                settle()
                dve.memset(half_ident[0:1, 0:1], 0.5).then_inc(prepared.sem, 1)
                for b in range(7):
                    lo, hi = 4 * b, min(4 * b + 4, NWT)
                    dve.wait_ge(turned.sem, b + 1)
                    if hi == NWT:
                        did(dve.tensor_copy(wt[:, lo:lo + 1, :], bank[b][:, 0:P].rearrange("p (t d) -> p t d", d=P)))
                        did(dve.tensor_copy(wt[:, GW1, 0:8], bank[b][:, P:P + 8]))
                    else:
                        did(dve.tensor_copy(wt[:, lo:hi, :], bank[b][:, :].rearrange("p (t d) -> p t d", d=P)))
                dve.wait_ge(small_ps.sem, 1)
                did(dve.tensor_copy(th_rep[:, :], bank[7][:, 0:HEADS]))
                settle()
                did(dve.tensor_tensor(mix[:, :, :], th_rep[:, :].unsqueeze(2).broadcast_to([P, HEADS, 8]),
                                      c("step8").unsqueeze(1).broadcast_to([P, HEADS, 8]), ALU.mult))
                for hp in range(8):
                    for par in range(2):
                        h = par * 8 + hp
                        did(dve.tensor_copy(wqx[:, hp, 64 * par:64 * par + 64].rearrange("p (i d) -> p i d", d=DK),
                                            wt[:, WQ0:WQ0 + 1, DK * h:DK * h + DK].broadcast_to([P, 8, DK])))
                settle()
                dve.memset(half_ident[0:1, 0:1], 0.5).then_inc(moved.sem, 1)
                dve.wait_ge(small_ps.sem, 2)
                dve.tensor_copy(er_rev[:, :], bank[6][:, :]).then_inc(er_ready.sem, 1)

            @block.tensor
            def _(pe):
                pe.wait_ge(prepared.sem, 1)
                for b in range(7):
                    lo, hi = 4 * b, min(4 * b + 4, NWT)
                    for k in range(lo, hi):
                        rows = 8 if k == GW1 else P
                        last = pe.transpose(bank[b][:, (k - lo) * P:(k - lo) * P + rows], raw[0:rows, k, :],
                                            c("ident")[0:rows, 0:rows])
                    last.then_inc(turned.sem, 1)
                pe.matmul(bank[7][:, 0:HEADS], c("spread_heads")[0:HEADS, :], thT[:, :], start=True, stop=True).then_inc(small_ps.sem, 1)
                pe.wait_ge(moved.sem, 1)
                for t in range(2):
                    last = pe.matmul(bank[6][:, :], er_rep[:, t, :, :].rearrange("p h d -> p (h d)"), back[:, t, :],
                                     start=(t == 0), stop=(t == 1))
                last.then_inc(small_ps.sem, 1)


def x_tiles(g, t, n):
    return g["x_all"][:, bass.ds(t * (n * P), n * P)].rearrange("p (k d) -> p k d", d=P)


def norm_parts(nc, sb, pre, n):
    return {
        "n": n, "stats": sb(pre + "stats", [P, n, 6]), "mv": sb(pre + "mv", [P, n, 2]), "apart": sb(pre + "apart", [P, n]), "mean": sb(pre + "mean", [P, n]), "var": sb(pre + "var", [P, n]),
        "power": sb(pre + "power", [P, n]), "rstd": sb(pre + "rstd", [P, n]), "xn": sb(pre + "xn", [P, n, P]),
        "var_ready": Signal(nc, pre + "var_ready"), "rstd_ready": Signal(nc, pre + "rstd_ready"),
        "xn_ready": Signal(nc, pre + "xn_ready", n), "steps": Signal(nc, pre + "norm_steps", n + 5), "power_set": Signal(nc, pre + "power_set"),
    }


def norm_stats(dve, g, ln, t):
    n, x = ln["n"], x_tiles(g, t, ln["n"])
    ch = Chain(dve, ln["steps"], t)
    for k in range(n):
        ch.did(dve.bn_stats(ln["stats"][:, k, :], x[:, k, :]))
    ch.settle()
    ch.did(dve.tensor_tensor(ln["mv"][:, :, 0:2], ln["stats"][:, :, 1:3], ln["stats"][:, :, 4:6], ALU.add))
    ch.did(dve.tensor_tensor(ln["apart"][:, :], ln["stats"][:, :, 1], ln["stats"][:, :, 4], ALU.subtract))
    ch.settle()
    ch.did(dve.tensor_scalar(ln["mean"][:, :], ln["mv"][:, :, 0], 0.5, None, ALU.mult))
    ch.did(dve.tensor_tensor(ln["apart"][:, :], ln["apart"][:, :], ln["apart"][:, :], ALU.mult))
    ch.settle()
    ch.did(dve.scalar_tensor_tensor(out=ln["var"][:, :], in0=ln["apart"][:, :], scalar=P / 4, in1=ln["mv"][:, :, 1], op0=ALU.mult, op1=ALU.add))
    ch.settle()
    ch.end()
    dve.tensor_scalar(ln["var"][:, :], ln["var"][:, :], 1.0 / P, EPS, ALU.mult, ALU.add).then_inc(ln["var_ready"].sem, 1)


def norm_apply(dve, g, ln, t):
    n, x = ln["n"], x_tiles(g, t, ln["n"])
    dve.wait_ge(ln["rstd_ready"].sem, ln["rstd_ready"].at(t, 1))
    for k in range(n):
        dve.tensor_scalar(ln["xn"][:, k, :], x[:, k, :], ln["mean"][:, k:k + 1], ln["rstd"][:, k:k + 1],
                          ALU.subtract, ALU.mult).then_inc(ln["xn_ready"].sem, 1)


def norm_vector(dve, g, ln, t):
    norm_stats(dve, g, ln, t)
    norm_apply(dve, g, ln, t)


def norm_pool(pool, ln, t):
    pool.wait_ge(ln["var_ready"].sem, ln["var_ready"].at(t, 1))
    pool.tensor_tensor(ln["rstd"][:, :], ln["var"][:, :], ln["power"][:, :], ALU.pow).then_inc(ln["rstd_ready"].sem, 1)


def norm_pool_setup(pool, ln):
    pool.memset(ln["power"][:, :], -0.5).then_inc(ln["power_set"].sem, 1)
    pool.wait_ge(ln["power_set"].sem, 1)


def turn_tokens(pe, g, ln, ps, signal, t):
    for k in range(ln["n"]):
        pe.wait_ge(ln["xn_ready"].sem, ln["xn_ready"].at(t, k + 1))
        last = pe.transpose(ps[:, k * P:(k + 1) * P], ln["xn"][:, k, :], g["c"]("ident"))
    last.then_inc(signal.sem, 1)


def add_bias(pe, g, out, row, stop):
    return pe.matmul(out, g["ones_row"][:, :], g["bias_row"][:, row * P:(row + 1) * P], start=False, stop=stop)


def each_turn(eng, n, turn):
    if n > 1:
        with eng.Fori(0, n - 1) as t:
            turn(t, t + 1)
    turn(n - 1, None)


def ffn0(nc, g, NB, pre):
    N = 4
    with ExitStack() as ctx:
        sb = lambda name, shape, dt=F32: ctx.enter_context(nc.sbuf_tensor(name, shape, dt))
        ln = norm_parts(nc, sb, pre, N)
        xT = sb(pre + "xT", [P, N * P])
        y = sb(pre + "y", [P, N, P])
        xT_ps, xT_ready, y_ps, chain = Signal(nc, pre + "xT_ps"), Signal(nc, pre + "xT_ready"), Signal(nc, pre + "y_ps"), Signal(nc, pre + "chain", 2)
        turned, prod = g["bank"][0], g["bank"][1]
        turns = NB * 2 // N
        with nc.Block() as block:
            @block.vector
            def _(dve):
                def turn(t, nxt):
                    ch = Chain(dve, chain, t)
                    if nxt is not None:
                        norm_stats(dve, g, ln, nxt)
                    dve.wait_ge(y_ps.sem, y_ps.at(t, 1))
                    ch.did(dve.tensor_scalar(y[:, :, :], prod[:, :].rearrange("p (k d) -> p k d", d=P), 100.0, -100.0, ALU.min, ALU.max))
                    if nxt is not None:
                        norm_apply(dve, g, ln, nxt)
                    ch.settle()
                    x = x_tiles(g, t, N)
                    ch.did(dve.scalar_tensor_tensor(out=x, in0=y[:, :, :], scalar=0.5, in1=x, op0=ALU.mult, op1=ALU.add))
                    ch.settle()
                    ch.end()

                norm_vector(dve, g, ln, 0)
                each_turn(dve, turns, turn)

            @block.gpsimd
            def _(pool):
                norm_pool_setup(pool, ln)
                with pool.Fori(0, turns) as t:
                    norm_pool(pool, ln, t)

            @block.scalar
            def _(act):
                with act.Fori(0, turns) as t:
                    act.wait_ge(xT_ps.sem, xT_ps.at(t, 1))
                    act.copy(xT[:, :], turned[:, :]).then_inc(xT_ready.sem, 1)

            @block.tensor
            def _(pe):
                def turn(t, nxt):
                    pe.wait_ge(xT_ready.sem, xT_ready.at(t, 1))
                    for k in range(N):
                        pe.matmul(prod[:, k * P:(k + 1) * P], xT[:, k * P:(k + 1) * P], g["wt"][:, WF0, :], start=True, stop=False)
                        last = add_bias(pe, g, prod[:, k * P:(k + 1) * P], B_F0, True)
                    last.then_inc(y_ps.sem, 1)
                    if nxt is not None:
                        turn_tokens(pe, g, ln, turned, xT_ps, nxt)

                turn_tokens(pe, g, ln, turned, xT_ps, 0)
                each_turn(pe, turns, turn)


def ffn1(nc, g, NB, pre):
    N, E = 4, 8
    with ExitStack() as ctx:
        sb = lambda name, shape, dt=F32: ctx.enter_context(nc.sbuf_tensor(name, shape, dt))
        ln = norm_parts(nc, sb, pre, N)
        xT = sb(pre + "xT", [P, N * P])
        score = sb(pre + "score", [P, N, E])
        key = sb(pre + "key", [P, N, E])
        chosen = sb(pre + "chosen", [P, N, E])
        best = sb(pre + "best", [P, N])
        xT_ps, xT_ready, gate_ps = Signal(nc, pre + "xT_ps"), Signal(nc, pre + "xT_ready"), Signal(nc, pre + "gate_ps")
        y_ps = Signal(nc, pre + "y_ps", N)
        y_free = Signal(nc, pre + "y_free", N)
        chain = Signal(nc, pre + "chain", E * N)
        routing = Signal(nc, pre + "routing", 6)
        turned, gate = g["bank"][0], g["bank"][1]
        y_banks = [g["bank"][2:4], g["bank"][4:6]]
        turns = NB * 2 // N
        c = g["c"]
        with nc.Block() as block:
            @block.vector
            def _(dve):
                def route(t):
                    ch = Chain(dve, routing, t)
                    dve.wait_ge(gate_ps.sem, gate_ps.at(t, 1))
                    ch.did(dve.tensor_copy(score[:, :, :], gate[:, 0:N * E].rearrange("p (k e) -> p k e", e=E)))
                    ch.settle()
                    first_largest(dve, ch, score, best, key, chosen, c("rank8"), N, E)
                    ch.end()

                def turn(t, nxt):
                    ch = Chain(dve, chain, t)
                    for k in range(N):
                        x = x_tiles(g, t, N)[:, k, :]
                        dve.wait_ge(y_ps.sem, y_ps.at(t, k + 1))
                        for e in range(E):
                            y = y_banks[k % 2][e // 4][:, (e % 4) * P:(e % 4 + 1) * P]
                            ch.did(dve.scalar_tensor_tensor(out=x, in0=y, scalar=chosen[:, k, e:e + 1], in1=x, op0=ALU.mult, op1=ALU.add))
                            ch.settle()
                        dve.nop().then_inc(y_free.sem, 1)
                        if nxt is not None:
                            if k == 0:
                                norm_stats(dve, g, ln, nxt)
                            if k == 1:
                                norm_apply(dve, g, ln, nxt)
                    ch.end()
                    if nxt is not None:
                        route(nxt)

                dve.nop().then_inc(y_free.sem, 2)
                norm_vector(dve, g, ln, 0)
                route(0)
                each_turn(dve, turns, turn)

            @block.gpsimd
            def _(pool):
                norm_pool_setup(pool, ln)
                with pool.Fori(0, turns) as t:
                    norm_pool(pool, ln, t)

            @block.scalar
            def _(act):
                with act.Fori(0, turns) as t:
                    act.wait_ge(xT_ps.sem, xT_ps.at(t, 1))
                    act.copy(xT[:, :], turned[:, :]).then_inc(xT_ready.sem, 1)

            @block.tensor
            def _(pe):
                def gates(t):
                    pe.wait_ge(xT_ready.sem, xT_ready.at(t, 1))
                    for k in range(N):
                        last = pe.matmul(gate[:, k * E:(k + 1) * E], xT[:, k * P:(k + 1) * P], g["wt"][:, GW1, 0:E], start=True, stop=True)
                    last.then_inc(gate_ps.sem, 1)

                def turn(t, nxt):
                    for k in range(N):
                        pe.wait_ge(y_free.sem, y_free.at(t, k + 1))
                        for half in range(2):
                            last = pe.matmul(y_banks[k % 2][half][:, :], xT[:, k * P:(k + 1) * P],
                                             g["wt"][:, WE1 + 4 * half:WE1 + 4 * half + 4, :].rearrange("p e d -> p (e d)"), start=True, stop=True)
                        last.then_inc(y_ps.sem, 1)
                    if nxt is not None:
                        turn_tokens(pe, g, ln, turned, xT_ps, nxt)
                        gates(nxt)

                turn_tokens(pe, g, ln, turned, xT_ps, 0)
                gates(0)
                each_turn(pe, turns, turn)


def first_largest(dve, ch, value, best, key, chosen, rank, n, m):
    def over(v):
        return v[:, :].unsqueeze(2).broadcast_to([P, n, m])

    ch.did(dve.tensor_reduce(best[:, :], value[:, :, :], AX.X, ALU.max))
    ch.settle()
    ch.did(dve.tensor_tensor(key[:, :, :], value[:, :, :], over(best), ALU.is_equal))
    ch.settle()
    ch.did(dve.tensor_tensor(key[:, :, :], key[:, :, :], rank.unsqueeze(1).broadcast_to([P, n, m]), ALU.mult))
    ch.settle()
    ch.did(dve.tensor_reduce(best[:, :], key[:, :, :], AX.X, ALU.max))
    ch.settle()
    ch.did(dve.tensor_tensor(chosen[:, :, :], key[:, :, :], over(best), ALU.is_equal))
    ch.settle()


def ffn2(nc, g, NB, pre):
    N, E = 4, 16
    NP = E // 2 + 1
    with ExitStack() as ctx:
        sb = lambda name, shape, dt=F32: ctx.enter_context(nc.sbuf_tensor(name, shape, dt))
        ln = norm_parts(nc, sb, pre, N)
        xT_new = sb(pre + "xT_new", [P, N * P])
        xT = sb(pre + "xT", [P, N * P])
        prob = sb(pre + "prob", [P, N, E])
        rest = sb(pre + "rest", [P, N, E])
        key = sb(pre + "key", [P, N, E])
        one1 = sb(pre + "one1", [P, N, E])
        one2 = sb(pre + "one2", [P, N, E])
        weight = sb(pre + "weight", [P, N, E])
        top = sb(pre + "top", [P, N])
        best = sb(pre + "best", [P, N])
        total = sb(pre + "total", [P, N])
        rounded = sb(pre + "rounded", [P, 2, N, E], BF16)
        left = sb(pre + "left", [P, N, E])
        parts = sb(pre + "parts", [P, N, P // E, E])
        wT = sb(pre + "wT", [3 * E, N * P], BF16)
        pick = sb(pre + "pick", [3 * E, E // 2 * P], BF16)
        th = sb(pre + "th", [P, 2, N * P])
        hid = sb(pre + "hid", [P, 2, N * P])
        names = ("xT_ps", "xT_ready", "adopted", "logit_ps", "shifted", "exped", "weight_ready", "split", "wT_ps", "wT_ready", "pick_ready", "cleared")
        s = {n: Signal(nc, pre + n) for n in names}
        pair_ps, tanhed, hid_ready, hid_used = (Signal(nc, pre + n, NP) for n in ("pair_ps", "tanhed", "hid_ready", "hid_used"))
        chain = Signal(nc, pre + "chain", 2 * NP - 1)
        routing = Signal(nc, pre + "routing", 1 + 3 + 5 + 1 + 5 + 1)
        splitting = Signal(nc, pre + "splitting", 5)
        added = Signal(nc, pre + "added")
        misc, acc = g["bank"][0], g["bank"][1]
        gb, ub, cb = g["bank"][2:4], g["bank"][4:6], g["bank"][6:8]
        turns = NB * 2 // N
        c = g["c"]
        over = lambda v: v[:, :].unsqueeze(2).broadcast_to([P, N, E])
        with nc.Block() as block:
            @block.vector
            def _(dve):
                def shift(t, ch):
                    dve.wait_ge(s["logit_ps"].sem, s["logit_ps"].at(t, 1))
                    logit = misc[:, 0:N * E].rearrange("p (k e) -> p k e", e=E)
                    ch.did(dve.tensor_reduce(top[:, :], logit, AX.X, ALU.max))
                    ch.settle()
                    dve.tensor_tensor(rest[:, :, :], logit, over(top), ALU.subtract).then_inc(s["shifted"].sem, 1)

                def probabilities(t, ch):
                    dve.wait_ge(s["exped"].sem, s["exped"].at(t, 1))
                    ch.did(dve.tensor_reduce(total[:, :], key[:, :, :], AX.X, ALU.add))
                    ch.settle()
                    ch.did(dve.reciprocal(total[:, :], total[:, :]))
                    ch.settle()
                    ch.did(dve.tensor_tensor(prob[:, :, :], key[:, :, :], over(total), ALU.mult))
                    ch.settle()

                def first(ch):
                    first_largest(dve, ch, prob, best, key, one1, c("rank16"), N, E)

                def second(ch):
                    ch.did(dve.scalar_tensor_tensor(out=rest[:, :, :], in0=one1[:, :, :], scalar=-2.0, in1=prob[:, :, :], op0=ALU.mult, op1=ALU.add))
                    ch.settle()
                    first_largest(dve, ch, rest, best, key, one2, c("rank16"), N, E)
                    ch.did(dve.tensor_tensor(one2[:, :, :], one2[:, :, :], one1[:, :, :], ALU.add))
                    ch.settle()
                    ch.end()
                    dve.tensor_tensor(weight[:, :, :], prob[:, :, :], one2[:, :, :], ALU.mult).then_inc(s["weight_ready"].sem, 1)

                def split(t):
                    ch = Chain(dve, splitting, t)
                    dve.wait_ge(s["weight_ready"].sem, s["weight_ready"].at(t, 1))
                    ch.did(dve.tensor_copy(rounded[:, 0, :, :], weight[:, :, :]))
                    ch.settle()
                    ch.did(dve.tensor_copy(parts[:, :, 0, :], rounded[:, 0, :, :]))
                    ch.did(dve.tensor_tensor(left[:, :, :], weight[:, :, :], rounded[:, 0, :, :], ALU.subtract))
                    ch.settle()
                    ch.did(dve.tensor_copy(rounded[:, 1, :, :], left[:, :, :]))
                    ch.settle()
                    ch.did(dve.tensor_copy(parts[:, :, 1, :], rounded[:, 1, :, :]))
                    ch.settle()
                    ch.end()
                    dve.tensor_tensor(parts[:, :, 2, :], left[:, :, :], rounded[:, 1, :, :], ALU.subtract).then_inc(s["split"].sem, 1)

                def weights_in(t):
                    dve.wait_ge(s["wT_ps"].sem, s["wT_ps"].at(t, 1))
                    dve.tensor_copy(wT[:, :], misc[0:3 * E, :]).then_inc(s["wT_ready"].sem, 1)

                def turn(t, nxt):
                    ch = Chain(dve, chain, t)
                    if nxt is not None:
                        route = Chain(dve, routing, nxt)
                    for j in range(NP):
                        dve.wait_ge(tanhed.sem, tanhed.at(t, j + 1))
                        if j >= 2:
                            dve.wait_ge(hid_used.sem, hid_used.at(t, j - 1))
                        h = hid[:, j % 2, :]
                        ch.did(dve.scalar_tensor_tensor(out=h, in0=th[:, j % 2, :], scalar=1.0, in1=gb[j % 2][:, :], op0=ALU.add, op1=ALU.mult))
                        ch.settle()
                        if j < NP - 1:
                            ch.did(dve.tensor_tensor(h, h, ub[j % 2][:, :], ALU.mult))
                            ch.settle()
                            dve.tensor_tensor(h, h, cb[j % 2][:, :], ALU.mult).then_inc(hid_ready.sem, 1)
                        else:
                            dve.tensor_tensor(h, h, ub[j % 2][:, :], ALU.mult).then_inc(hid_ready.sem, 1)
                        if nxt is not None:
                            if j == 0:
                                norm_stats(dve, g, ln, nxt)
                            if j == 1:
                                norm_apply(dve, g, ln, nxt)
                            if j == 3:
                                shift(nxt, route)
                            if j == 4:
                                probabilities(nxt, route)
                                first(route)
                            if j == 5:
                                second(route)
                            if j == 6:
                                split(nxt)
                            if j == 7:
                                dve.wait_ge(pair_ps.sem, pair_ps.at(t, NP - 1))
                                weights_in(nxt)
                    ch.end()
                    dve.wait_ge(hid_used.sem, hid_used.at(t, NP))
                    x = x_tiles(g, t, N)
                    dve.tensor_tensor(x, acc[:, :].rearrange("p (k d) -> p k d", d=P), x, ALU.add).then_inc(added.sem, 1)

                dve.nop().then_inc(added.sem, 1)
                dve.memset(parts[:, :, :, :], 0.0).then_inc(s["cleared"].sem, 1)
                dve.tensor_copy(pick[:, :], c("pick_expert")[0:3 * E, :]).then_inc(s["pick_ready"].sem, 1)
                norm_vector(dve, g, ln, 0)
                route = Chain(dve, routing, 0)
                shift(0, route)
                probabilities(0, route)
                first(route)
                second(route)
                dve.wait_ge(s["cleared"].sem, 1)
                split(0)
                weights_in(0)
                each_turn(dve, turns, turn)

            @block.gpsimd
            def _(pool):
                norm_pool_setup(pool, ln)
                with pool.Fori(0, turns) as t:
                    norm_pool(pool, ln, t)

            @block.scalar
            def _(act):
                def x_in(t):
                    act.wait_ge(s["xT_ps"].sem, s["xT_ps"].at(t, 1))
                    act.copy(xT_new[:, :], misc[:, :]).then_inc(s["xT_ready"].sem, 1)

                def exponentials(t):
                    act.wait_ge(s["shifted"].sem, s["shifted"].at(t, 1))
                    act.activation(key[:, :, :], rest[:, :, :], ACT.Exp).then_inc(s["exped"].sem, 1)

                def adopt(t):
                    act.wait_ge(s["xT_ready"].sem, s["xT_ready"].at(t, 1))
                    act.copy(xT[:, :], xT_new[:, :]).then_inc(s["adopted"].sem, 1)

                def turn(t, nxt):
                    for j in range(NP):
                        act.wait_ge(pair_ps.sem, pair_ps.at(t, j + 1))
                        if j >= 2:
                            act.wait_ge(hid_ready.sem, hid_ready.at(t, j - 1))
                        act.activation(th[:, j % 2, :], gb[j % 2][:, :], ACT.Tanh, scale=0.5).then_inc(tanhed.sem, 1)
                        if nxt is not None:
                            if j == 2:
                                x_in(nxt)
                            if j == 4:
                                exponentials(nxt)
                    if nxt is not None:
                        adopt(nxt)

                x_in(0)
                adopt(0)
                exponentials(0)
                each_turn(act, turns, turn)

            @block.tensor
            def _(pe):
                def logits(t):
                    pe.wait_ge(s["xT_ready"].sem, s["xT_ready"].at(t, 1))
                    for k in range(N):
                        last = pe.matmul(misc[:, k * E:(k + 1) * E], xT_new[:, k * P:(k + 1) * P], g["wr2"][:, :], start=True, stop=True)
                    last.then_inc(s["logit_ps"].sem, 1)

                def turn_weights(t):
                    pe.wait_ge(s["split"].sem, s["split"].at(t, 1))
                    for k in range(N):
                        last = pe.transpose(misc[:, k * P:(k + 1) * P], parts[:, k, :, :].rearrange("p a e -> p (a e)"), c("ident"))
                    last.then_inc(s["wT_ps"].sem, 1)

                def down(t, j):
                    pe.wait_ge(hid_ready.sem, hid_ready.at(t, j + 1))
                    if j == 0:
                        pe.wait_ge(added.sem, added.at(t, 1))
                    for k in range(N):
                        last = pe.matmul(acc[:, k * P:(k + 1) * P], hid[:, j % 2, k * P:(k + 1) * P], g["wd2"][:, j, :],
                                         start=(j == 0 and k == 0), stop=(j == NP - 1), skip_group_check=True)
                    last.then_inc(hid_used.sem, 1)

                def turn(t, nxt):
                    pe.wait_ge(s["adopted"].sem, s["adopted"].at(t, 1))
                    pe.wait_ge(s["wT_ready"].sem, s["wT_ready"].at(t, 1))
                    for j in range(NP):
                        if j >= 2:
                            pe.wait_ge(hid_ready.sem, hid_ready.at(t, j - 1))
                        if j < NP - 1:
                            wg = g["wg2"][:, 2 * j:2 * j + 2, :].rearrange("p e f -> p (e f)")
                            wu = g["wu2"][:, 2 * j:2 * j + 2, :].rearrange("p e f -> p (e f)")
                            pe.matmul(cb[j % 2][:, :], pick[:, j * P:(j + 1) * P], wT[:, :], start=True, stop=True)
                        else:
                            wg, wu = g["sgu2"][:, 0, :], g["sgu2"][:, 1, :]
                        pe.matmul(gb[j % 2][:, :], wg, xT[:, :], start=True, stop=True)
                        pe.matmul(ub[j % 2][:, :], wu, xT[:, :], start=True, stop=True).then_inc(pair_ps.sem, 1)
                        if j >= 1:
                            down(t, j - 1)
                        if nxt is not None:
                            if j == 2:
                                turn_tokens(pe, g, ln, misc, s["xT_ps"], nxt)
                            if j == 3:
                                logits(nxt)
                            if j == 7:
                                turn_weights(nxt)
                    down(t, NP - 1)

                pe.wait_ge(s["pick_ready"].sem, 1)
                turn_tokens(pe, g, ln, misc, s["xT_ps"], 0)
                logits(0)
                turn_weights(0)
                each_turn(pe, turns, turn)


def ffn3(nc, g, NB, pre):
    N, NH = 4, 3
    with ExitStack() as ctx:
        sb = lambda name, shape, dt=F32: ctx.enter_context(nc.sbuf_tensor(name, shape, dt))
        ln = norm_parts(nc, sb, pre, N)
        xT = sb(pre + "xT", [P, N * P])
        th = sb(pre + "th", [P, NH, N * P])
        hid = sb(pre + "hid", [P, NH, N * P])
        xT_ps, xT_ready = Signal(nc, pre + "xT_ps"), Signal(nc, pre + "xT_ready")
        part_ps, tanhed, hid_ready, down_ps = (Signal(nc, pre + n, NH) for n in ("part_ps", "tanhed", "hid_ready", "down_ps"))
        chain = Signal(nc, pre + "chain", NH)
        added = Signal(nc, pre + "added")
        misc, acc = g["bank"][0], g["bank"][1]
        gb, ub = g["bank"][2:5], g["bank"][5:8]
        turns = NB * 2 // N
        with nc.Block() as block:
            @block.vector
            def _(dve):
                def turn(t, nxt):
                    ch = Chain(dve, chain, t)
                    for j in range(NH):
                        if nxt is not None and j == 0:
                            norm_stats(dve, g, ln, nxt)
                        dve.wait_ge(tanhed.sem, tanhed.at(t, j + 1))
                        ch.did(dve.scalar_tensor_tensor(out=hid[:, j, :], in0=th[:, j, :], scalar=1.0, in1=gb[j][:, :], op0=ALU.add, op1=ALU.mult))
                        ch.settle()
                        dve.tensor_tensor(hid[:, j, :], hid[:, j, :], ub[j][:, :], ALU.mult).then_inc(hid_ready.sem, 1)
                        if nxt is not None and j == 0:
                            norm_apply(dve, g, ln, nxt)
                    ch.end()
                    dve.wait_ge(down_ps.sem, down_ps.at(t, NH))
                    x = x_tiles(g, t, N)
                    dve.tensor_tensor(x, acc[:, :].rearrange("p (k d) -> p k d", d=P), x, ALU.add).then_inc(added.sem, 1)

                dve.nop().then_inc(added.sem, 1)
                norm_vector(dve, g, ln, 0)
                each_turn(dve, turns, turn)

            @block.gpsimd
            def _(pool):
                norm_pool_setup(pool, ln)
                with pool.Fori(0, turns) as t:
                    norm_pool(pool, ln, t)

            @block.scalar
            def _(act):
                def x_in(t):
                    act.wait_ge(xT_ps.sem, xT_ps.at(t, 1))
                    act.copy(xT[:, :], misc[:, :]).then_inc(xT_ready.sem, 1)

                def turn(t, nxt):
                    for j in range(NH):
                        act.wait_ge(part_ps.sem, part_ps.at(t, j + 1))
                        act.activation(th[:, j, :], gb[j][:, :], ACT.Tanh, scale=0.5).then_inc(tanhed.sem, 1)
                    if nxt is not None:
                        x_in(nxt)

                x_in(0)
                each_turn(act, turns, turn)

            @block.tensor
            def _(pe):
                def turn(t, nxt):
                    pe.wait_ge(xT_ready.sem, xT_ready.at(t, 1))
                    for j in range(NH):
                        pe.matmul(gb[j][:, :], g["wt"][:, WG3 + j, :], xT[:, :], start=True, stop=True)
                        pe.matmul(ub[j][:, :], g["wt"][:, WU3 + j, :], xT[:, :], start=True, stop=True).then_inc(part_ps.sem, 1)
                    if nxt is not None:
                        turn_tokens(pe, g, ln, misc, xT_ps, nxt)
                    pe.wait_ge(added.sem, added.at(t, 1))
                    for j in range(NH):
                        pe.wait_ge(hid_ready.sem, hid_ready.at(t, j + 1))
                        for k in range(N):
                            last = pe.matmul(acc[:, k * P:(k + 1) * P], hid[:, j, k * P:(k + 1) * P], g["wt"][:, WD3 + j, :],
                                             start=(j == 0 and k == 0), stop=(j == NH - 1), skip_group_check=True)
                        last.then_inc(down_ps.sem, 1)

                turn_tokens(pe, g, ln, misc, xT_ps, 0)
                each_turn(pe, turns, turn)


def att2(nc, g, NB, pre):
    N = 2
    with ExitStack() as ctx:
        sb = lambda name, shape, dt=F32: ctx.enter_context(nc.sbuf_tensor(name, shape, dt))
        ln = norm_parts(nc, sb, pre, N)
        xT = sb(pre + "xT", [P, S])
        qk = sb(pre + "qk", [P, 2, S])
        v = sb(pre + "v", [P, N, P])
        low = sb(pre + "low", [P, N])
        prob = sb(pre + "prob", [P, N, S])
        total = sb(pre + "total", [P, N])
        inv = sb(pre + "inv", [P, N])
        probT = sb(pre + "probT", [P, N, S])
        names = ("xT_ps", "xT_ready", "qk_ps", "qk_ready", "v_ps", "v_ready", "score_ps", "low_ready", "exped", "probT_ps", "probT_ready", "out_ps")
        s = {n: Signal(nc, pre + n, 2 if n == "exped" else 1) for n in names}
        chain = Signal(nc, pre + "chain", 3)
        turned, qk_b, v_b, score_b, probT_b, out_b = g["bank"][0:6]
        with nc.Block() as block:
            @block.vector
            def _(dve):
                def values_in(t):
                    dve.wait_ge(s["v_ps"].sem, s["v_ps"].at(t, 1))
                    dve.tensor_copy(v[:, :, :], v_b[:, 0:N * P].rearrange("p (k d) -> p k d", d=P)).then_inc(s["v_ready"].sem, 1)

                def turn(t, nxt):
                    ch = Chain(dve, chain, t)
                    if nxt is not None:
                        norm_stats(dve, g, ln, nxt)
                    dve.wait_ge(s["score_ps"].sem, s["score_ps"].at(t, 1))
                    dve.tensor_reduce(low[:, :], score_b[:, :].rearrange("p (k j) -> p k j", j=S), AX.X, ALU.max, negate=True).then_inc(s["low_ready"].sem, 1)
                    if nxt is not None:
                        norm_apply(dve, g, ln, nxt)
                    dve.wait_ge(s["exped"].sem, s["exped"].at(t, 2))
                    ch.did(dve.reciprocal(inv[:, :], total[:, :]))
                    ch.settle()
                    dve.wait_ge(s["out_ps"].sem, s["out_ps"].at(t, 1))
                    for k in range(N):
                        x = x_tiles(g, t, N)[:, k, :]
                        ch.did(dve.scalar_tensor_tensor(out=x, in0=out_b[:, k * P:(k + 1) * P], scalar=inv[:, k:k + 1], in1=x, op0=ALU.mult, op1=ALU.add))
                    ch.settle()
                    ch.end()
                    if nxt is not None:
                        values_in(nxt)

                norm_vector(dve, g, ln, 0)
                values_in(0)
                each_turn(dve, NB, turn)

            @block.gpsimd
            def _(pool):
                norm_pool_setup(pool, ln)
                with pool.Fori(0, NB) as t:
                    norm_pool(pool, ln, t)

            @block.scalar
            def _(act):
                def x_in(t):
                    act.wait_ge(s["xT_ps"].sem, s["xT_ps"].at(t, 1))
                    act.copy(xT[:, :], turned[:, 0:S]).then_inc(s["xT_ready"].sem, 1)

                def queries_and_keys(t):
                    act.wait_ge(s["qk_ps"].sem, s["qk_ps"].at(t, 1))
                    act.copy(qk[:, :, :], qk_b[:, :].rearrange("p (a i) -> p a i", a=2)).then_inc(s["qk_ready"].sem, 1)

                def turn(t, nxt):
                    act.wait_ge(s["low_ready"].sem, s["low_ready"].at(t, 1))
                    for k in range(N):
                        act.activation(prob[:, k, :], score_b[:, k * S:(k + 1) * S], ACT.Exp, bias=low[:, k:k + 1],
                                       accum_out=total[:, k:k + 1]).then_inc(s["exped"].sem, 1)
                    if nxt is not None:
                        x_in(nxt)
                    act.wait_ge(s["probT_ps"].sem, s["probT_ps"].at(t, 1))
                    act.copy(probT[:, :, :], probT_b[:, :].rearrange("p (k i) -> p k i", k=N)).then_inc(s["probT_ready"].sem, 1)
                    if nxt is not None:
                        queries_and_keys(nxt)

                x_in(0)
                queries_and_keys(0)
                each_turn(act, NB, turn)

            @block.tensor
            def _(pe):
                def project(t):
                    pe.wait_ge(s["xT_ready"].sem, s["xT_ready"].at(t, 1))
                    for a in range(2):
                        last = pe.matmul(qk_b[:, a * S:(a + 1) * S], g["wt"][:, WQ2 + a, :], xT[:, :], start=True, stop=True)
                    last.then_inc(s["qk_ps"].sem, 1)
                    for k in range(N):
                        last = pe.matmul(v_b[:, k * P:(k + 1) * P], xT[:, k * P:(k + 1) * P], g["wt"][:, WV2, :], start=True, stop=True)
                    last.then_inc(s["v_ps"].sem, 1)

                def turn(t, nxt):
                    pe.wait_ge(s["qk_ready"].sem, s["qk_ready"].at(t, 1))
                    for k in range(N):
                        last = pe.matmul(score_b[:, k * S:(k + 1) * S], qk[:, 0, k * P:(k + 1) * P], qk[:, 1, :], start=True, stop=True)
                    last.then_inc(s["score_ps"].sem, 1)
                    if nxt is not None:
                        turn_tokens(pe, g, ln, turned, s["xT_ps"], nxt)
                    for k in range(N):
                        pe.wait_ge(s["exped"].sem, s["exped"].at(t, k + 1))
                        for j in range(N):
                            last = pe.transpose(probT_b[:, j * S + k * P:j * S + (k + 1) * P], prob[:, k, j * P:(j + 1) * P], g["c"]("ident"))
                    last.then_inc(s["probT_ps"].sem, 1)
                    pe.wait_ge(s["v_ready"].sem, s["v_ready"].at(t, 1))
                    if nxt is not None:
                        project(nxt)
                    pe.wait_ge(s["probT_ready"].sem, s["probT_ready"].at(t, 1))
                    for k in range(N):
                        for j in range(N):
                            last = pe.matmul(out_b[:, k * P:(k + 1) * P], probT[:, j, k * P:(k + 1) * P], v[:, j, :], start=(j == 0), stop=(j == N - 1))
                    last.then_inc(s["out_ps"].sem, 1)

                turn_tokens(pe, g, ln, turned, s["xT_ps"], 0)
                project(0)
                each_turn(pe, NB, turn)


def att0(nc, g, NB, pre):
    N, U, R = 2, S // 8, S // 16
    with ExitStack() as ctx:
        sb = lambda name, shape, dt=F32: ctx.enter_context(nc.sbuf_tensor(name, shape, dt))
        ln = norm_parts(nc, sb, pre, N)
        xT = sb(pre + "xT", [P, S])
        q = sb(pre + "q", [P, S])
        k = sb(pre + "k", [P, S])
        v = sb(pre + "v", [P, N, HEADS * (P + DK)])
        q_heads = sb(pre + "q_heads", [P, U, HEADS, 8])
        q_steps = sb(pre + "q_steps", [P, U, HEADS, 8])
        low = sb(pre + "low", [P, 2, 2])
        total = sb(pre + "total", [P, 2, 2])
        inv = sb(pre + "inv", [P, 2, 2])
        prob = sb(pre + "prob", [P, 2, 2, S])
        probT = sb(pre + "probT", [P, N, HEADS, S])
        oT = sb(pre + "oT", [P, S])
        s = {n: Signal(nc, pre + n) for n in ("xT_ps", "xT_ready", "proj_ps", "q_ready", "k_ready", "v_ready",
                                              "o_ps", "oT_ready", "out_ps", "cleared", "added")}
        qx_ps, qx_read, heads_ready = Signal(nc, pre + "qx_ps", 4), Signal(nc, pre + "qx_read", 4), Signal(nc, pre + "heads_ready", 4)
        score_ps, low_ready, inverted, normed, probT_ps, moved_act, moved_dve = (Signal(nc, pre + n, R) for n in (
            "score_ps", "low_ready", "inverted", "normed", "probT_ps", "moved_act", "moved_dve"))
        exped = Signal(nc, pre + "exped", 2 * R)
        bank = g["bank"]
        turned, qk_b, score_b, flip_b, o_b = bank[0], bank[1], bank[2:4], bank[4:6], bank[6]
        v_b, out_b = turned[:, S:2 * S], o_b[:, S:2 * S]
        qx_b = (bank[7], score_b[0])
        c = g["c"]

        def flipped(r, j):
            src = flip_b[r % 2][:, :].rearrange("p (k j h i) -> p k j h i", k=2, j=N, i=8)[:, :, j, :, :]
            dst = probT[:, j, :, 16 * r:16 * r + 16].rearrange("p h (k i) -> p k h i", k=2)
            return dst, src

        with nc.Block() as block:
            @block.vector
            def _(dve):
                def steps_in(t):
                    for w in range(4):
                        dve.wait_ge(qx_ps.sem, qx_ps.at(t, w + 1))
                        for m in range(2):
                            hp = 2 * w + m
                            for par in range(2):
                                rows = slice(64 * par, 64 * par + 64)
                                last = dve.scalar_tensor_tensor(
                                    out=q_steps[rows, :, 8 * par + hp, :], in0=qx_b[w % 2][rows, m * S:(m + 1) * S].rearrange("p (u i) -> p u i", i=8),
                                    scalar=g["col"][rows, hp:hp + 1], in1=c("step_of")[rows, :].rearrange("p (u i) -> p u i", i=8),
                                    op0=ALU.add, op1=ALU.mult)
                        last.then_inc(qx_read.sem, 1)

                def values_in(t):
                    dve.wait_ge(s["proj_ps"].sem, s["proj_ps"].at(t, 1))
                    for n in range(N):
                        last = dve.tensor_copy(v[:, n, :].rearrange("p (h c) -> p h c", h=HEADS)[:, :, 0:DK],
                                               v_b[:, n * P:(n + 1) * P].rearrange("p (h d) -> p h d", d=DK))
                    last.then_inc(s["v_ready"].sem, 1)

                def turn(t, nxt):
                    for r in range(R + 2):
                        if r < R:
                            dve.wait_ge(score_ps.sem, score_ps.at(t, r + 1))
                            if r >= 2:
                                dve.wait_ge(exped.sem, exped.at(t, 2 * (r - 1)))
                            dve.tensor_reduce(low[:, r % 2, :], score_b[r % 2][:, :].rearrange("p (k j) -> p k j", j=S),
                                              AX.X, ALU.max, negate=True).then_inc(low_ready.sem, 1)
                        if 1 <= r <= R:
                            m = (r - 1) % 2
                            dve.wait_ge(exped.sem, exped.at(t, 2 * r))
                            dve.reciprocal(inv[:, m, :], total[:, m, :]).then_inc(inverted.sem, 1)
                            dve.wait_ge(inverted.sem, inverted.at(t, r))
                            for half in range(2):
                                last = dve.tensor_scalar(prob[:, m, half, :], prob[:, m, half, :], inv[:, m, half:half + 1], None, ALU.mult)
                            last.then_inc(normed.sem, 1)
                        if r >= 2:
                            dve.wait_ge(probT_ps.sem, probT_ps.at(t, r - 1))
                            dve.wait_ge(moved_act.sem, moved_act.at(t, r - 1))
                            dve.tensor_copy(*flipped(r - 2, 1)).then_inc(moved_dve.sem, 1)
                        if nxt is not None:
                            if r == 1:
                                norm_stats(dve, g, ln, nxt)
                            if r == 2:
                                norm_apply(dve, g, ln, nxt)
                    if nxt is not None:
                        steps_in(nxt)
                        dve.wait_ge(s["o_ps"].sem, s["o_ps"].at(t, 1))
                        values_in(nxt)
                    dve.wait_ge(s["out_ps"].sem, s["out_ps"].at(t, 1))
                    x = x_tiles(g, t, N)
                    dve.tensor_tensor(x, out_b.rearrange("p (k d) -> p k d", d=P), x, ALU.add).then_inc(s["added"].sem, 1)

                dve.memset(q_steps[:, :, :, :], 0.0).then_inc(s["cleared"].sem, 1)
                dve.memset(v[:, :, :], 0.0).then_inc(s["cleared"].sem, 1)
                dve.wait_ge(s["cleared"].sem, 2)
                norm_vector(dve, g, ln, 0)
                steps_in(0)
                values_in(0)
                each_turn(dve, NB, turn)

            @block.gpsimd
            def _(pool):
                def heads_in(t, before):
                    pool.wait_ge(s["q_ready"].sem, s["q_ready"].at(t, 1))
                    for w in range(4):
                        if before is not None:
                            pool.wait_ge(score_ps.sem, score_ps.at(before, 4 * w + 4))
                        us = slice(8 * w, 8 * w + 8)
                        pool.tensor_tensor(q_heads[:, us, :, :],
                                           q[:, 64 * w:64 * w + 64].rearrange("p (u i) -> p u i", i=8).unsqueeze(2).broadcast_to([P, 8, HEADS, 8]),
                                           c("head_of").unsqueeze(1).unsqueeze(3).broadcast_to([P, 8, HEADS, 8]),
                                           ALU.mult).then_inc(heads_ready.sem, 1)

                def turn(t, nxt):
                    if nxt is not None:
                        norm_pool(pool, ln, nxt)
                        heads_in(nxt, t)

                norm_pool_setup(pool, ln)
                norm_pool(pool, ln, 0)
                heads_in(0, None)
                each_turn(pool, NB, turn)

            @block.scalar
            def _(act):
                def x_in(t):
                    act.wait_ge(s["xT_ps"].sem, s["xT_ps"].at(t, 1))
                    act.copy(xT[:, :], turned[:, 0:S]).then_inc(s["xT_ready"].sem, 1)

                def queries_in(t):
                    act.wait_ge(s["proj_ps"].sem, s["proj_ps"].at(t, 1))
                    act.activation(q[:, :], qk_b[:, 0:S], ACT.Identity, bias=g["col"][:, 8:9]).then_inc(s["q_ready"].sem, 1)

                def keys_in(t):
                    act.activation(k[:, :], qk_b[:, S:2 * S], ACT.Identity, bias=g["col"][:, 9:10]).then_inc(s["k_ready"].sem, 1)

                def turn(t, nxt):
                    for r in range(R + 2):
                        if r < R:
                            act.wait_ge(low_ready.sem, low_ready.at(t, r + 1))
                            if r >= 2:
                                act.wait_ge(probT_ps.sem, probT_ps.at(t, r - 1))
                            for m in range(2):
                                act.activation(prob[:, r % 2, m, :], score_b[r % 2][:, m * S:(m + 1) * S], ACT.Exp,
                                               bias=low[:, r % 2, m:m + 1], accum_out=total[:, r % 2, m:m + 1]).then_inc(exped.sem, 1)
                        if r >= 2:
                            act.wait_ge(probT_ps.sem, probT_ps.at(t, r - 1))
                            act.copy(*flipped(r - 2, 0)).then_inc(moved_act.sem, 1)
                        if nxt is not None:
                            if r == 6:
                                x_in(nxt)
                            if r == 8:
                                queries_in(nxt)
                            if r == R - 1:
                                keys_in(nxt)
                    act.wait_ge(s["o_ps"].sem, s["o_ps"].at(t, 1))
                    act.copy(oT[:, :], o_b[:, 0:S]).then_inc(s["oT_ready"].sem, 1)

                x_in(0)
                queries_in(0)
                keys_in(0)
                each_turn(act, NB, turn)

            @block.tensor
            def _(pe):
                def project(t):
                    pe.wait_ge(s["xT_ready"].sem, s["xT_ready"].at(t, 1))
                    for a in range(2):
                        pe.matmul(qk_b[:, a * S:(a + 1) * S], g["wt"][:, WQ0 + a, :], xT[:, :], start=True, stop=True)
                    for n in range(N):
                        pe.matmul(v_b[:, n * P:(n + 1) * P], xT[:, n * P:(n + 1) * P], g["wt"][:, WV0, :], start=True, stop=False)
                        last = add_bias(pe, g, v_b[:, n * P:(n + 1) * P], B_V0, True)
                    last.then_inc(s["proj_ps"].sem, 1)

                def repeated_queries(t, w):
                    if w >= 2:
                        pe.wait_ge(qx_read.sem, qx_read.at(t, w - 1))
                    for m in range(2):
                        last = pe.matmul(qx_b[w % 2][:, m * S:(m + 1) * S], g["wqx"][:, 2 * w + m, :], xT[:, :], start=True, stop=True)
                    last.then_inc(qx_ps.sem, 1)

                def scores(t, r):
                    if r >= 2:
                        pe.wait_ge(exped.sem, exped.at(t, 2 * (r - 1)))
                    if r == 0:
                        pe.wait_ge(s["k_ready"].sem, s["k_ready"].at(t, 1))
                        pe.wait_ge(qx_read.sem, qx_read.at(t, 4))
                    if r % 4 == 0:
                        pe.wait_ge(heads_ready.sem, heads_ready.at(t, r // 4 + 1))
                    for m in range(2):
                        u = 2 * r + m
                        dst = score_b[r % 2][:, m * S:(m + 1) * S]
                        pe.matmul(dst, q_heads[:, u, :, :].rearrange("p h i -> p (h i)"), k[:, :], start=True, stop=False)
                        last = pe.matmul(dst, q_steps[:, u, :, :].rearrange("p h i -> p (h i)"), g["er_win"][:, S - 8 - 8 * u:2 * S - 8 - 8 * u],
                                         start=False, stop=True)
                    last.then_inc(score_ps.sem, 1)

                def flips(t, r):
                    pe.wait_ge(normed.sem, normed.at(t, r + 1))
                    if r >= 2:
                        pe.wait_ge(moved_dve.sem, moved_dve.at(t, r - 1))
                    for m in range(2):
                        for j in range(N):
                            last = pe.transpose(flip_b[r % 2][:, (2 * m + j) * P:(2 * m + j + 1) * P], prob[:, r % 2, m, j * P:(j + 1) * P], c("ident"))
                    last.then_inc(probT_ps.sem, 1)

                def turn(t, nxt):
                    scores(t, 1)
                    for r in range(R):
                        if r + 2 < R:
                            scores(t, r + 2)
                        flips(t, r)
                        if nxt is not None:
                            if r == 4:
                                turn_tokens(pe, g, ln, turned, s["xT_ps"], nxt)
                            if r == 6:
                                project(nxt)
                    if nxt is not None:
                        for w in range(2):
                            repeated_queries(nxt, w)
                    pe.wait_ge(s["v_ready"].sem, s["v_ready"].at(t, 1))
                    pe.wait_ge(moved_dve.sem, moved_dve.at(t, R))
                    for h in range(HEADS):
                        for j in range(N):
                            last = pe.matmul(o_b[:, 0:S], v[:, j, h * P:(h + 1) * P], probT[:, j, h, :],
                                             start=(h == 0 and j == 0), stop=(h == HEADS - 1 and j == N - 1))
                        if nxt is not None and h in (5, 8):
                            repeated_queries(nxt, 2 if h == 5 else 3)
                    last.then_inc(s["o_ps"].sem, 1)
                    if nxt is not None:
                        scores(nxt, 0)
                    pe.wait_ge(s["oT_ready"].sem, s["oT_ready"].at(t, 1))
                    for n in range(N):
                        pe.matmul(out_b[:, n * P:(n + 1) * P], oT[:, n * P:(n + 1) * P], g["wt"][:, WO0, :], start=True, stop=False)
                        last = add_bias(pe, g, out_b[:, n * P:(n + 1) * P], B_O0, True)
                    last.then_inc(s["out_ps"].sem, 1)

                pe.wait_ge(s["cleared"].sem, 2)
                turn_tokens(pe, g, ln, turned, s["xT_ps"], 0)
                project(0)
                for w in range(4):
                    repeated_queries(0, w)
                scores(0, 0)
                each_turn(pe, NB, turn)


def att3(nc, g, NB, pre):
    N = 2
    with ExitStack() as ctx:
        sb = lambda name, shape, dt=F32: ctx.enter_context(nc.sbuf_tensor(name, shape, dt))
        ln = norm_parts(nc, sb, pre, N)
        xT = sb(pre + "xT", [P, S])
        lin = sb(pre + "lin", [P, 2, S])
        neg = sb(pre + "neg", [P, 2, S])
        feat = sb(pre + "feat", [P, 2, S])
        rot = sb(pre + "rot", [P, 2, S])
        part = sb(pre + "part", [P, 2, S])
        q = sb(pre + "q", [P, 2, S])
        k_pick = sb(pre + "k_pick", [P, 2, HEADS, S])
        v = sb(pre + "v", [P, N, HEADS * (P + DK)])
        log_den = sb(pre + "log_den", [P, 2, N * S])
        inv = sb(pre + "inv", [P, 2, N * S])
        miss = sb(pre + "miss", [P, 2, N * S])
        rough = sb(pre + "rough", [P, 2, N * S])
        w = sb(pre + "w", [P, 2, N, S])
        oT = sb(pre + "oT", [P, S])
        s = {n: Signal(nc, pre + n) for n in ("xT_ps", "xT_ready", "qk_ps", "neg_ready", "exped", "feat_ready", "swap_ps", "rot_ready",
                                              "v_ps", "v_ready", "oT_ready", "out_ps", "cleared")}
        lin_ready, pick_ready, q_ready = Signal(nc, pre + "lin_ready", 2), Signal(nc, pre + "pick_ready", 8), Signal(nc, pre + "q_ready", 2)
        den_ps, num_ps, logged, inverted, w_ready, w_used = (Signal(nc, pre + n, HEADS) for n in (
            "den_ps", "num_ps", "logged", "inverted", "w_ready", "w_used"))
        rotated = Signal(nc, pre + "rotated", 2)
        refined = Signal(nc, pre + "refined", 2 * HEADS)
        added = Signal(nc, pre + "added")
        bank = g["bank"]
        turned, qk_b, swap_b, o_b, num_b, den_b = bank[0], bank[1], bank[2], bank[3], bank[4:6], bank[6:8]
        v_b = turned[:, S:2 * S]
        c = g["c"]
        flat = lambda a: a[:, :, :].rearrange("p a i -> p (a i)")
        with nc.Block() as block:
            @block.vector
            def _(dve):
                def negatives(t):
                    dve.wait_ge(lin_ready.sem, lin_ready.at(t, 2))
                    dve.tensor_scalar(flat(neg), flat(lin), 0.0, None, ALU.min).then_inc(s["neg_ready"].sem, 1)

                def features(t):
                    dve.wait_ge(s["exped"].sem, s["exped"].at(t, 1))
                    dve.scalar_tensor_tensor(out=flat(feat), in0=flat(lin), scalar=0.0, in1=flat(neg), op0=ALU.max, op1=ALU.add).then_inc(s["feat_ready"].sem, 1)

                def turn_features(t):
                    dve.wait_ge(s["feat_ready"].sem, s["feat_ready"].at(t, 1))
                    dve.tensor_tensor(flat(part), flat(feat), c("cos"), ALU.mult).then_inc(rotated.sem, 1)
                    dve.wait_ge(s["swap_ps"].sem, s["swap_ps"].at(t, 1))
                    dve.tensor_tensor(flat(rot), swap_b[:, :], c("sin"), ALU.mult).then_inc(rotated.sem, 1)
                    dve.wait_ge(rotated.sem, rotated.at(t, 2))
                    dve.tensor_tensor(flat(rot), flat(rot), flat(part), ALU.add).then_inc(s["rot_ready"].sem, 1)

                def values_in(t):
                    dve.wait_ge(s["v_ps"].sem, s["v_ps"].at(t, 1))
                    for n in range(N):
                        last = dve.tensor_scalar(v[:, n, :].rearrange("p (h c) -> p h c", h=HEADS)[:, :, 0:DK],
                                                 v_b[:, n * P:(n + 1) * P].rearrange("p (h d) -> p h d", d=DK), -1.0, None, ALU.mult)
                    last.then_inc(s["v_ready"].sem, 1)

                def turn(t, nxt):
                    for h in range(HEADS):
                        if h >= 2:
                            dve.wait_ge(w_ready.sem, w_ready.at(t, h - 1))
                        dve.wait_ge(inverted.sem, inverted.at(t, h + 1))
                        dve.tensor_tensor(miss[:, h % 2, :], den_b[h % 2][:, :], inv[:, h % 2, :], ALU.mult).then_inc(refined.sem, 1)
                        dve.wait_ge(num_ps.sem, num_ps.at(t, h + 1))
                        dve.tensor_tensor(rough[:, h % 2, :], num_b[h % 2][:, :], inv[:, h % 2, :], ALU.mult).then_inc(refined.sem, 1)
                        dve.wait_ge(refined.sem, refined.at(t, 2 * h + 2))
                        if h >= 2:
                            dve.wait_ge(w_used.sem, w_used.at(t, h - 1))
                        dve.scalar_tensor_tensor(out=w[:, h % 2, :, :].rearrange("p n i -> p (n i)"), in0=miss[:, h % 2, :], scalar=2.0, in1=rough[:, h % 2, :],
                                                 op0=ALU.subtract, op1=ALU.mult).then_inc(w_ready.sem, 1)
                        if nxt is not None:
                            if h == 0:
                                norm_vector(dve, g, ln, nxt)
                            if h == 5:
                                negatives(nxt)
                            if h == 6:
                                dve.wait_ge(pick_ready.sem, pick_ready.at(t, 8))
                                dve.wait_ge(q_ready.sem, q_ready.at(t, 2))
                                features(nxt)
                            if h == 7:
                                turn_features(nxt)
                    if nxt is not None:
                        dve.wait_ge(w_used.sem, w_used.at(t, HEADS))
                        values_in(nxt)
                    dve.wait_ge(s["out_ps"].sem, s["out_ps"].at(t, 1))
                    x = x_tiles(g, t, N)
                    dve.tensor_tensor(x, swap_b[:, 0:N * P].rearrange("p (k d) -> p k d", d=P), x, ALU.add).then_inc(added.sem, 1)

                dve.memset(v[:, :, :], 0.0).then_inc(s["cleared"].sem, 1)
                dve.wait_ge(s["cleared"].sem, 1)
                norm_vector(dve, g, ln, 0)
                negatives(0)
                features(0)
                turn_features(0)
                values_in(0)
                each_turn(dve, NB, turn)

            @block.gpsimd
            def _(pool):
                def picks(t, before):
                    pool.wait_ge(s["rot_ready"].sem, s["rot_ready"].at(t, 1))
                    for b in range(4):
                        hs = slice(4 * b, 4 * b + 4)
                        pick = c("head_of")[:, hs].unsqueeze(2).broadcast_to([P, 4, S])
                        if before is not None:
                            pool.wait_ge(num_ps.sem, num_ps.at(before, 4 * b + 4))
                        for kind, src in ((0, feat), (1, rot)):
                            pool.tensor_tensor(k_pick[:, kind, hs, :], src[:, 1:2, :].broadcast_to([P, 4, S]), pick, ALU.mult).then_inc(pick_ready.sem, 1)

                def turn(t, nxt):
                    if nxt is not None:
                        norm_pool(pool, ln, nxt)
                        picks(nxt, t)

                norm_pool_setup(pool, ln)
                norm_pool(pool, ln, 0)
                picks(0, None)
                each_turn(pool, NB, turn)

            @block.scalar
            def _(act):
                def x_in(t):
                    act.wait_ge(s["xT_ps"].sem, s["xT_ps"].at(t, 1))
                    act.copy(xT[:, :], turned[:, 0:S]).then_inc(s["xT_ready"].sem, 1)

                def linear(t):
                    act.wait_ge(s["qk_ps"].sem, s["qk_ps"].at(t, 1))
                    for a in range(2):
                        act.activation(lin[:, a, :], qk_b[:, a * S:(a + 1) * S], ACT.Identity, bias=g["col"][:, 10 + a:11 + a]).then_inc(lin_ready.sem, 1)

                def exponentials(t):
                    act.wait_ge(s["neg_ready"].sem, s["neg_ready"].at(t, 1))
                    act.activation(flat(neg), flat(neg), ACT.Exp).then_inc(s["exped"].sem, 1)

                def queries(t):
                    act.wait_ge(s["feat_ready"].sem, s["feat_ready"].at(t, 1))
                    act.copy(q[:, 0, :], feat[:, 0, :]).then_inc(q_ready.sem, 1)
                    act.wait_ge(s["rot_ready"].sem, s["rot_ready"].at(t, 1))
                    act.copy(q[:, 1, :], rot[:, 0, :]).then_inc(q_ready.sem, 1)

                def turn(t, nxt):
                    for h in range(HEADS):
                        act.wait_ge(den_ps.sem, den_ps.at(t, h + 1))
                        if h >= 2:
                            act.wait_ge(inverted.sem, inverted.at(t, h - 1))
                        act.activation(log_den[:, h % 2, :], den_b[h % 2][:, :], ACT.Ln).then_inc(logged.sem, 1)
                        act.wait_ge(logged.sem, logged.at(t, h + 1))
                        if h >= 2:
                            act.wait_ge(w_ready.sem, w_ready.at(t, h - 1))
                        act.activation(inv[:, h % 2, :], log_den[:, h % 2, :], ACT.Exp, scale=-1.0).then_inc(inverted.sem, 1)
                        if nxt is not None:
                            if h == 3:
                                x_in(nxt)
                            if h == 4:
                                linear(nxt)
                            if h == 5:
                                exponentials(nxt)
                    if nxt is not None:
                        act.wait_ge(num_ps.sem, num_ps.at(t, HEADS))
                        queries(nxt)
                    act.wait_ge(w_used.sem, w_used.at(t, HEADS))
                    act.copy(oT[:, :], o_b[:, 0:S]).then_inc(s["oT_ready"].sem, 1)

                act.add_instruction(mybir.InstLoadActFuncSet(name=nc.get_next_instruction_name(), act_func_set_id=6))
                x_in(0)
                linear(0)
                exponentials(0)
                queries(0)
                each_turn(act, NB, turn)

            @block.tensor
            def _(pe):
                def project(t):
                    pe.wait_ge(s["xT_ready"].sem, s["xT_ready"].at(t, 1))
                    for a in range(2):
                        last = pe.matmul(qk_b[:, a * S:(a + 1) * S], g["wqkv3"][:, a * P:(a + 1) * P], xT[:, :], start=True, stop=True)
                    last.then_inc(s["qk_ps"].sem, 1)
                    for n in range(N):
                        pe.matmul(v_b[:, n * P:(n + 1) * P], xT[:, n * P:(n + 1) * P], g["wqkv3"][:, 2 * P:3 * P], start=True, stop=False)
                        last = add_bias(pe, g, v_b[:, n * P:(n + 1) * P], B_V3, True)
                    last.then_inc(s["v_ps"].sem, 1)

                def swap(t):
                    pe.wait_ge(s["feat_ready"].sem, s["feat_ready"].at(t, 1))
                    pe.matmul(swap_b[:, :], c("swap"), flat(feat), start=True, stop=True).then_inc(s["swap_ps"].sem, 1)

                def weights(t, h):
                    if h % 4 == 0:
                        pe.wait_ge(pick_ready.sem, pick_ready.at(t, 2 * (h // 4) + 2))
                    for kind, banks, done in ((0, den_b, den_ps), (1, num_b, num_ps)):
                        if h >= 2:
                            pe.wait_ge(w_ready.sem, w_ready.at(t, h - 1))
                        for j in range(N):
                            last = pe.matmul(banks[h % 2][:, j * S:(j + 1) * S], k_pick[:, kind, h, j * P:(j + 1) * P],
                                             q[:, kind, :], start=True, stop=True)
                        last.then_inc(done.sem, 1)

                def values(t, h):
                    pe.wait_ge(w_ready.sem, w_ready.at(t, h + 1))
                    for j in range(N):
                        last = pe.matmul(o_b[:, 0:S], v[:, j, h * P:(h + 1) * P], w[:, h % 2, j, :],
                                         start=(h == 0 and j == 0), stop=(h == HEADS - 1 and j == N - 1))
                    last.then_inc(w_used.sem, 1)

                def turn(t, nxt):
                    pe.wait_ge(q_ready.sem, q_ready.at(t, 2))
                    weights(t, 0)
                    pe.wait_ge(s["v_ready"].sem, s["v_ready"].at(t, 1))
                    for h in range(HEADS):
                        if h + 1 < HEADS:
                            weights(t, h + 1)
                        values(t, h)
                        if nxt is not None:
                            if h == 2:
                                turn_tokens(pe, g, ln, turned, s["xT_ps"], nxt)
                            if h == 3:
                                project(nxt)
                            if h == 7:
                                swap(nxt)
                    if nxt is not None:
                        pe.wait_ge(s["rot_ready"].sem, s["rot_ready"].at(nxt, 1))
                    pe.wait_ge(s["oT_ready"].sem, s["oT_ready"].at(t, 1))
                    for n in range(N):
                        pe.matmul(swap_b[:, n * P:(n + 1) * P], oT[:, n * P:(n + 1) * P], g["wout3"][:, :], start=True, stop=False)
                        last = add_bias(pe, g, swap_b[:, n * P:(n + 1) * P], B_O3, True)
                    last.then_inc(s["out_ps"].sem, 1)

                pe.wait_ge(s["cleared"].sem, 1)
                turn_tokens(pe, g, ln, turned, s["xT_ps"], 0)
                project(0)
                swap(0)
                each_turn(pe, NB, turn)


def att1(nc, g, NB, pre):
    N, B, H, D = 2, 4, 16, 64
    U, KEYS, BK = 8, 3 * WIN, 6 * WIN
    G = H // 2
    with ExitStack() as ctx:
        sb = lambda name, shape, dt=F32: ctx.enter_context(nc.sbuf_tensor(name, shape, dt))
        ln = norm_parts(nc, sb, pre, N)
        xT = sb(pre + "xT", [P, ROWS, WIN])
        q = sb(pre + "q", [P, G, B * U, 4, 8])
        k = sb(pre + "k", [P, G, ROWS * WIN])
        v = sb(pre + "v", [BK, 2, H * D])
        masked = sb(pre + "masked", [P, 2, U, KEYS])
        moved = sb(pre + "moved", [P, U, KEYS])
        ex = sb(pre + "ex", [P, U, KEYS])
        low = sb(pre + "low", [P, U])
        total = sb(pre + "total", [P, U])
        prob = sb(pre + "prob", [P, 4 * (2 * BK + WIN)])
        mixed = sb(pre + "mixed", [BK, H, U, 8])
        oT = sb(pre + "oT", [P, G, S + 4])
        s = {n: Signal(nc, pre + n) for n in ("xT_ps", "xT_ready", "first_ps", "first_ready", "out_ps", "cleared", "out_read")}
        q_ps, q_act, q_dve = (Signal(nc, pre + n, G // 2) for n in ("q_ps", "q_act", "q_dve"))
        k_ps, k_ready = Signal(nc, pre + "k_ps", G), Signal(nc, pre + "k_ready", G)
        v_ps, v_act, v_dve, score_ps, masked_ready, low_ready, moved_ready, exped, prob_ready, pv_ps, oT_ready = (
            Signal(nc, pre + n, B) for n in ("v_ps", "v_act", "v_dve", "score_ps", "masked_ready", "low_ready", "moved_ready",
                                             "exped", "prob_ready", "pv_ps", "oT_ready"))
        mix_ps, mixed_ready = Signal(nc, pre + "mix_ps", 2 * B), Signal(nc, pre + "mixed_ready", 2 * B)
        chain = Signal(nc, pre + "chain", 2 * B + 1)
        bank = g["bank"]
        turned, qk_b, v_b, score_b, mix_b = bank[0], bank[1:3], bank[3:5], bank[5], bank[6:8]
        out_ps = turned[:, S:2 * S]
        c = g["c"]
        window = c("window").rearrange("p (f u k) -> p f u k", f=2, u=U)

        def query_block(gp, half):
            rows = slice(D * half, D * half + D)
            src = qk_b[(gp // 2) % 2][rows, (gp % 2) * S:(gp % 2 + 1) * S].rearrange("p (u i) -> p u i", i=8)
            return q[rows, gp, :, 2 * (gp % 2) + half, :], src

        with nc.Block() as block:
            @block.vector
            def _(dve):
                dve.memset(q[:, :, :, :, :].rearrange("p a b c d -> p (a b c d)"), 0.0).then_inc(s["cleared"].sem, 1)
                dve.memset(prob[:, :], 0.0).then_inc(s["cleared"].sem, 1)
                dve.memset(xT[:, :, :], 0.0).then_inc(s["cleared"].sem, 1)
                dve.wait_ge(s["cleared"].sem, 3)

                with dve.Fori(0, NB) as t:
                    ch = Chain(dve, chain, t)
                    norm_vector(dve, g, ln, t)
                    for w in range(G // 2):
                        dve.wait_ge(q_ps.sem, q_ps.at(t, w + 1))
                        dve.wait_ge(q_act.sem, q_act.at(t, w + 1))
                        dve.tensor_copy(*query_block(2 * w + 1, 0))
                        dve.tensor_copy(*query_block(2 * w + 1, 1)).then_inc(q_dve.sem, 1)
                    for b in range(B):
                        dve.wait_ge(v_ps.sem, v_ps.at(t, b + 1))
                        if b >= 2:
                            dve.wait_ge(pv_ps.sem, pv_ps.at(t, b - 1))
                        dve.tensor_copy(v[:, b % 2, 0:512], v_b[0][0:BK, :]).then_inc(v_dve.sem, 1)
                        dve.wait_ge(score_ps.sem, score_ps.at(t, b + 1))
                        dve.tensor_tensor(masked[:, b % 2, :, :], score_b[:, 0:U * KEYS].rearrange("p (u k) -> p u k", k=KEYS),
                                          window[:, min(b, 1), :, :], ALU.add).then_inc(masked_ready.sem, 1)
                        dve.wait_ge(masked_ready.sem, masked_ready.at(t, b + 1))
                        dve.tensor_reduce(low[:, :], masked[:, b % 2, :, :], AX.X, ALU.max, negate=True).then_inc(low_ready.sem, 1)
                        dve.wait_ge(exped.sem, exped.at(t, b + 1))
                        ch.did(dve.tensor_reduce(total[:, :], ex[:, :, :], AX.X, ALU.add))
                        ch.settle()
                        ch.did(dve.reciprocal(total[:, :], total[:, :]))
                        ch.settle()
                        if b >= 1:
                            dve.wait_ge(mix_ps.sem, mix_ps.at(t, 2 * b))
                        place = prob[:, :].rearrange("p (r c) -> p r c", r=4)[:, :, 0:2 * BK].rearrange("p r (u k) -> p r u k", u=2)[:, :, :, 0:KEYS]
                        dve.tensor_tensor(place, ex[:, :, :].rearrange("p (r u) k -> p r u k", u=2),
                                          total[:, :].rearrange("p (r u) -> p r u", u=2).unsqueeze(3).broadcast_to([P, 4, 2, KEYS]),
                                          ALU.mult).then_inc(prob_ready.sem, 1)
                    dve.wait_ge(s["out_ps"].sem, s["out_ps"].at(t, 1))
                    x = x_tiles(g, t, N)
                    ch.did(dve.tensor_tensor(x, out_ps.rearrange("p (k d) -> p k d", d=P), x, ALU.add))
                    ch.settle()
                    ch.end()

            @block.gpsimd
            def _(pool):
                norm_pool_setup(pool, ln)
                with pool.Fori(0, NB) as t:
                    norm_pool(pool, ln, t)
                    for b in range(B):
                        pool.wait_ge(low_ready.sem, low_ready.at(t, b + 1))
                        if b >= 1:
                            pool.wait_ge(exped.sem, exped.at(t, b))
                        pool.tensor_tensor(moved[:, :, :], masked[:, b % 2, :, :], low[:, :].unsqueeze(2).broadcast_to([P, U, KEYS]),
                                           ALU.add).then_inc(moved_ready.sem, 1)

            @block.scalar
            def _(act):
                act.wait_ge(s["cleared"].sem, 3)
                with act.Fori(0, NB) as t:
                    act.wait_ge(s["xT_ps"].sem, s["xT_ps"].at(t, 1))
                    act.copy(xT[:, 2:ROWS - 1, 1:WIN], turned[:, 1:1 + 16 * 15].rearrange("p (r k) -> p r k", k=16))
                    act.copy(xT[:, ROWS - 1, 1:WIN - 1], turned[:, 241:S])
                    act.copy(xT[:, :, 0], turned[:, 0:1].broadcast_to([P, ROWS])).then_inc(s["xT_ready"].sem, 1)
                    for w in range(G // 2):
                        act.wait_ge(q_ps.sem, q_ps.at(t, w + 1))
                        act.copy(*query_block(2 * w, 0))
                        act.copy(*query_block(2 * w, 1)).then_inc(q_act.sem, 1)
                    for gp in range(G):
                        act.wait_ge(k_ps.sem, k_ps.at(t, gp + 1))
                        act.copy(k[:, gp, :], qk_b[gp % 2][:, 0:ROWS * WIN]).then_inc(k_ready.sem, 1)
                    act.wait_ge(s["first_ps"].sem, s["first_ps"].at(t, 1))
                    act.copy(oT[:, :, 0], turned[:, 0:G]).then_inc(s["first_ready"].sem, 1)

                    def values_in(b):
                        act.wait_ge(v_ps.sem, v_ps.at(t, b + 1))
                        if b >= 2:
                            act.wait_ge(pv_ps.sem, pv_ps.at(t, b - 1))
                        act.copy(v[:, b % 2, 512:1024], v_b[1][0:BK, :]).then_inc(v_act.sem, 1)

                    values_in(0)
                    for b in range(B):
                        act.wait_ge(moved_ready.sem, moved_ready.at(t, b + 1))
                        if b >= 1:
                            act.wait_ge(prob_ready.sem, prob_ready.at(t, b))
                        act.activation(ex[:, :, :], moved[:, :, :], ACT.Exp).then_inc(exped.sem, 1)
                        if b + 1 < B:
                            values_in(b + 1)
                        for half in range(2):
                            act.wait_ge(mix_ps.sem, mix_ps.at(t, 2 * b + half + 1))
                            if b >= 1 and half == 0:
                                act.wait_ge(pv_ps.sem, pv_ps.at(t, b))
                            act.copy(mixed[:, :, 4 * half:4 * half + 4, :].rearrange("p g u i -> p u g i"),
                                     mix_b[half][0:BK, :].rearrange("p (u g i) -> p u g i", u=4, i=8)).then_inc(mixed_ready.sem, 1)
                        act.wait_ge(pv_ps.sem, pv_ps.at(t, b + 1))
                        act.copy(oT[:, :, 1 + 64 * b:65 + 64 * b], qk_b[b % 2][:, :].rearrange("p (g i) -> p g i", g=G)).then_inc(oT_ready.sem, 1)

            @block.tensor
            def _(pe):
                wq, wk, wv = (g["wqkv1"][:, a * H * D:(a + 1) * H * D] for a in range(3))

                def values_and_scores(t, b):
                    if b >= 1:
                        pe.wait_ge(v_act.sem, v_act.at(t, b))
                        pe.wait_ge(v_dve.sem, v_dve.at(t, b))
                    for half in range(2):
                        last = pe.matmul(v_b[half][0:BK, :], xT[:, 4 * b:4 * b + 6, :].rearrange("p r k -> p (r k)"),
                                         wv[:, 512 * half:512 * half + 512], start=True, stop=True)
                    last.then_inc(v_ps.sem, 1)
                    if b >= 1:
                        pe.wait_ge(masked_ready.sem, masked_ready.at(t, b))
                    for u in range(U):
                        row = 4 * b + u // 2
                        for gp in range(G):
                            four = gp // 2
                            last = pe.matmul(score_b[32 * four:32 * four + 32, u * KEYS:(u + 1) * KEYS],
                                             q[:, gp, U * b + u, :, :].rearrange("p h i -> p (h i)"), k[:, gp, WIN * row:WIN * row + KEYS],
                                             start=(gp % 2 == 0), stop=(gp % 2 == 1))
                    last.then_inc(score_ps.sem, 1)

                pe.wait_ge(s["cleared"].sem, 3)
                with pe.Fori(0, NB) as t:
                    turn_tokens(pe, g, ln, turned, s["xT_ps"], t)
                    pe.wait_ge(s["xT_ready"].sem, s["xT_ready"].at(t, 1))
                    for w in range(G // 2):
                        if w >= 2:
                            pe.wait_ge(q_dve.sem, q_dve.at(t, w - 1))
                        for m in range(2):
                            gp = 2 * w + m
                            last = pe.matmul(qk_b[w % 2][:, m * S:(m + 1) * S], wq[:, gp * P:(gp + 1) * P], xT[:, 2:ROWS, 1:WIN], start=True, stop=True)
                        last.then_inc(q_ps.sem, 1)
                    for gp in range(G):
                        if gp < 2:
                            pe.wait_ge(q_dve.sem, q_dve.at(t, G // 2 - 1 + gp))
                        else:
                            pe.wait_ge(k_ready.sem, k_ready.at(t, gp - 1))
                        pe.matmul(qk_b[gp % 2][:, 0:ROWS * WIN], wk[:, gp * P:(gp + 1) * P], xT[:, :, :].rearrange("p r k -> p (r k)"),
                                  start=True, stop=True).then_inc(k_ps.sem, 1)
                    for gp in range(G):
                        last = pe.matmul(turned[:, gp:gp + 1], wv[:, gp * P:(gp + 1) * P], xT[:, 0, 0:1], start=True, stop=True)
                    last.then_inc(s["first_ps"].sem, 1)
                    pe.wait_ge(k_ready.sem, k_ready.at(t, G))
                    values_and_scores(t, 0)
                    for b in range(B):
                        if b + 1 < B:
                            values_and_scores(t, b + 1)
                        pe.wait_ge(prob_ready.sem, prob_ready.at(t, b + 1))
                        for half in range(2):
                            if b >= 1:
                                pe.wait_ge(mixed_ready.sem, mixed_ready.at(t, 2 * b - 1 + half))
                            for u in range(4 * half, 4 * half + 4):
                                last = pe.matmul(mix_b[half][0:BK, (u % 4) * P:(u % 4 + 1) * P], prob[:, u * BK:(u + 1) * BK],
                                                 g["mix"][:, :, :].rearrange("p g i -> p (g i)"), start=True, stop=True)
                            last.then_inc(mix_ps.sem, 1)
                        pe.wait_ge(mixed_ready.sem, mixed_ready.at(t, 2 * b + 2))
                        pe.wait_ge(v_act.sem, v_act.at(t, b + 1))
                        pe.wait_ge(v_dve.sem, v_dve.at(t, b + 1))
                        if b >= 2:
                            pe.wait_ge(oT_ready.sem, oT_ready.at(t, b - 1))
                        for h in range(H):
                            last = pe.matmul(qk_b[b % 2][D * (h % 2):D * (h % 2) + D, (h // 2) * 64:(h // 2) * 64 + 64], v[:, b % 2, h * D:(h + 1) * D],
                                             mixed[:, h, :, :].rearrange("p u i -> p (u i)"), start=True, stop=True)
                        last.then_inc(pv_ps.sem, 1)
                    pe.wait_ge(oT_ready.sem, oT_ready.at(t, B))
                    pe.wait_ge(s["first_ready"].sem, s["first_ready"].at(t, 1))
                    for n in range(N):
                        dst = out_ps[:, n * P:(n + 1) * P]
                        for gp in range(G):
                            pe.matmul(dst, oT[:, gp, n * P:(n + 1) * P], g["wout1"][:, gp, :], start=(gp == 0), stop=False)
                        last = add_bias(pe, g, dst, B_O1, True)
                    last.then_inc(s["out_ps"].sem, 1)


_INS = ['L0_attn_x', 'L0_attn_Wq', 'L0_attn_bq', 'L0_attn_Wk', 'L0_attn_bk', 'L0_attn_Wv', 'L0_attn_bv', 'L0_attn_Wo',
        'L0_attn_bo', 'L0_attn_Er', 'L0_ffn_weights', 'L0_ffn_scale', 'L0_ffn_bias', 'L1_attn_w_qkv', 'L1_attn_w_out',
        'L1_attn_b_out', 'L1_attn_w_th', 'L1_ffn_gate_w', 'L1_ffn_expert_w', 'L2_attn_W_qkv', 'L2_ffn_Wr', 'L2_ffn_Wg',
        'L2_ffn_Wu', 'L2_ffn_Wd', 'L2_ffn_Sg', 'L2_ffn_Su', 'L2_ffn_Sd', 'L3_attn_w_qkv', 'L3_attn_b_qkv',
        'L3_attn_w_out', 'L3_attn_b_out', 'L3_ffn_w_gate', 'L3_ffn_w_up', 'L3_ffn_w_down']


def kernel(**inputs):
    import numpy as _np
    import concourse.bacc as _bacc
    from concourse import mybir as _mybir
    from concourse.bass_utils import run_bass_kernel_spmd as _run

    nc = _bacc.Bacc("TRN2", target_bir_lowering=False, num_devices=1)
    arrays, aps = {}, {}
    for name in _INS + ["const"]:
        a = CONST if name == "const" else _np.ascontiguousarray(inputs[name])
        arrays[f"in_{name}_dram"] = a
        aps[name] = nc.dram_tensor(f"in_{name}_dram", a.shape, _mybir.dt.from_np(a.dtype), kind="ExternalInput").ap()
    shape = tuple(inputs["L0_attn_x"].shape)
    out = nc.dram_tensor("out_0_dram", shape, F32, kind="ExternalOutput").ap()
    network(nc, aps, out)
    r = _run(nc, [arrays], core_ids=[0])
    return r.results[0]["out_0_dram"]
```

```python
from contextlib import ExitStack

import numpy as np
import concourse.bass as bass
from concourse import mybir

F32 = mybir.dt.float32
BF16 = mybir.dt.bfloat16
I32 = mybir.dt.int32
ALU = mybir.AluOpType
ACT = mybir.ActivationFunctionType
AX = mybir.AxisListType

P = 128
S = 256
HEADS = 16
DK = P // HEADS
EPS = 1e-5
NEG = -1e30
WIN = 17
ROWS = S // 16 + 2
STAGES = list(range(12))

WQ0, WK0, WV0, WO0, WF0, WE1, WQ2, WK2, WV2, WG3, WU3, WD3, GW1, NWT = 0, 1, 2, 3, 4, 5, 13, 14, 15, 16, 19, 22, 25, 26
B_F0, B_V0, B_O0, B_O1, B_V3, B_O3, NBIAS = 0, 1, 2, 3, 4, 5, 6


def constants():
    part = np.arange(P)
    out = {}
    out["ident"] = np.eye(P)
    i = np.arange(S)
    out["head_of"] = (part[:, None] // DK == np.arange(HEADS)[None, :])
    out["step_of"] = (i[None, :] % 8 == (part[:, None] // DK) % 8)
    out["step8"] = (part[:, None] % 8 == np.arange(8)[None, :])
    out["spread_heads"] = (np.arange(HEADS)[:, None] == part[None, :] // 8)
    theta = 1.0 / 1250.0 ** ((part % DK) // 2 / (DK // 2))
    ang = (np.arange(S, dtype=np.float32)[None, :] * theta.astype(np.float32)[:, None]).astype(np.float32)
    out["cos"] = np.tile(np.cos(ang), (1, 2))
    out["sin"] = np.tile(np.sin(ang), (1, 2))
    swap = np.zeros((P, P))
    for m in range(P):
        swap[m + 1 if m % 2 == 0 else m - 1, m] = -1.0 if m % 2 == 0 else 1.0
    out["swap"] = swap
    out["rank8"] = np.tile(8.0 - np.arange(8), (P, 1))
    out["rank16"] = np.tile(16.0 - np.arange(16), (P, 1))
    sel = np.zeros((P, 8, P))
    for e in range(16):
        sel[e:48:16, e // 2, 64 * (e % 2):64 * (e % 2) + 64] = 1
    out["pick_expert"] = sel.reshape(P, -1)
    mask = np.zeros((P, 2, 8, 3, WIN))
    for first in range(2):
        for u in range(8):
            x = u // 2 if first == 0 else 4 + u // 2
            for p in range(P):
                n = 8 * (u % 2) + p % 8
                mask[p, first, u, :2, 0] = NEG
                for slot in range(3):
                    if x - 2 + slot < 0:
                        mask[p, first, u, slot, 1:] = NEG
                mask[p, first, u, 2, 2 + n:] = NEG
    out["window"] = mask.reshape(P, -1)
    back = np.zeros((2, P, 2 * S))
    for c in range(2 * S - 1):
        r = min(S - 1, 2 * S - 2 - c)
        back[r // P, r % P, c] = 1
    out["back0"], out["back1"] = back[0], back[1]
    at, cols, parts = {}, 0, []
    for name, a in out.items():
        a = np.asarray(a, np.float32)
        if a.shape[0] < P:
            a = np.concatenate([a, np.zeros((P - a.shape[0], a.shape[1]), np.float32)])
        at[name] = (cols, a.shape[1])
        cols += a.shape[1]
        parts.append(a)
    return np.ascontiguousarray(np.concatenate(parts, 1)), at


CONST, CONST_AT = constants()


class Signal:

    def __init__(self, nc, name, per=1):
        self.sem, self.per = nc.alloc_semaphore(name=name), per

    def at(self, t, k):
        return t * self.per + k


class Chain:

    def __init__(self, eng, steps, t):
        self.eng, self.steps, self.t, self.n = eng, steps, t, 0

    def did(self, ins):
        self.n += 1
        ins.then_inc(self.steps.sem, 1)

    def settle(self):
        self.eng.wait_ge(self.steps.sem, self.steps.at(self.t, self.n))

    def end(self):
        assert self.n == self.steps.per, (self.n, self.steps.per)


def network(nc, ins, out):
    NB = ins["L0_attn_x"].shape[0]
    x_dram = ins["L0_attn_x"].rearrange("b (h p) d -> p (b h) d", p=P)
    out_dram = out.rearrange("b (h p) d -> p (b h) d", p=P)
    ctx = ExitStack()
    with ctx:
        def sb(name, shape, dt=F32):
            return ctx.enter_context(nc.sbuf_tensor(name, shape, dt))

        bank = [ctx.enter_context(nc.psum_tensor(f"bank{i}", [P, 512], F32)) for i in range(8)]
        x_all = sb("x_all", [P, NB * 2 * P])
        wt = sb("wt", [P, NWT, P])
        small = {n: CONST_AT[n] for n in CONST_AT if n not in ("back0", "back1")}
        const_cols = CONST_AT["back0"][0]
        const = sb("const", [P, const_cols])
        bias_row = sb("bias_row", [1, NBIAS * P])
        ones_row = sb("ones_row", [1, P])
        col = sb("col", [P, 16])
        wqx = sb("wqx", [P, 8, P])
        er_win = sb("er_win", [P, 2 * S - 8])
        mix = sb("mix", [P, HEADS, 8])
        wqkv1 = sb("wqkv1", [P, 3 * 1024])
        wout1 = sb("wout1", [P, 8, P])
        wg2 = sb("wg2", [P, 16, 64])
        wu2 = sb("wu2", [P, 16, 64])
        wd2 = sb("wd2", [P, 9, P])
        sgu2 = sb("sgu2", [P, 2, P])
        wr2 = sb("wr2", [P, 16])
        wqkv3 = sb("wqkv3", [P, 3 * P])
        wout3 = sb("wout3", [P, P])
        g = dict(locals())

        def c(name):
            a, n = small[name]
            return const[:, a:a + n]

        g["c"] = c
        with nc.cleanup_on_exit():
            setup(nc, ins, g)
        stages = [("ffn0",), ("att0",), ("ffn0",), ("ffn1",), ("att1",), ("ffn1",),
                  ("ffn2",), ("att2",), ("ffn2",), ("ffn3",), ("att3",), ("ffn3",)]
        build = {"ffn0": ffn0, "att0": att0, "ffn1": ffn1, "att1": att1, "ffn2": ffn2, "att2": att2,
                 "ffn3": ffn3, "att3": att3}
        for n in STAGES:
            with nc.cleanup_on_exit():
                build[stages[n][0]](nc, g, NB, f"{stages[n][0]}_{n}_")
        with nc.cleanup_on_exit():
            stored = Signal(nc, "stored")
            with nc.Block() as block:
                @block.sync
                def _(sp):
                    xv = x_all[:, :].rearrange("p (t d) -> p t d", d=P)
                    half = NB
                    sp.dma_start(out_dram[:, 0:half, :], xv[:, 0:half, :]).then_inc(stored.sem, 16)
                    sp.dma_start(out_dram[:, half:, :], xv[:, half:, :]).then_inc(stored.sem, 16)
                    sp.wait_ge(stored.sem, 32)


def setup(nc, ins, g):
    wt, const, bias_row, ones_row, col, c = (g[k] for k in ("wt", "const", "bias_row", "ones_row", "col", "c"))
    bank, wqx, er_win, mix, wd2, x_all = (g[k] for k in ("bank", "wqx", "er_win", "mix", "wd2", "x_all"))
    with ExitStack() as ctx:
        def sb(name, shape, dt=F32):
            return ctx.enter_context(nc.sbuf_tensor(name, shape, dt))

        raw = sb("raw", [P, NWT, P])
        raw_int = sb("raw_int", [P, 9, P], I32)
        scale0 = sb("scale0", [P, 1])
        er = sb("er", [P, 2, DK])
        er_rep = sb("er_rep", [P, 2, HEADS, DK])
        back = sb("back", [P, 2, 2 * S])
        er_rev = sb("er_rev", [P, 2 * S])
        thT = sb("thT", [HEADS, HEADS])
        th_rep = sb("th_rep", [P, HEADS])
        half_ident = sb("half_ident", [P, P])
        loaded, x_in, prepared, turned, moved, chain = (Signal(nc, n) for n in (
            "loaded", "x_in", "prepared", "turned", "moved", "chain"))
        tiny_loaded = Signal(nc, "tiny_loaded")
        small_ps, er_ready, shifted = (Signal(nc, n) for n in ("small_ps", "er_ready", "shifted"))
        loads, tiny_loads = [], []

        def blocks(name):
            return ins[name].rearrange("(t p) d -> p t d", p=P)

        loads.append((const[:, :], ins["const"][:, 0:g["const_cols"]]))
        loads.append((back[:, :, :], ins["const"][:, g["const_cols"]:].rearrange("p (t c) -> p t c", t=2)))
        for n, name in ((WQ0, "L0_attn_Wq"), (WK0, "L0_attn_Wk"), (WV0, "L0_attn_Wv"), (WO0, "L0_attn_Wo"), (WF0, "L0_ffn_weights")):
            loads.append((raw[:, n, :], ins[name]))
        loads.append((raw[:, WE1:WE1 + 8, :], ins["L1_ffn_expert_w"].rearrange("e f h -> f e h")))
        loads.append((raw[:, WQ2:WQ2 + 3, :], blocks("L2_attn_W_qkv")))
        loads.append((raw[0:8, GW1, :], ins["L1_ffn_gate_w"]))
        loads.append((raw_int[:, 0:3, :], blocks("L3_ffn_w_gate")))
        loads.append((raw_int[:, 3:6, :], blocks("L3_ffn_w_up")))
        loads.append((raw_int[:, 6:9, :], ins["L3_ffn_w_down"].rearrange("d (t h) -> d t h", t=3)))
        for n, name in ((B_F0, "L0_ffn_bias"), (B_V0, "L0_attn_bv"), (B_O0, "L0_attn_bo"), (B_O1, "L1_attn_b_out"), (B_O3, "L3_attn_b_out")):
            loads.append((bias_row[:, n * P:(n + 1) * P], ins[name].rearrange("(a d) -> a d", a=1)))
        loads.append((bias_row[:, B_V3 * P:(B_V3 + 1) * P], ins["L3_attn_b_qkv"][2 * P:3 * P].rearrange("(a d) -> a d", a=1)))
        loads.append((scale0[:, :], ins["L0_ffn_scale"].rearrange("(d a) -> d a", a=1)))
        loads.append((col[:, 8:9], ins["L0_attn_bq"].rearrange("(d a) -> d a", a=1)))
        loads.append((col[:, 9:10], ins["L0_attn_bk"].rearrange("(d a) -> d a", a=1)))
        loads.append((col[:, 10:12], ins["L3_attn_b_qkv"][0:2 * P].rearrange("(a d) -> d a", a=2)))
        for par in range(2):
            for i in range(8):
                tiny_loads.append((col[64 * par + 8 * i:64 * par + 8 * i + 8, 0:8],
                                   ins["L0_attn_bq"][64 * par:64 * par + 64].rearrange("(h d) -> d h", d=DK)))
        loads.append((er[:, :, :], ins["L0_attn_Er"].rearrange("(t p) d -> p t d", p=P)))
        loads.append((thT[:, :], ins["L1_attn_w_th"].rearrange("g h -> h g")))
        loads.append((g["wqkv1"][:, :], ins["L1_attn_w_qkv"]))
        loads.append((g["wout1"][:, :, :], ins["L1_attn_w_out"].rearrange("(t p) d -> p t d", p=P)))
        loads.append((g["wg2"][:, :, :], ins["L2_ffn_Wg"].rearrange("e d f -> d e f")))
        loads.append((g["wu2"][:, :, :], ins["L2_ffn_Wu"].rearrange("e d f -> d e f")))
        loads.append((wd2[:, 0:8, :], ins["L2_ffn_Wd"].rearrange("(t e) f d -> (e f) t d", e=2)))
        loads.append((wd2[:, 8, :], ins["L2_ffn_Sd"]))
        loads.append((g["sgu2"][:, 0, :], ins["L2_ffn_Sg"]))
        loads.append((g["sgu2"][:, 1, :], ins["L2_ffn_Su"]))
        loads.append((g["wr2"][:, :], ins["L2_ffn_Wr"]))
        loads.append((g["wqkv3"][:, :], ins["L3_attn_w_qkv"]))
        loads.append((g["wout3"][:, :], ins["L3_attn_w_out"]))
        NL, NT = len(loads), len(tiny_loads)

        with nc.Block() as block:
            @block.sync
            def _(sp):
                for n, (dst, src) in enumerate(loads):
                    sp.dma_start(dst, src, allow_slow_non_contiguous=True).then_inc(loaded.sem, 16)
                sp.wait_ge(er_ready.sem, 1)
                for par in range(2):
                    for i in range(8):
                        rows = slice(64 * par + 8 * i, 64 * par + 8 * i + 8)
                        sp.dma_start(er_win[rows, :], er_rev[rows, 7 - i:7 - i + 2 * S - 8]).then_inc(shifted.sem, 16)
                sp.wait_ge(shifted.sem, 16 * 16)

            @block.gpsimd
            def _(pool):
                for dst, src in tiny_loads:
                    pool.dma_start(dst, src, allow_slow_non_contiguous=True).then_inc(tiny_loaded.sem, 16)

            @block.scalar
            def _(act):
                act.dma_start(x_all[:, :].rearrange("p (t d) -> p t d", d=P), g["x_dram"]).then_inc(x_in.sem, 16)
                act.wait_ge(x_in.sem, 16)

            @block.vector
            def _(dve):
                n = [0]

                def did(ins_):
                    n[0] += 1
                    ins_.then_inc(chain.sem, 1)

                def settle():
                    dve.wait_ge(chain.sem, n[0])

                did(dve.memset(ones_row[:, :], 1.0))
                dve.wait_ge(loaded.sem, 16 * NL)
                dve.wait_ge(tiny_loaded.sem, 16 * NT)
                did(dve.tensor_copy(raw[:, WG3:WG3 + 9, :], raw_int[:, :, :]))
                did(dve.tensor_scalar(raw[:, WF0, :], raw[:, WF0, :], 0.0, 2.0, ALU.is_ge, ALU.mult))
                did(dve.tensor_scalar(half_ident[:, :], c("ident"), 0.5, None, ALU.mult))
                did(dve.tensor_scalar(raw[:, WQ0, :], raw[:, WQ0, :], DK ** -0.5, None, ALU.mult))
                did(dve.tensor_scalar(col[:, 0:9], col[:, 0:9], DK ** -0.5, None, ALU.mult))
                did(dve.tensor_scalar(col[:, 12:14], col[:, 10:12], -1.0, None, ALU.mult))
                did(dve.tensor_scalar(raw[:, WQ2, :], raw[:, WQ2, :], P ** -0.5, None, ALU.mult))
                did(dve.tensor_scalar(g["wqkv1"][:, 0:1024], g["wqkv1"][:, 0:1024], 64 ** -0.5, None, ALU.mult))
                did(dve.tensor_scalar(wd2[:, :, :], wd2[:, :, :], 0.25, None, ALU.mult))
                for t in range(2):
                    did(dve.tensor_copy(er_rep[:, t, :, :], er[:, t:t + 1, :].broadcast_to([P, HEADS, DK])))
                settle()
                did(dve.tensor_scalar(raw[:, WG3:WG3 + 9, :], raw[:, WG3:WG3 + 9, :], float(np.float32(1.0 / 127.0)), None, ALU.mult))
                did(dve.tensor_scalar(raw[:, WF0, :], raw[:, WF0, :], 1.0, scale0[:, 0:1], ALU.subtract, ALU.mult))
                for e in range(8):
                    did(dve.scalar_tensor_tensor(out=raw[:, WE1 + e, :], in0=raw[:, WE1 + e, :], scalar=0.5,
                                                 in1=half_ident[:, :], op0=ALU.mult, op1=ALU.add))
                settle()
                did(dve.tensor_scalar(raw[:, WD3:WD3 + 3, :], raw[:, WD3:WD3 + 3, :], 0.25, None, ALU.mult))
                settle()
                dve.memset(half_ident[0:1, 0:1], 0.5).then_inc(prepared.sem, 1)
                for b in range(7):
                    lo, hi = 4 * b, min(4 * b + 4, NWT)
                    dve.wait_ge(turned.sem, b + 1)
                    if hi == NWT:
                        did(dve.tensor_copy(wt[:, lo:lo + 1, :], bank[b][:, 0:P].rearrange("p (t d) -> p t d", d=P)))
                        did(dve.tensor_copy(wt[:, GW1, 0:8], bank[b][:, P:P + 8]))
                    else:
                        did(dve.tensor_copy(wt[:, lo:hi, :], bank[b][:, :].rearrange("p (t d) -> p t d", d=P)))
                dve.wait_ge(small_ps.sem, 1)
                did(dve.tensor_copy(th_rep[:, :], bank[7][:, 0:HEADS]))
                settle()
                did(dve.tensor_tensor(mix[:, :, :], th_rep[:, :].unsqueeze(2).broadcast_to([P, HEADS, 8]),
                                      c("step8").unsqueeze(1).broadcast_to([P, HEADS, 8]), ALU.mult))
                for hp in range(8):
                    for par in range(2):
                        h = par * 8 + hp
                        did(dve.tensor_copy(wqx[:, hp, 64 * par:64 * par + 64].rearrange("p (i d) -> p i d", d=DK),
                                            wt[:, WQ0:WQ0 + 1, DK * h:DK * h + DK].broadcast_to([P, 8, DK])))
                settle()
                dve.memset(half_ident[0:1, 0:1], 0.5).then_inc(moved.sem, 1)
                dve.wait_ge(small_ps.sem, 2)
                dve.tensor_copy(er_rev[:, :], bank[6][:, :]).then_inc(er_ready.sem, 1)

            @block.tensor
            def _(pe):
                pe.wait_ge(prepared.sem, 1)
                for b in range(7):
                    lo, hi = 4 * b, min(4 * b + 4, NWT)
                    for k in range(lo, hi):
                        rows = 8 if k == GW1 else P
                        last = pe.transpose(bank[b][:, (k - lo) * P:(k - lo) * P + rows], raw[0:rows, k, :],
                                            c("ident")[0:rows, 0:rows])
                    last.then_inc(turned.sem, 1)
                pe.matmul(bank[7][:, 0:HEADS], c("spread_heads")[0:HEADS, :], thT[:, :], start=True, stop=True).then_inc(small_ps.sem, 1)
                pe.wait_ge(moved.sem, 1)
                for t in range(2):
                    last = pe.matmul(bank[6][:, :], er_rep[:, t, :, :].rearrange("p h d -> p (h d)"), back[:, t, :],
                                     start=(t == 0), stop=(t == 1))
                last.then_inc(small_ps.sem, 1)


def x_tiles(g, t, n):
    return g["x_all"][:, bass.ds(t * (n * P), n * P)].rearrange("p (k d) -> p k d", d=P)


def norm_parts(nc, sb, pre, n):
    return {
        "n": n, "stats": sb(pre + "stats", [P, n, 6]), "mv": sb(pre + "mv", [P, n, 2]), "apart": sb(pre + "apart", [P, n]), "mean": sb(pre + "mean", [P, n]), "var": sb(pre + "var", [P, n]),
        "power": sb(pre + "power", [P, n]), "rstd": sb(pre + "rstd", [P, n]), "xn": sb(pre + "xn", [P, n, P]),
        "var_ready": Signal(nc, pre + "var_ready"), "rstd_ready": Signal(nc, pre + "rstd_ready"),
        "xn_ready": Signal(nc, pre + "xn_ready", n), "steps": Signal(nc, pre + "norm_steps", n + 5), "power_set": Signal(nc, pre + "power_set"),
    }


def norm_stats(dve, g, ln, t):
    n, x = ln["n"], x_tiles(g, t, ln["n"])
    ch = Chain(dve, ln["steps"], t)
    for k in range(n):
        ch.did(dve.bn_stats(ln["stats"][:, k, :], x[:, k, :]))
    ch.settle()
    ch.did(dve.tensor_tensor(ln["mv"][:, :, 0:2], ln["stats"][:, :, 1:3], ln["stats"][:, :, 4:6], ALU.add))
    ch.did(dve.tensor_tensor(ln["apart"][:, :], ln["stats"][:, :, 1], ln["stats"][:, :, 4], ALU.subtract))
    ch.settle()
    ch.did(dve.tensor_scalar(ln["mean"][:, :], ln["mv"][:, :, 0], 0.5, None, ALU.mult))
    ch.did(dve.tensor_tensor(ln["apart"][:, :], ln["apart"][:, :], ln["apart"][:, :], ALU.mult))
    ch.settle()
    ch.did(dve.scalar_tensor_tensor(out=ln["var"][:, :], in0=ln["apart"][:, :], scalar=P / 4, in1=ln["mv"][:, :, 1], op0=ALU.mult, op1=ALU.add))
    ch.settle()
    ch.end()
    dve.tensor_scalar(ln["var"][:, :], ln["var"][:, :], 1.0 / P, EPS, ALU.mult, ALU.add).then_inc(ln["var_ready"].sem, 1)


def norm_apply(dve, g, ln, t):
    n, x = ln["n"], x_tiles(g, t, ln["n"])
    dve.wait_ge(ln["rstd_ready"].sem, ln["rstd_ready"].at(t, 1))
    for k in range(n):
        dve.tensor_scalar(ln["xn"][:, k, :], x[:, k, :], ln["mean"][:, k:k + 1], ln["rstd"][:, k:k + 1],
                          ALU.subtract, ALU.mult).then_inc(ln["xn_ready"].sem, 1)


def norm_vector(dve, g, ln, t):
    norm_stats(dve, g, ln, t)
    norm_apply(dve, g, ln, t)


def norm_pool(pool, ln, t):
    pool.wait_ge(ln["var_ready"].sem, ln["var_ready"].at(t, 1))
    pool.tensor_tensor(ln["rstd"][:, :], ln["var"][:, :], ln["power"][:, :], ALU.pow).then_inc(ln["rstd_ready"].sem, 1)


def norm_pool_setup(pool, ln):
    pool.memset(ln["power"][:, :], -0.5).then_inc(ln["power_set"].sem, 1)
    pool.wait_ge(ln["power_set"].sem, 1)


def turn_tokens(pe, g, ln, ps, signal, t):
    for k in range(ln["n"]):
        pe.wait_ge(ln["xn_ready"].sem, ln["xn_ready"].at(t, k + 1))
        last = pe.transpose(ps[:, k * P:(k + 1) * P], ln["xn"][:, k, :], g["c"]("ident"))
    last.then_inc(signal.sem, 1)


def add_bias(pe, g, out, row, stop):
    return pe.matmul(out, g["ones_row"][:, :], g["bias_row"][:, row * P:(row + 1) * P], start=False, stop=stop)


def each_turn(eng, n, turn):
    if n > 1:
        with eng.Fori(0, n - 1) as t:
            turn(t, t + 1)
    turn(n - 1, None)


def ffn0(nc, g, NB, pre):
    N = 4
    with ExitStack() as ctx:
        sb = lambda name, shape, dt=F32: ctx.enter_context(nc.sbuf_tensor(name, shape, dt))
        ln = norm_parts(nc, sb, pre, N)
        xT = sb(pre + "xT", [P, N * P])
        y = sb(pre + "y", [P, N, P])
        xT_ps, xT_ready, y_ps, chain = Signal(nc, pre + "xT_ps"), Signal(nc, pre + "xT_ready"), Signal(nc, pre + "y_ps"), Signal(nc, pre + "chain", 2)
        bank_free = Signal(nc, pre + "bank_free")
        turned, prod = g["bank"][0], g["bank"][1]
        turns = NB * 2 // N
        with nc.Block() as block:
            @block.vector
            def _(dve):
                def turn(t, nxt):
                    ch = Chain(dve, chain, t)
                    if nxt is not None:
                        norm_stats(dve, g, ln, nxt)
                        dve.wait_ge(xT_ps.sem, xT_ps.at(t, 1))
                        norm_apply(dve, g, ln, nxt)
                    dve.wait_ge(y_ps.sem, y_ps.at(t, 1))
                    ch.did(dve.tensor_scalar(y[:, :, :], prod[:, :].rearrange("p (k d) -> p k d", d=P), 100.0, -100.0, ALU.min, ALU.max))
                    ch.settle()
                    dve.nop().then_inc(bank_free.sem, 1)
                    x = x_tiles(g, t, N)
                    ch.did(dve.scalar_tensor_tensor(out=x, in0=y[:, :, :], scalar=0.5, in1=x, op0=ALU.mult, op1=ALU.add))
                    ch.settle()
                    ch.end()

                dve.nop().then_inc(bank_free.sem, 1)
                norm_vector(dve, g, ln, 0)
                each_turn(dve, turns, turn)

            @block.gpsimd
            def _(pool):
                norm_pool_setup(pool, ln)
                with pool.Fori(0, turns) as t:
                    norm_pool(pool, ln, t)

            @block.scalar
            def _(act):
                with act.Fori(0, turns) as t:
                    act.wait_ge(xT_ps.sem, xT_ps.at(t, 1))
                    act.copy(xT[:, :], turned[:, :]).then_inc(xT_ready.sem, 1)

            @block.tensor
            def _(pe):
                def turn(t, nxt):
                    pe.wait_ge(xT_ready.sem, xT_ready.at(t, 1))
                    pe.wait_ge(bank_free.sem, bank_free.at(t, 1))
                    for k in range(N):
                        pe.matmul(prod[:, k * P:(k + 1) * P], xT[:, k * P:(k + 1) * P], g["wt"][:, WF0, :], start=True, stop=False)
                        last = add_bias(pe, g, prod[:, k * P:(k + 1) * P], B_F0, True)
                    last.then_inc(y_ps.sem, 1)
                    if nxt is not None:
                        turn_tokens(pe, g, ln, turned, xT_ps, nxt)

                turn_tokens(pe, g, ln, turned, xT_ps, 0)
                each_turn(pe, turns, turn)


def ffn1(nc, g, NB, pre):
    N, E = 4, 8
    SPREAD, OWN = 6, 4
    with ExitStack() as ctx:
        sb = lambda name, shape, dt=F32: ctx.enter_context(nc.sbuf_tensor(name, shape, dt))
        ln = norm_parts(nc, sb, pre, N)
        xT_new = sb(pre + "xT_new", [P, N * P])
        xT = sb(pre + "xT", [P, N * P])
        score = sb(pre + "score", [P, N, E])
        key = sb(pre + "key", [P, N, E])
        chosen = sb(pre + "chosen", [P, N, 2 * E])
        best = sb(pre + "best", [P, N])
        choice = sb(pre + "choice", [2 * E, N * P], BF16)
        rows = sb(pre + "rows", [2 * E, E * P], BF16)
        own = sb(pre + "own", [P, OWN, N * P])
        names = ("xT_ps", "xT_ready", "adopted", "gate_ps", "routed", "choice_ps", "choice_ready", "rows_ready", "cleared", "added")
        s = {n: Signal(nc, pre + n) for n in names}
        spread_ps, own_ready, own_used = (Signal(nc, pre + n, E) for n in ("spread_ps", "own_ready", "own_used"))
        routing = Signal(nc, pre + "routing", 6)
        misc, acc, spread_b = g["bank"][0], g["bank"][1], g["bank"][2:2 + SPREAD]
        turns = NB * 2 // N
        c = g["c"]
        with nc.Block() as block:
            @block.vector
            def _(dve):
                def route(t):
                    ch = Chain(dve, routing, t)
                    dve.wait_ge(s["gate_ps"].sem, s["gate_ps"].at(t, 1))
                    ch.did(dve.tensor_copy(score[:, :, :], misc[:, 0:N * E].rearrange("p (k e) -> p k e", e=E)))
                    ch.settle()
                    first_largest(dve, ch, score, best, key, chosen[:, :, 0:E], c("rank8"), N, E)
                    ch.end()
                    dve.nop().then_inc(s["routed"].sem, 1)

                def choice_in(t):
                    dve.wait_ge(s["choice_ps"].sem, s["choice_ps"].at(t, 1))
                    dve.tensor_copy(choice[:, :], misc[0:2 * E, :]).then_inc(s["choice_ready"].sem, 1)

                def turn(t, nxt):
                    dve.wait_ge(s["adopted"].sem, s["adopted"].at(t, 1))
                    for e in range(E):
                        dve.wait_ge(spread_ps.sem, spread_ps.at(t, e + 1))
                        if e >= OWN:
                            dve.wait_ge(own_used.sem, own_used.at(t, e - OWN + 1))
                        dve.tensor_tensor(own[:, e % OWN, :], spread_b[e % SPREAD][:, :], xT[:, :], ALU.mult).then_inc(own_ready.sem, 1)
                        if nxt is not None:
                            if e == 0:
                                norm_stats(dve, g, ln, nxt)
                            if e == 1:
                                norm_apply(dve, g, ln, nxt)
                            if e == 5:
                                route(nxt)
                    if nxt is not None:
                        choice_in(nxt)
                    dve.wait_ge(own_used.sem, own_used.at(t, E))
                    x = x_tiles(g, t, N)
                    dve.tensor_tensor(x, acc[:, :].rearrange("p (k d) -> p k d", d=P), x, ALU.add).then_inc(s["added"].sem, 1)

                dve.nop().then_inc(s["added"].sem, 1)
                dve.memset(chosen[:, :, :], 0.0).then_inc(s["cleared"].sem, 1)
                dve.tensor_copy(rows[:, :].rearrange("p (e d) -> p e d", d=P),
                                c("ident")[0:2 * E, 0:E].unsqueeze(2).broadcast_to([2 * E, E, P])).then_inc(s["rows_ready"].sem, 1)
                norm_vector(dve, g, ln, 0)
                dve.wait_ge(s["cleared"].sem, 1)
                route(0)
                choice_in(0)
                each_turn(dve, turns, turn)

            @block.gpsimd
            def _(pool):
                norm_pool_setup(pool, ln)
                with pool.Fori(0, turns) as t:
                    norm_pool(pool, ln, t)

            @block.scalar
            def _(act):
                def x_in(t):
                    act.wait_ge(s["xT_ps"].sem, s["xT_ps"].at(t, 1))
                    act.copy(xT_new[:, :], misc[:, :]).then_inc(s["xT_ready"].sem, 1)

                def adopt(t):
                    act.wait_ge(s["xT_ready"].sem, s["xT_ready"].at(t, 1))
                    act.copy(xT[:, :], xT_new[:, :]).then_inc(s["adopted"].sem, 1)

                def turn(t, nxt):
                    if nxt is not None:
                        x_in(nxt)
                        act.wait_ge(own_ready.sem, own_ready.at(t, E))
                        adopt(nxt)

                x_in(0)
                adopt(0)
                each_turn(act, turns, turn)

            @block.tensor
            def _(pe):
                def gates(t):
                    pe.wait_ge(s["xT_ready"].sem, s["xT_ready"].at(t, 1))
                    for k in range(N):
                        last = pe.matmul(misc[:, k * E:(k + 1) * E], xT_new[:, k * P:(k + 1) * P], g["wt"][:, GW1, 0:E], start=True, stop=True)
                    last.then_inc(s["gate_ps"].sem, 1)

                def turn_choice(t):
                    pe.wait_ge(s["routed"].sem, s["routed"].at(t, 1))
                    for k in range(N):
                        last = pe.transpose(misc[0:2 * E, k * P:(k + 1) * P], chosen[:, k, :], c("ident"))
                    last.then_inc(s["choice_ps"].sem, 1)

                def spread(t, e):
                    if e >= SPREAD:
                        pe.wait_ge(own_ready.sem, own_ready.at(t, e - SPREAD + 1))
                    pe.matmul(spread_b[e % SPREAD][:, :], rows[:, e * P:(e + 1) * P], choice[:, :], start=True, stop=True).then_inc(spread_ps.sem, 1)

                def turn(t, nxt):
                    pe.wait_ge(s["choice_ready"].sem, s["choice_ready"].at(t, 1))
                    for e in range(SPREAD):
                        spread(t, e)
                    for e in range(E):
                        pe.wait_ge(own_ready.sem, own_ready.at(t, e + 1))
                        if e == 0:
                            pe.wait_ge(s["added"].sem, s["added"].at(t, 1))
                        for k in range(N):
                            last = pe.matmul(acc[:, k * P:(k + 1) * P], own[:, e % OWN, k * P:(k + 1) * P], g["wt"][:, WE1 + e, :],
                                             start=(e == 0 and k == 0), stop=(e == E - 1), skip_group_check=True)
                        last.then_inc(own_used.sem, 1)
                        if e + SPREAD < E:
                            spread(t, e + SPREAD)
                        if nxt is not None:
                            if e == 2:
                                turn_tokens(pe, g, ln, misc, s["xT_ps"], nxt)
                            if e == 3:
                                gates(nxt)
                            if e == 6:
                                turn_choice(nxt)

                pe.wait_ge(s["rows_ready"].sem, 1)
                turn_tokens(pe, g, ln, misc, s["xT_ps"], 0)
                gates(0)
                turn_choice(0)
                each_turn(pe, turns, turn)


def first_largest(dve, ch, value, best, key, chosen, rank, n, m):
    def over(v):
        return v[:, :].unsqueeze(2).broadcast_to([P, n, m])

    ch.did(dve.tensor_reduce(best[:, :], value[:, :, :], AX.X, ALU.max))
    ch.settle()
    ch.did(dve.tensor_tensor(key[:, :, :], value[:, :, :], over(best), ALU.is_equal))
    ch.settle()
    ch.did(dve.tensor_tensor(key[:, :, :], key[:, :, :], rank.unsqueeze(1).broadcast_to([P, n, m]), ALU.mult))
    ch.settle()
    ch.did(dve.tensor_reduce(best[:, :], key[:, :, :], AX.X, ALU.max))
    ch.settle()
    ch.did(dve.tensor_tensor(chosen[:, :, :], key[:, :, :], over(best), ALU.is_equal))
    ch.settle()


def ffn2(nc, g, NB, pre):
    N, E = 4, 16
    NP = E // 2 + 1
    HID = 3
    with ExitStack() as ctx:
        sb = lambda name, shape, dt=F32: ctx.enter_context(nc.sbuf_tensor(name, shape, dt))
        ln = norm_parts(nc, sb, pre, N)
        xT_new = sb(pre + "xT_new", [P, N * P])
        xT = sb(pre + "xT", [P, N * P])
        prob = sb(pre + "prob", [P, N, E])
        rest = sb(pre + "rest", [P, N, E])
        key = sb(pre + "key", [P, N, E])
        one1 = sb(pre + "one1", [P, N, E])
        one2 = sb(pre + "one2", [P, N, E])
        weight = sb(pre + "weight", [P, N, E])
        top = sb(pre + "top", [P, N])
        best = sb(pre + "best", [P, N])
        total = sb(pre + "total", [P, N])
        rounded = sb(pre + "rounded", [P, 2, N, E], BF16)
        left = sb(pre + "left", [P, N, E])
        parts = sb(pre + "parts", [P, N, P // E, E])
        wT = sb(pre + "wT", [3 * E, N * P], BF16)
        pick = sb(pre + "pick", [3 * E, E // 2 * P], BF16)
        th = sb(pre + "th", [P, 2, N * P])
        share = sb(pre + "share", [P, 2, N * P])
        hid = sb(pre + "hid", [P, HID, N * P])
        names = ("xT_ps", "xT_ready", "adopted", "logit_ps", "shifted", "exped", "weight_ready", "split", "wT_ps", "wT_ready", "pick_ready", "cleared")
        s = {n: Signal(nc, pre + n) for n in names}
        pair_ps, tanhed, gated, hid_used = (Signal(nc, pre + n, NP) for n in ("pair_ps", "tanhed", "gated", "hid_used"))
        share_ready, hid_ready = Signal(nc, pre + "share_ready", NP - 1), Signal(nc, pre + "hid_ready", NP - 1)
        chain = Signal(nc, pre + "chain", NP)
        routing = Signal(nc, pre + "routing", 1 + 3 + 5 + 1 + 5 + 1)
        splitting = Signal(nc, pre + "splitting", 5)
        added = Signal(nc, pre + "added")
        misc, acc = g["bank"][0], g["bank"][1]
        gb, ub, cb = g["bank"][2:4], g["bank"][4:6], g["bank"][6:8]
        turns = NB * 2 // N
        c = g["c"]
        over = lambda v: v[:, :].unsqueeze(2).broadcast_to([P, N, E])
        with nc.Block() as block:
            @block.vector
            def _(dve):
                def shift(t, ch):
                    dve.wait_ge(s["logit_ps"].sem, s["logit_ps"].at(t, 1))
                    logit = misc[:, 0:N * E].rearrange("p (k e) -> p k e", e=E)
                    ch.did(dve.tensor_reduce(top[:, :], logit, AX.X, ALU.max))
                    ch.settle()
                    dve.tensor_tensor(rest[:, :, :], logit, over(top), ALU.subtract).then_inc(s["shifted"].sem, 1)

                def probabilities(t, ch):
                    dve.wait_ge(s["exped"].sem, s["exped"].at(t, 1))
                    ch.did(dve.tensor_reduce(total[:, :], key[:, :, :], AX.X, ALU.add))
                    ch.settle()
                    ch.did(dve.reciprocal(total[:, :], total[:, :]))
                    ch.settle()
                    ch.did(dve.tensor_tensor(prob[:, :, :], key[:, :, :], over(total), ALU.mult))
                    ch.settle()

                def first(ch):
                    first_largest(dve, ch, prob, best, key, one1, c("rank16"), N, E)

                def second(ch):
                    ch.did(dve.scalar_tensor_tensor(out=rest[:, :, :], in0=one1[:, :, :], scalar=-2.0, in1=prob[:, :, :], op0=ALU.mult, op1=ALU.add))
                    ch.settle()
                    first_largest(dve, ch, rest, best, key, one2, c("rank16"), N, E)
                    ch.did(dve.tensor_tensor(one2[:, :, :], one2[:, :, :], one1[:, :, :], ALU.add))
                    ch.settle()
                    ch.end()
                    dve.tensor_tensor(weight[:, :, :], prob[:, :, :], one2[:, :, :], ALU.mult).then_inc(s["weight_ready"].sem, 1)

                def split(t):
                    ch = Chain(dve, splitting, t)
                    dve.wait_ge(s["weight_ready"].sem, s["weight_ready"].at(t, 1))
                    ch.did(dve.tensor_copy(rounded[:, 0, :, :], weight[:, :, :]))
                    ch.settle()
                    ch.did(dve.tensor_copy(parts[:, :, 0, :], rounded[:, 0, :, :]))
                    ch.did(dve.tensor_tensor(left[:, :, :], weight[:, :, :], rounded[:, 0, :, :], ALU.subtract))
                    ch.settle()
                    ch.did(dve.tensor_copy(rounded[:, 1, :, :], left[:, :, :]))
                    ch.settle()
                    ch.did(dve.tensor_copy(parts[:, :, 1, :], rounded[:, 1, :, :]))
                    ch.settle()
                    ch.end()
                    dve.tensor_tensor(parts[:, :, 2, :], left[:, :, :], rounded[:, 1, :, :], ALU.subtract).then_inc(s["split"].sem, 1)

                def weights_in(t):
                    dve.wait_ge(s["wT_ps"].sem, s["wT_ps"].at(t, 1))
                    dve.tensor_copy(wT[:, :], misc[0:3 * E, :]).then_inc(s["wT_ready"].sem, 1)

                def turn(t, nxt):
                    ch = Chain(dve, chain, t)
                    if nxt is not None:
                        route = Chain(dve, routing, nxt)
                    for j in range(NP):
                        dve.wait_ge(tanhed.sem, tanhed.at(t, j + 1))
                        if j >= HID:
                            dve.wait_ge(hid_used.sem, hid_used.at(t, j - HID + 1))
                        h = hid[:, j % HID, :]
                        ch.did(dve.scalar_tensor_tensor(out=h, in0=th[:, j % 2, :], scalar=1.0, in1=gb[j % 2][:, :], op0=ALU.add, op1=ALU.mult))
                        ch.settle()
                        dve.tensor_tensor(h, h, ub[j % 2][:, :], ALU.mult).then_inc(gated.sem, 1)
                        if nxt is not None:
                            if j == 0:
                                norm_stats(dve, g, ln, nxt)
                            if j == 1:
                                norm_apply(dve, g, ln, nxt)
                            if j == 3:
                                shift(nxt, route)
                            if j == 4:
                                probabilities(nxt, route)
                                first(route)
                            if j == 5:
                                second(route)
                            if j == 6:
                                split(nxt)
                            if j == 7:
                                dve.wait_ge(pair_ps.sem, pair_ps.at(t, NP - 1))
                                weights_in(nxt)
                    ch.end()
                    dve.wait_ge(hid_used.sem, hid_used.at(t, NP))
                    x = x_tiles(g, t, N)
                    dve.tensor_tensor(x, acc[:, :].rearrange("p (k d) -> p k d", d=P), x, ALU.add).then_inc(added.sem, 1)

                dve.nop().then_inc(added.sem, 1)
                dve.memset(parts[:, :, :, :], 0.0).then_inc(s["cleared"].sem, 1)
                dve.tensor_copy(pick[:, :], c("pick_expert")[0:3 * E, :]).then_inc(s["pick_ready"].sem, 1)
                norm_vector(dve, g, ln, 0)
                route = Chain(dve, routing, 0)
                shift(0, route)
                probabilities(0, route)
                first(route)
                second(route)
                dve.wait_ge(s["cleared"].sem, 1)
                split(0)
                weights_in(0)
                each_turn(dve, turns, turn)

            @block.gpsimd
            def _(pool):
                def turn(t, nxt):
                    for j in range(NP - 1):
                        pool.wait_ge(gated.sem, gated.at(t, j + 1))
                        pool.wait_ge(share_ready.sem, share_ready.at(t, j + 1))
                        h = hid[:, j % HID, :]
                        pool.tensor_tensor(h, h, share[:, j % 2, :], ALU.mult).then_inc(hid_ready.sem, 1)
                        if nxt is not None and j == 0:
                            norm_pool(pool, ln, nxt)

                norm_pool_setup(pool, ln)
                norm_pool(pool, ln, 0)
                each_turn(pool, turns, turn)

            @block.scalar
            def _(act):
                def x_in(t):
                    act.wait_ge(s["xT_ps"].sem, s["xT_ps"].at(t, 1))
                    act.copy(xT_new[:, :], misc[:, :]).then_inc(s["xT_ready"].sem, 1)

                def exponentials(t):
                    act.wait_ge(s["shifted"].sem, s["shifted"].at(t, 1))
                    act.activation(key[:, :, :], rest[:, :, :], ACT.Exp).then_inc(s["exped"].sem, 1)

                def adopt(t):
                    act.wait_ge(s["xT_ready"].sem, s["xT_ready"].at(t, 1))
                    act.copy(xT[:, :], xT_new[:, :]).then_inc(s["adopted"].sem, 1)

                def turn(t, nxt):
                    for j in range(NP):
                        act.wait_ge(pair_ps.sem, pair_ps.at(t, j + 1))
                        if j >= 2:
                            act.wait_ge(gated.sem, gated.at(t, j - 1))
                        act.activation(th[:, j % 2, :], gb[j % 2][:, :], ACT.Tanh, scale=0.5).then_inc(tanhed.sem, 1)
                        if j < NP - 1:
                            if j >= 2:
                                act.wait_ge(hid_ready.sem, hid_ready.at(t, j - 1))
                            act.copy(share[:, j % 2, :], cb[j % 2][:, :]).then_inc(share_ready.sem, 1)
                        if nxt is not None:
                            if j == 2:
                                x_in(nxt)
                            if j == 4:
                                exponentials(nxt)
                    if nxt is not None:
                        adopt(nxt)

                x_in(0)
                adopt(0)
                exponentials(0)
                each_turn(act, turns, turn)

            @block.tensor
            def _(pe):
                def logits(t):
                    pe.wait_ge(s["xT_ready"].sem, s["xT_ready"].at(t, 1))
                    for k in range(N):
                        last = pe.matmul(misc[:, k * E:(k + 1) * E], xT_new[:, k * P:(k + 1) * P], g["wr2"][:, :], start=True, stop=True)
                    last.then_inc(s["logit_ps"].sem, 1)

                def turn_weights(t):
                    pe.wait_ge(s["split"].sem, s["split"].at(t, 1))
                    for k in range(N):
                        last = pe.transpose(misc[:, k * P:(k + 1) * P], parts[:, k, :, :].rearrange("p a e -> p (a e)"), c("ident"))
                    last.then_inc(s["wT_ps"].sem, 1)

                def down(t, j):
                    if j < NP - 1:
                        pe.wait_ge(hid_ready.sem, hid_ready.at(t, j + 1))
                    else:
                        pe.wait_ge(gated.sem, gated.at(t, NP))
                    if j == 0:
                        pe.wait_ge(added.sem, added.at(t, 1))
                    for k in range(N):
                        last = pe.matmul(acc[:, k * P:(k + 1) * P], hid[:, j % HID, k * P:(k + 1) * P], g["wd2"][:, j, :],
                                         start=(j == 0 and k == 0), stop=(j == NP - 1), skip_group_check=True)
                    last.then_inc(hid_used.sem, 1)

                def turn(t, nxt):
                    pe.wait_ge(s["adopted"].sem, s["adopted"].at(t, 1))
                    pe.wait_ge(s["wT_ready"].sem, s["wT_ready"].at(t, 1))
                    for j in range(NP):
                        if j >= 2:
                            pe.wait_ge(gated.sem, gated.at(t, j - 1))
                            pe.wait_ge(share_ready.sem, share_ready.at(t, j - 1))
                        if j < NP - 1:
                            wg = g["wg2"][:, 2 * j:2 * j + 2, :].rearrange("p e f -> p (e f)")
                            wu = g["wu2"][:, 2 * j:2 * j + 2, :].rearrange("p e f -> p (e f)")
                            pe.matmul(cb[j % 2][:, :], pick[:, j * P:(j + 1) * P], wT[:, :], start=True, stop=True)
                        else:
                            wg, wu = g["sgu2"][:, 0, :], g["sgu2"][:, 1, :]
                        pe.matmul(gb[j % 2][:, :], wg, xT[:, :], start=True, stop=True)
                        pe.matmul(ub[j % 2][:, :], wu, xT[:, :], start=True, stop=True).then_inc(pair_ps.sem, 1)
                        if j >= 2:
                            down(t, j - 2)
                        if nxt is not None:
                            if j == 2:
                                turn_tokens(pe, g, ln, misc, s["xT_ps"], nxt)
                            if j == 3:
                                logits(nxt)
                            if j == 7:
                                turn_weights(nxt)
                    down(t, NP - 2)
                    down(t, NP - 1)

                pe.wait_ge(s["pick_ready"].sem, 1)
                turn_tokens(pe, g, ln, misc, s["xT_ps"], 0)
                logits(0)
                turn_weights(0)
                each_turn(pe, turns, turn)


def ffn3(nc, g, NB, pre):
    N, NH = 4, 3
    with ExitStack() as ctx:
        sb = lambda name, shape, dt=F32: ctx.enter_context(nc.sbuf_tensor(name, shape, dt))
        ln = norm_parts(nc, sb, pre, N)
        xT = sb(pre + "xT", [P, N * P])
        th = sb(pre + "th", [P, NH, N * P])
        hid = sb(pre + "hid", [P, NH, N * P])
        xT_ps, xT_ready = Signal(nc, pre + "xT_ps"), Signal(nc, pre + "xT_ready")
        part_ps, tanhed, hid_ready, down_ps = (Signal(nc, pre + n, NH) for n in ("part_ps", "tanhed", "hid_ready", "down_ps"))
        chain = Signal(nc, pre + "chain", NH)
        added = Signal(nc, pre + "added")
        misc, acc = g["bank"][0], g["bank"][1]
        gb, ub = g["bank"][2:5], g["bank"][5:8]
        turns = NB * 2 // N
        with nc.Block() as block:
            @block.vector
            def _(dve):
                def turn(t, nxt):
                    ch = Chain(dve, chain, t)
                    for j in range(NH):
                        if nxt is not None and j == 0:
                            norm_stats(dve, g, ln, nxt)
                        dve.wait_ge(tanhed.sem, tanhed.at(t, j + 1))
                        ch.did(dve.scalar_tensor_tensor(out=hid[:, j, :], in0=th[:, j, :], scalar=1.0, in1=gb[j][:, :], op0=ALU.add, op1=ALU.mult))
                        ch.settle()
                        dve.tensor_tensor(hid[:, j, :], hid[:, j, :], ub[j][:, :], ALU.mult).then_inc(hid_ready.sem, 1)
                        if nxt is not None and j == 0:
                            norm_apply(dve, g, ln, nxt)
                    ch.end()
                    dve.wait_ge(down_ps.sem, down_ps.at(t, NH))
                    x = x_tiles(g, t, N)
                    dve.tensor_tensor(x, acc[:, :].rearrange("p (k d) -> p k d", d=P), x, ALU.add).then_inc(added.sem, 1)

                dve.nop().then_inc(added.sem, 1)
                norm_vector(dve, g, ln, 0)
                each_turn(dve, turns, turn)

            @block.gpsimd
            def _(pool):
                norm_pool_setup(pool, ln)
                with pool.Fori(0, turns) as t:
                    norm_pool(pool, ln, t)

            @block.scalar
            def _(act):
                def x_in(t):
                    act.wait_ge(xT_ps.sem, xT_ps.at(t, 1))
                    act.copy(xT[:, :], misc[:, :]).then_inc(xT_ready.sem, 1)

                def turn(t, nxt):
                    for j in range(NH):
                        act.wait_ge(part_ps.sem, part_ps.at(t, j + 1))
                        act.activation(th[:, j, :], gb[j][:, :], ACT.Tanh, scale=0.5).then_inc(tanhed.sem, 1)
                    if nxt is not None:
                        x_in(nxt)

                x_in(0)
                each_turn(act, turns, turn)

            @block.tensor
            def _(pe):
                def turn(t, nxt):
                    pe.wait_ge(xT_ready.sem, xT_ready.at(t, 1))
                    for j in range(NH):
                        pe.matmul(gb[j][:, :], g["wt"][:, WG3 + j, :], xT[:, :], start=True, stop=True)
                        pe.matmul(ub[j][:, :], g["wt"][:, WU3 + j, :], xT[:, :], start=True, stop=True).then_inc(part_ps.sem, 1)
                    if nxt is not None:
                        turn_tokens(pe, g, ln, misc, xT_ps, nxt)
                    pe.wait_ge(added.sem, added.at(t, 1))
                    for j in range(NH):
                        pe.wait_ge(hid_ready.sem, hid_ready.at(t, j + 1))
                        for k in range(N):
                            last = pe.matmul(acc[:, k * P:(k + 1) * P], hid[:, j, k * P:(k + 1) * P], g["wt"][:, WD3 + j, :],
                                             start=(j == 0 and k == 0), stop=(j == NH - 1), skip_group_check=True)
                        last.then_inc(down_ps.sem, 1)

                turn_tokens(pe, g, ln, misc, xT_ps, 0)
                each_turn(pe, turns, turn)


def att2(nc, g, NB, pre):
    N = 2
    with ExitStack() as ctx:
        sb = lambda name, shape, dt=F32: ctx.enter_context(nc.sbuf_tensor(name, shape, dt))
        ln = norm_parts(nc, sb, pre, N)
        xT = sb(pre + "xT", [P, S])
        qk = sb(pre + "qk", [P, 2, S])
        v = sb(pre + "v", [P, N, P])
        low = sb(pre + "low", [P, N])
        prob = sb(pre + "prob", [P, N, S])
        total = sb(pre + "total", [P, N])
        inv = sb(pre + "inv", [P, N])
        probT = sb(pre + "probT", [P, N, S])
        names = ("xT_ps", "xT_ready", "qk_ps", "qk_ready", "v_ps", "v_ready", "score_ps", "low_ready", "exped", "probT_ps", "probT_ready", "out_ps")
        s = {n: Signal(nc, pre + n, 2 if n == "exped" else 1) for n in names}
        chain = Signal(nc, pre + "chain", 3)
        turned, qk_b, v_b, score_b, probT_b, out_b = g["bank"][0:6]
        with nc.Block() as block:
            @block.vector
            def _(dve):
                def values_in(t):
                    dve.wait_ge(s["v_ps"].sem, s["v_ps"].at(t, 1))
                    dve.tensor_copy(v[:, :, :], v_b[:, 0:N * P].rearrange("p (k d) -> p k d", d=P)).then_inc(s["v_ready"].sem, 1)

                def turn(t, nxt):
                    ch = Chain(dve, chain, t)
                    dve.wait_ge(s["score_ps"].sem, s["score_ps"].at(t, 1))
                    dve.tensor_reduce(low[:, :], score_b[:, :].rearrange("p (k j) -> p k j", j=S), AX.X, ALU.max, negate=True).then_inc(s["low_ready"].sem, 1)
                    if nxt is not None:
                        norm_stats(dve, g, ln, nxt)
                        norm_apply(dve, g, ln, nxt)
                    dve.wait_ge(s["exped"].sem, s["exped"].at(t, 2))
                    ch.did(dve.reciprocal(inv[:, :], total[:, :]))
                    ch.settle()
                    dve.wait_ge(s["out_ps"].sem, s["out_ps"].at(t, 1))
                    for k in range(N):
                        x = x_tiles(g, t, N)[:, k, :]
                        ch.did(dve.scalar_tensor_tensor(out=x, in0=out_b[:, k * P:(k + 1) * P], scalar=inv[:, k:k + 1], in1=x, op0=ALU.mult, op1=ALU.add))
                    ch.settle()
                    ch.end()
                    if nxt is not None:
                        values_in(nxt)

                norm_vector(dve, g, ln, 0)
                values_in(0)
                each_turn(dve, NB, turn)

            @block.gpsimd
            def _(pool):
                norm_pool_setup(pool, ln)
                with pool.Fori(0, NB) as t:
                    norm_pool(pool, ln, t)

            @block.scalar
            def _(act):
                def x_in(t):
                    act.wait_ge(s["xT_ps"].sem, s["xT_ps"].at(t, 1))
                    act.copy(xT[:, :], turned[:, 0:S]).then_inc(s["xT_ready"].sem, 1)

                def queries_and_keys(t):
                    act.wait_ge(s["qk_ps"].sem, s["qk_ps"].at(t, 1))
                    act.copy(qk[:, :, :], qk_b[:, :].rearrange("p (a i) -> p a i", a=2)).then_inc(s["qk_ready"].sem, 1)

                def turn(t, nxt):
                    act.wait_ge(s["low_ready"].sem, s["low_ready"].at(t, 1))
                    for k in range(N):
                        act.activation(prob[:, k, :], score_b[:, k * S:(k + 1) * S], ACT.Exp, bias=low[:, k:k + 1],
                                       accum_out=total[:, k:k + 1]).then_inc(s["exped"].sem, 1)
                    act.wait_ge(s["probT_ps"].sem, s["probT_ps"].at(t, 1))
                    act.copy(probT[:, :, :], probT_b[:, :].rearrange("p (k i) -> p k i", k=N)).then_inc(s["probT_ready"].sem, 1)
                    if nxt is not None:
                        x_in(nxt)
                        queries_and_keys(nxt)

                x_in(0)
                queries_and_keys(0)
                each_turn(act, NB, turn)

            @block.tensor
            def _(pe):
                def project(t):
                    pe.wait_ge(s["xT_ready"].sem, s["xT_ready"].at(t, 1))
                    for a in range(2):
                        last = pe.matmul(qk_b[:, a * S:(a + 1) * S], g["wt"][:, WQ2 + a, :], xT[:, :], start=True, stop=True)
                    last.then_inc(s["qk_ps"].sem, 1)
                    for k in range(N):
                        last = pe.matmul(v_b[:, k * P:(k + 1) * P], xT[:, k * P:(k + 1) * P], g["wt"][:, WV2, :], start=True, stop=True)
                    last.then_inc(s["v_ps"].sem, 1)

                def scores(t):
                    pe.wait_ge(s["qk_ready"].sem, s["qk_ready"].at(t, 1))
                    for k in range(N):
                        last = pe.matmul(score_b[:, k * S:(k + 1) * S], qk[:, 0, k * P:(k + 1) * P], qk[:, 1, :], start=True, stop=True)
                    last.then_inc(s["score_ps"].sem, 1)

                def turn(t, nxt):
                    for k in range(N):
                        pe.wait_ge(s["exped"].sem, s["exped"].at(t, k + 1))
                        for j in range(N):
                            last = pe.transpose(probT_b[:, j * S + k * P:j * S + (k + 1) * P], prob[:, k, j * P:(j + 1) * P], g["c"]("ident"))
                    last.then_inc(s["probT_ps"].sem, 1)
                    if nxt is not None:
                        turn_tokens(pe, g, ln, turned, s["xT_ps"], nxt)
                    pe.wait_ge(s["v_ready"].sem, s["v_ready"].at(t, 1))
                    pe.wait_ge(s["probT_ready"].sem, s["probT_ready"].at(t, 1))
                    for k in range(N):
                        for j in range(N):
                            last = pe.matmul(out_b[:, k * P:(k + 1) * P], probT[:, j, k * P:(k + 1) * P], v[:, j, :], start=(j == 0), stop=(j == N - 1))
                    last.then_inc(s["out_ps"].sem, 1)
                    if nxt is not None:
                        project(nxt)
                        scores(nxt)

                turn_tokens(pe, g, ln, turned, s["xT_ps"], 0)
                project(0)
                scores(0)
                each_turn(pe, NB, turn)


def att0(nc, g, NB, pre):
    N, U, R = 2, S // 8, S // 16
    with ExitStack() as ctx:
        sb = lambda name, shape, dt=F32: ctx.enter_context(nc.sbuf_tensor(name, shape, dt))
        ln = norm_parts(nc, sb, pre, N)
        xT = sb(pre + "xT", [P, S])
        q = sb(pre + "q", [P, S])
        k = sb(pre + "k", [P, S])
        v = sb(pre + "v", [P, N, HEADS * (P + DK)])
        q_heads = sb(pre + "q_heads", [P, U, HEADS, 8])
        q_steps = sb(pre + "q_steps", [P, U, HEADS, 8])
        low = sb(pre + "low", [P, 2, 2])
        total = sb(pre + "total", [P, 2, 2])
        inv = sb(pre + "inv", [P, 2, 2])
        prob = sb(pre + "prob", [P, 2, 2, S])
        probT = sb(pre + "probT", [P, N, HEADS, S])
        oT = sb(pre + "oT", [P, S])
        s = {n: Signal(nc, pre + n) for n in ("xT_ps", "xT_ready", "proj_ps", "q_ready", "k_ready", "v_ready",
                                              "o_ps", "oT_ready", "out_ps", "cleared", "added")}
        qx_ps, qx_read, heads_ready = Signal(nc, pre + "qx_ps", 4), Signal(nc, pre + "qx_read", 4), Signal(nc, pre + "heads_ready", 4)
        score_ps, low_ready, inverted, normed, probT_ps, moved_act, moved_dve = (Signal(nc, pre + n, R) for n in (
            "score_ps", "low_ready", "inverted", "normed", "probT_ps", "moved_act", "moved_dve"))
        exped = Signal(nc, pre + "exped", 2 * R)
        bank = g["bank"]
        turned, qk_b, score_b, flip_b, o_b = bank[0], bank[1], bank[2:4], bank[4:6], bank[6]
        v_b, out_b = turned[:, S:2 * S], o_b[:, S:2 * S]
        qx_b = (bank[7], score_b[0])
        c = g["c"]

        def flipped(r, j):
            src = flip_b[r % 2][:, :].rearrange("p (k j h i) -> p k j h i", k=2, j=N, i=8)[:, :, j, :, :]
            dst = probT[:, j, :, 16 * r:16 * r + 16].rearrange("p h (k i) -> p k h i", k=2)
            return dst, src

        with nc.Block() as block:
            @block.vector
            def _(dve):
                def steps_in(t):
                    for w in range(4):
                        dve.wait_ge(qx_ps.sem, qx_ps.at(t, w + 1))
                        for m in range(2):
                            hp = 2 * w + m
                            for par in range(2):
                                rows = slice(64 * par, 64 * par + 64)
                                last = dve.scalar_tensor_tensor(
                                    out=q_steps[rows, :, 8 * par + hp, :], in0=qx_b[w % 2][rows, m * S:(m + 1) * S].rearrange("p (u i) -> p u i", i=8),
                                    scalar=g["col"][rows, hp:hp + 1], in1=c("step_of")[rows, :].rearrange("p (u i) -> p u i", i=8),
                                    op0=ALU.add, op1=ALU.mult)
                        last.then_inc(qx_read.sem, 1)

                def values_in(t):
                    dve.wait_ge(s["proj_ps"].sem, s["proj_ps"].at(t, 1))
                    for n in range(N):
                        last = dve.tensor_copy(v[:, n, :].rearrange("p (h c) -> p h c", h=HEADS)[:, :, 0:DK],
                                               v_b[:, n * P:(n + 1) * P].rearrange("p (h d) -> p h d", d=DK))
                    last.then_inc(s["v_ready"].sem, 1)

                def turn(t, nxt):
                    for r in range(R + 2):
                        if r < R:
                            dve.wait_ge(score_ps.sem, score_ps.at(t, r + 1))
                            if r >= 2:
                                dve.wait_ge(exped.sem, exped.at(t, 2 * (r - 1)))
                            dve.tensor_reduce(low[:, r % 2, :], score_b[r % 2][:, :].rearrange("p (k j) -> p k j", j=S),
                                              AX.X, ALU.max, negate=True).then_inc(low_ready.sem, 1)
                        if 1 <= r <= R:
                            m = (r - 1) % 2
                            dve.wait_ge(exped.sem, exped.at(t, 2 * r))
                            dve.reciprocal(inv[:, m, :], total[:, m, :]).then_inc(inverted.sem, 1)
                            dve.wait_ge(inverted.sem, inverted.at(t, r))
                            for half in range(2):
                                last = dve.tensor_scalar(prob[:, m, half, :], prob[:, m, half, :], inv[:, m, half:half + 1], None, ALU.mult)
                            last.then_inc(normed.sem, 1)
                        if r >= 2:
                            dve.wait_ge(probT_ps.sem, probT_ps.at(t, r - 1))
                            dve.wait_ge(moved_act.sem, moved_act.at(t, r - 1))
                            dve.tensor_copy(*flipped(r - 2, 1)).then_inc(moved_dve.sem, 1)
                        if nxt is not None:
                            if r == 1:
                                norm_stats(dve, g, ln, nxt)
                            if r == 2:
                                norm_apply(dve, g, ln, nxt)
                    if nxt is not None:
                        steps_in(nxt)
                        dve.wait_ge(s["o_ps"].sem, s["o_ps"].at(t, 1))
                        values_in(nxt)
                    dve.wait_ge(s["out_ps"].sem, s["out_ps"].at(t, 1))
                    x = x_tiles(g, t, N)
                    dve.tensor_tensor(x, out_b.rearrange("p (k d) -> p k d", d=P), x, ALU.add).then_inc(s["added"].sem, 1)

                dve.memset(q_steps[:, :, :, :], 0.0).then_inc(s["cleared"].sem, 1)
                dve.memset(v[:, :, :], 0.0).then_inc(s["cleared"].sem, 1)
                dve.wait_ge(s["cleared"].sem, 2)
                norm_vector(dve, g, ln, 0)
                steps_in(0)
                values_in(0)
                each_turn(dve, NB, turn)

            @block.gpsimd
            def _(pool):
                def heads_in(t, before):
                    pool.wait_ge(s["q_ready"].sem, s["q_ready"].at(t, 1))
                    for w in range(4):
                        if before is not None:
                            pool.wait_ge(score_ps.sem, score_ps.at(before, 4 * w + 4))
                        us = slice(8 * w, 8 * w + 8)
                        pool.tensor_tensor(q_heads[:, us, :, :],
                                           q[:, 64 * w:64 * w + 64].rearrange("p (u i) -> p u i", i=8).unsqueeze(2).broadcast_to([P, 8, HEADS, 8]),
                                           c("head_of").unsqueeze(1).unsqueeze(3).broadcast_to([P, 8, HEADS, 8]),
                                           ALU.mult).then_inc(heads_ready.sem, 1)

                def turn(t, nxt):
                    if nxt is not None:
                        norm_pool(pool, ln, nxt)
                        heads_in(nxt, t)

                norm_pool_setup(pool, ln)
                norm_pool(pool, ln, 0)
                heads_in(0, None)
                each_turn(pool, NB, turn)

            @block.scalar
            def _(act):
                def x_in(t):
                    act.wait_ge(s["xT_ps"].sem, s["xT_ps"].at(t, 1))
                    act.copy(xT[:, :], turned[:, 0:S]).then_inc(s["xT_ready"].sem, 1)

                def queries_in(t):
                    act.wait_ge(s["proj_ps"].sem, s["proj_ps"].at(t, 1))
                    act.activation(q[:, :], qk_b[:, 0:S], ACT.Identity, bias=g["col"][:, 8:9]).then_inc(s["q_ready"].sem, 1)

                def keys_in(t):
                    act.activation(k[:, :], qk_b[:, S:2 * S], ACT.Identity, bias=g["col"][:, 9:10]).then_inc(s["k_ready"].sem, 1)

                def turn(t, nxt):
                    for r in range(R + 2):
                        if r < R:
                            act.wait_ge(low_ready.sem, low_ready.at(t, r + 1))
                            if r >= 2:
                                act.wait_ge(probT_ps.sem, probT_ps.at(t, r - 1))
                            for m in range(2):
                                act.activation(prob[:, r % 2, m, :], score_b[r % 2][:, m * S:(m + 1) * S], ACT.Exp,
                                               bias=low[:, r % 2, m:m + 1], accum_out=total[:, r % 2, m:m + 1]).then_inc(exped.sem, 1)
                        if r >= 2:
                            act.wait_ge(probT_ps.sem, probT_ps.at(t, r - 1))
                            act.copy(*flipped(r - 2, 0)).then_inc(moved_act.sem, 1)
                        if nxt is not None:
                            if r == 6:
                                x_in(nxt)
                            if r == 8:
                                queries_in(nxt)
                            if r == R - 1:
                                keys_in(nxt)
                    act.wait_ge(s["o_ps"].sem, s["o_ps"].at(t, 1))
                    act.copy(oT[:, :], o_b[:, 0:S]).then_inc(s["oT_ready"].sem, 1)

                x_in(0)
                queries_in(0)
                keys_in(0)
                each_turn(act, NB, turn)

            @block.tensor
            def _(pe):
                def project(t):
                    pe.wait_ge(s["xT_ready"].sem, s["xT_ready"].at(t, 1))
                    for a in range(2):
                        pe.matmul(qk_b[:, a * S:(a + 1) * S], g["wt"][:, WQ0 + a, :], xT[:, :], start=True, stop=True)
                    for n in range(N):
                        pe.matmul(v_b[:, n * P:(n + 1) * P], xT[:, n * P:(n + 1) * P], g["wt"][:, WV0, :], start=True, stop=False)
                        last = add_bias(pe, g, v_b[:, n * P:(n + 1) * P], B_V0, True)
                    last.then_inc(s["proj_ps"].sem, 1)

                def repeated_queries(t, w):
                    if w >= 2:
                        pe.wait_ge(qx_read.sem, qx_read.at(t, w - 1))
                    for m in range(2):
                        last = pe.matmul(qx_b[w % 2][:, m * S:(m + 1) * S], g["wqx"][:, 2 * w + m, :], xT[:, :], start=True, stop=True)
                    last.then_inc(qx_ps.sem, 1)

                def scores(t, r):
                    if r >= 2:
                        pe.wait_ge(exped.sem, exped.at(t, 2 * (r - 1)))
                    if r == 0:
                        pe.wait_ge(s["k_ready"].sem, s["k_ready"].at(t, 1))
                        pe.wait_ge(qx_read.sem, qx_read.at(t, 4))
                    if r % 4 == 0:
                        pe.wait_ge(heads_ready.sem, heads_ready.at(t, r // 4 + 1))
                    for m in range(2):
                        u = 2 * r + m
                        dst = score_b[r % 2][:, m * S:(m + 1) * S]
                        pe.matmul(dst, q_heads[:, u, :, :].rearrange("p h i -> p (h i)"), k[:, :], start=True, stop=False)
                        last = pe.matmul(dst, q_steps[:, u, :, :].rearrange("p h i -> p (h i)"), g["er_win"][:, S - 8 - 8 * u:2 * S - 8 - 8 * u],
                                         start=False, stop=True)
                    last.then_inc(score_ps.sem, 1)

                def flips(t, r):
                    pe.wait_ge(normed.sem, normed.at(t, r + 1))
                    if r >= 2:
                        pe.wait_ge(moved_dve.sem, moved_dve.at(t, r - 1))
                    for m in range(2):
                        for j in range(N):
                            last = pe.transpose(flip_b[r % 2][:, (2 * m + j) * P:(2 * m + j + 1) * P], prob[:, r % 2, m, j * P:(j + 1) * P], c("ident"))
                    last.then_inc(probT_ps.sem, 1)

                def turn(t, nxt):
                    scores(t, 1)
                    for r in range(R):
                        if r + 2 < R:
                            scores(t, r + 2)
                        elif nxt is not None:
                            if r == R - 1:
                                pe.wait_ge(exped.sem, exped.at(t, 2 * (R - 1)))
                            repeated_queries(nxt, r + 2 - R)
                        flips(t, r)
                        if nxt is not None:
                            if r == 4:
                                turn_tokens(pe, g, ln, turned, s["xT_ps"], nxt)
                            if r == 6:
                                project(nxt)
                    pe.wait_ge(s["v_ready"].sem, s["v_ready"].at(t, 1))
                    pe.wait_ge(moved_dve.sem, moved_dve.at(t, R))
                    for h in range(HEADS):
                        for j in range(N):
                            last = pe.matmul(o_b[:, 0:S], v[:, j, h * P:(h + 1) * P], probT[:, j, h, :],
                                             start=(h == 0 and j == 0), stop=(h == HEADS - 1 and j == N - 1))
                        if nxt is not None and h in (4, 7):
                            repeated_queries(nxt, 2 if h == 4 else 3)
                    last.then_inc(s["o_ps"].sem, 1)
                    if nxt is not None:
                        scores(nxt, 0)
                    pe.wait_ge(s["oT_ready"].sem, s["oT_ready"].at(t, 1))
                    for n in range(N):
                        pe.matmul(out_b[:, n * P:(n + 1) * P], oT[:, n * P:(n + 1) * P], g["wt"][:, WO0, :], start=True, stop=False)
                        last = add_bias(pe, g, out_b[:, n * P:(n + 1) * P], B_O0, True)
                    last.then_inc(s["out_ps"].sem, 1)

                pe.wait_ge(s["cleared"].sem, 2)
                turn_tokens(pe, g, ln, turned, s["xT_ps"], 0)
                project(0)
                for w in range(4):
                    repeated_queries(0, w)
                scores(0, 0)
                each_turn(pe, NB, turn)


def att3(nc, g, NB, pre):
    N = 2
    with ExitStack() as ctx:
        sb = lambda name, shape, dt=F32: ctx.enter_context(nc.sbuf_tensor(name, shape, dt))
        ln = norm_parts(nc, sb, pre, N)
        xT = sb(pre + "xT", [P, S])
        lin = sb(pre + "lin", [P, 2, S])
        neg = sb(pre + "neg", [P, 2, S])
        feat = sb(pre + "feat", [P, 2, S])
        rot = sb(pre + "rot", [P, 2, S])
        part = sb(pre + "part", [P, 2, S])
        q = sb(pre + "q", [P, 2, S])
        k_pick = sb(pre + "k_pick", [P, 2, HEADS, S])
        v = sb(pre + "v", [P, N, HEADS * (P + DK)])
        log_den = sb(pre + "log_den", [P, 2, N * S])
        inv = sb(pre + "inv", [P, 2, N * S])
        miss = sb(pre + "miss", [P, 2, N * S])
        rough = sb(pre + "rough", [P, 2, N * S])
        w = sb(pre + "w", [P, 2, N, S])
        oT = sb(pre + "oT", [P, S])
        s = {n: Signal(nc, pre + n) for n in ("xT_ps", "xT_ready", "qk_ps", "lin_ready", "exped", "part_ready", "swapped", "feat_ready", "swap_ps", "rot_ready",
                                              "v_ps", "v_ready", "oT_ready", "out_ps", "cleared")}
        pick_ready, q_ready = Signal(nc, pre + "pick_ready", 8), Signal(nc, pre + "q_ready", 2)
        den_ps, num_ps, logged, inverted, w_ready, w_used = (Signal(nc, pre + n, HEADS) for n in (
            "den_ps", "num_ps", "logged", "inverted", "w_ready", "w_used"))
        refined = Signal(nc, pre + "refined", 2 * HEADS)
        added = Signal(nc, pre + "added")
        bank = g["bank"]
        turned, qk_b, swap_b, o_b, num_b, den_b = bank[0], bank[1], bank[2], bank[3], bank[4:6], bank[6:8]
        v_b = turned[:, S:2 * S]
        c = g["c"]
        flat = lambda a: a[:, :, :].rearrange("p a i -> p (a i)")
        with nc.Block() as block:
            @block.vector
            def _(dve):
                def turn_swapped(t):
                    dve.wait_ge(s["swap_ps"].sem, s["swap_ps"].at(t, 1))
                    dve.tensor_tensor(flat(rot), swap_b[:, :], c("sin"), ALU.mult).then_inc(s["swapped"].sem, 1)

                def values_in(t):
                    dve.wait_ge(s["v_ps"].sem, s["v_ps"].at(t, 1))
                    for n in range(N):
                        last = dve.tensor_scalar(v[:, n, :].rearrange("p (h c) -> p h c", h=HEADS)[:, :, 0:DK],
                                                 v_b[:, n * P:(n + 1) * P].rearrange("p (h d) -> p h d", d=DK), -1.0, None, ALU.mult)
                    last.then_inc(s["v_ready"].sem, 1)

                def turn(t, nxt):
                    for h in range(HEADS):
                        if h >= 2:
                            dve.wait_ge(w_ready.sem, w_ready.at(t, h - 1))
                        dve.wait_ge(inverted.sem, inverted.at(t, h + 1))
                        dve.tensor_tensor(miss[:, h % 2, :], den_b[h % 2][:, :], inv[:, h % 2, :], ALU.mult).then_inc(refined.sem, 1)
                        dve.wait_ge(num_ps.sem, num_ps.at(t, h + 1))
                        dve.tensor_tensor(rough[:, h % 2, :], num_b[h % 2][:, :], inv[:, h % 2, :], ALU.mult).then_inc(refined.sem, 1)
                        dve.wait_ge(refined.sem, refined.at(t, 2 * h + 2))
                        if h >= 2:
                            dve.wait_ge(w_used.sem, w_used.at(t, h - 1))
                        dve.scalar_tensor_tensor(out=w[:, h % 2, :, :].rearrange("p n i -> p (n i)"), in0=miss[:, h % 2, :], scalar=2.0, in1=rough[:, h % 2, :],
                                                 op0=ALU.subtract, op1=ALU.mult).then_inc(w_ready.sem, 1)
                        if nxt is not None:
                            if h == 0:
                                norm_stats(dve, g, ln, nxt)
                            if h == 2:
                                norm_apply(dve, g, ln, nxt)
                            if h == 8:
                                dve.wait_ge(pick_ready.sem, pick_ready.at(t, 8))
                                dve.wait_ge(q_ready.sem, q_ready.at(t, 2))
                                turn_swapped(nxt)
                    if nxt is not None:
                        dve.wait_ge(w_used.sem, w_used.at(t, HEADS))
                        values_in(nxt)
                    dve.wait_ge(s["out_ps"].sem, s["out_ps"].at(t, 1))
                    x = x_tiles(g, t, N)
                    dve.tensor_tensor(x, swap_b[:, 0:N * P].rearrange("p (k d) -> p k d", d=P), x, ALU.add).then_inc(added.sem, 1)

                dve.memset(v[:, :, :], 0.0).then_inc(s["cleared"].sem, 1)
                dve.wait_ge(s["cleared"].sem, 1)
                norm_vector(dve, g, ln, 0)
                turn_swapped(0)
                values_in(0)
                each_turn(dve, NB, turn)

            @block.gpsimd
            def _(pool):
                def features(t):
                    pool.wait_ge(s["exped"].sem, s["exped"].at(t, 1))
                    pool.tensor_tensor(flat(feat), flat(lin), flat(neg), ALU.add).then_inc(s["feat_ready"].sem, 1)
                    pool.wait_ge(s["feat_ready"].sem, s["feat_ready"].at(t, 1))
                    pool.tensor_tensor(flat(part), flat(feat), c("cos"), ALU.mult).then_inc(s["part_ready"].sem, 1)
                    pool.wait_ge(s["part_ready"].sem, s["part_ready"].at(t, 1))
                    pool.wait_ge(s["swapped"].sem, s["swapped"].at(t, 1))
                    pool.tensor_tensor(flat(rot), flat(rot), flat(part), ALU.add).then_inc(s["rot_ready"].sem, 1)

                def picks(t, before):
                    pool.wait_ge(s["rot_ready"].sem, s["rot_ready"].at(t, 1))
                    for b in range(4):
                        hs = slice(4 * b, 4 * b + 4)
                        pick = c("head_of")[:, hs].unsqueeze(2).broadcast_to([P, 4, S])
                        if before is not None:
                            pool.wait_ge(num_ps.sem, num_ps.at(before, 4 * b + 4))
                        for kind, src in ((0, feat), (1, rot)):
                            pool.tensor_tensor(k_pick[:, kind, hs, :], src[:, 1:2, :].broadcast_to([P, 4, S]), pick, ALU.mult).then_inc(pick_ready.sem, 1)

                def turn(t, nxt):
                    if nxt is not None:
                        norm_pool(pool, ln, nxt)
                        pool.wait_ge(q_ready.sem, q_ready.at(t, 2))
                        features(nxt)
                        picks(nxt, t)

                norm_pool_setup(pool, ln)
                norm_pool(pool, ln, 0)
                features(0)
                picks(0, None)
                each_turn(pool, NB, turn)

            @block.scalar
            def _(act):
                def x_in(t):
                    act.wait_ge(s["xT_ps"].sem, s["xT_ps"].at(t, 1))
                    act.copy(xT[:, :], turned[:, 0:S]).then_inc(s["xT_ready"].sem, 1)

                def linear(t):
                    act.wait_ge(s["qk_ps"].sem, s["qk_ps"].at(t, 1))
                    for a in range(2):
                        act.activation(lin[:, a, :], qk_b[:, a * S:(a + 1) * S], ACT.Relu, bias=g["col"][:, 10 + a:11 + a])
                        last = act.activation(neg[:, a, :], qk_b[:, a * S:(a + 1) * S], ACT.Relu, bias=g["col"][:, 12 + a:13 + a], scale=-1.0)
                    last.then_inc(s["lin_ready"].sem, 1)

                def exponentials(t):
                    act.wait_ge(s["lin_ready"].sem, s["lin_ready"].at(t, 1))
                    act.activation(flat(neg), flat(neg), ACT.Exp, scale=-1.0).then_inc(s["exped"].sem, 1)

                def queries(t):
                    act.wait_ge(s["feat_ready"].sem, s["feat_ready"].at(t, 1))
                    act.copy(q[:, 0, :], feat[:, 0, :]).then_inc(q_ready.sem, 1)
                    act.wait_ge(s["rot_ready"].sem, s["rot_ready"].at(t, 1))
                    act.copy(q[:, 1, :], rot[:, 0, :]).then_inc(q_ready.sem, 1)

                def turn(t, nxt):
                    for h in range(HEADS):
                        act.wait_ge(den_ps.sem, den_ps.at(t, h + 1))
                        if h >= 2:
                            act.wait_ge(inverted.sem, inverted.at(t, h - 1))
                        act.activation(log_den[:, h % 2, :], den_b[h % 2][:, :], ACT.Ln).then_inc(logged.sem, 1)
                        act.wait_ge(logged.sem, logged.at(t, h + 1))
                        if h >= 2:
                            act.wait_ge(w_ready.sem, w_ready.at(t, h - 1))
                        act.activation(inv[:, h % 2, :], log_den[:, h % 2, :], ACT.Exp, scale=-1.0).then_inc(inverted.sem, 1)
                        if nxt is not None:
                            if h == 4:
                                x_in(nxt)
                            if h == 5:
                                linear(nxt)
                            if h == 6:
                                exponentials(nxt)
                    if nxt is not None:
                        act.wait_ge(num_ps.sem, num_ps.at(t, HEADS))
                        queries(nxt)
                    act.wait_ge(w_used.sem, w_used.at(t, HEADS))
                    act.copy(oT[:, :], o_b[:, 0:S]).then_inc(s["oT_ready"].sem, 1)

                act.add_instruction(mybir.InstLoadActFuncSet(name=nc.get_next_instruction_name(), act_func_set_id=6))
                x_in(0)
                linear(0)
                exponentials(0)
                queries(0)
                each_turn(act, NB, turn)

            @block.tensor
            def _(pe):
                def project(t):
                    pe.wait_ge(s["xT_ready"].sem, s["xT_ready"].at(t, 1))
                    for a in range(2):
                        last = pe.matmul(qk_b[:, a * S:(a + 1) * S], g["wqkv3"][:, a * P:(a + 1) * P], xT[:, :], start=True, stop=True)
                    last.then_inc(s["qk_ps"].sem, 1)
                    for n in range(N):
                        pe.matmul(v_b[:, n * P:(n + 1) * P], xT[:, n * P:(n + 1) * P], g["wqkv3"][:, 2 * P:3 * P], start=True, stop=False)
                        last = add_bias(pe, g, v_b[:, n * P:(n + 1) * P], B_V3, True)
                    last.then_inc(s["v_ps"].sem, 1)

                def swap(t):
                    pe.wait_ge(s["feat_ready"].sem, s["feat_ready"].at(t, 1))
                    pe.matmul(swap_b[:, :], c("swap"), flat(feat), start=True, stop=True).then_inc(s["swap_ps"].sem, 1)

                def weights(t, h, before=None):
                    if h == 0:
                        pe.wait_ge(q_ready.sem, q_ready.at(t, 2))
                        if before is not None:
                            pe.wait_ge(w_ready.sem, w_ready.at(before, HEADS - 1))
                    if h % 4 == 0:
                        pe.wait_ge(pick_ready.sem, pick_ready.at(t, 2 * (h // 4) + 2))
                    for kind, banks, done in ((0, den_b, den_ps), (1, num_b, num_ps)):
                        if h >= 2:
                            pe.wait_ge(w_ready.sem, w_ready.at(t, h - 1))
                        for j in range(N):
                            last = pe.matmul(banks[h % 2][:, j * S:(j + 1) * S], k_pick[:, kind, h, j * P:(j + 1) * P],
                                             q[:, kind, :], start=True, stop=True)
                        last.then_inc(done.sem, 1)

                def values(t, h):
                    pe.wait_ge(w_ready.sem, w_ready.at(t, h + 1))
                    for j in range(N):
                        last = pe.matmul(o_b[:, 0:S], v[:, j, h * P:(h + 1) * P], w[:, h % 2, j, :],
                                         start=(h == 0 and j == 0), stop=(h == HEADS - 1 and j == N - 1))
                    last.then_inc(w_used.sem, 1)

                def turn(t, nxt):
                    pe.wait_ge(s["v_ready"].sem, s["v_ready"].at(t, 1))
                    for h in range(HEADS):
                        if h + 1 < HEADS:
                            weights(t, h + 1)
                        elif nxt is not None:
                            weights(nxt, 0, t)
                        values(t, h)
                        if nxt is not None:
                            if h == 3:
                                turn_tokens(pe, g, ln, turned, s["xT_ps"], nxt)
                            if h == 4:
                                project(nxt)
                            if h == 7:
                                swap(nxt)
                    if nxt is not None:
                        pe.wait_ge(s["rot_ready"].sem, s["rot_ready"].at(nxt, 1))
                    pe.wait_ge(s["oT_ready"].sem, s["oT_ready"].at(t, 1))
                    for n in range(N):
                        pe.matmul(swap_b[:, n * P:(n + 1) * P], oT[:, n * P:(n + 1) * P], g["wout3"][:, :], start=True, stop=False)
                        last = add_bias(pe, g, swap_b[:, n * P:(n + 1) * P], B_O3, True)
                    last.then_inc(s["out_ps"].sem, 1)

                pe.wait_ge(s["cleared"].sem, 1)
                turn_tokens(pe, g, ln, turned, s["xT_ps"], 0)
                project(0)
                swap(0)
                weights(0, 0)
                each_turn(pe, NB, turn)


def att1(nc, g, NB, pre):
    N, B, H, D = 2, 4, 16, 64
    U, KEYS, BK = 8, 3 * WIN, 6 * WIN
    G = H // 2
    with ExitStack() as ctx:
        sb = lambda name, shape, dt=F32: ctx.enter_context(nc.sbuf_tensor(name, shape, dt))
        ln = norm_parts(nc, sb, pre, N)
        xT = sb(pre + "xT", [P, ROWS, WIN])
        q = sb(pre + "q", [P, G, B * U, 4, 8])
        k = sb(pre + "k", [P, G, ROWS * WIN])
        v = sb(pre + "v", [BK, 2, H * D])
        masked = sb(pre + "masked", [P, 2, U, KEYS])
        moved = sb(pre + "moved", [P, U, KEYS])
        ex = sb(pre + "ex", [P, U, KEYS])
        low = sb(pre + "low", [P, U])
        total = sb(pre + "total", [P, U])
        prob = sb(pre + "prob", [P, 4 * (2 * BK + WIN)])
        mixed = sb(pre + "mixed", [BK, H, U, 8])
        oT = sb(pre + "oT", [P, G, S + 4])
        s = {n: Signal(nc, pre + n) for n in ("xT_ps", "xT_ready", "first_ps", "first_ready", "out_ps", "cleared", "out_read")}
        q_ps, q_act, q_dve = (Signal(nc, pre + n, G // 2) for n in ("q_ps", "q_act", "q_dve"))
        k_ps, k_ready = Signal(nc, pre + "k_ps", G), Signal(nc, pre + "k_ready", G)
        v_ps, v_act, v_dve, score_ps, masked_ready, low_ready, moved_ready, exped, prob_ready, pv_ps, oT_ready = (
            Signal(nc, pre + n, B) for n in ("v_ps", "v_act", "v_dve", "score_ps", "masked_ready", "low_ready", "moved_ready",
                                             "exped", "prob_ready", "pv_ps", "oT_ready"))
        mix_ps, mixed_ready = Signal(nc, pre + "mix_ps", 2 * B), Signal(nc, pre + "mixed_ready", 2 * B)
        chain = Signal(nc, pre + "chain", 2 * B + 1)
        bank = g["bank"]
        turned, pv_b, v_b, score_b, mix_b = bank[0], bank[1:3], bank[3:5], bank[5], bank[6:8]
        out_ps = pv_b[0][:, 0:S]
        c = g["c"]
        window = c("window").rearrange("p (f u k) -> p f u k", f=2, u=U)

        def query_block(gp, half):
            rows = slice(D * half, D * half + D)
            src = v_b[(gp // 2) % 2][rows, (gp % 2) * S:(gp % 2 + 1) * S].rearrange("p (u i) -> p u i", i=8)
            return q[rows, gp, :, 2 * (gp % 2) + half, :], src

        with nc.Block() as block:
            @block.vector
            def _(dve):
                def queries_in(t):
                    for w in range(G // 2):
                        dve.wait_ge(q_ps.sem, q_ps.at(t, w + 1))
                        dve.wait_ge(q_act.sem, q_act.at(t, w + 1))
                        dve.tensor_copy(*query_block(2 * w + 1, 0))
                        dve.tensor_copy(*query_block(2 * w + 1, 1)).then_inc(q_dve.sem, 1)

                def turn(t, nxt):
                    ch = Chain(dve, chain, t)
                    for b in range(B):
                        dve.wait_ge(v_ps.sem, v_ps.at(t, b + 1))
                        if b >= 2:
                            dve.wait_ge(pv_ps.sem, pv_ps.at(t, b - 1))
                        dve.tensor_copy(v[:, b % 2, 0:512], v_b[0][0:BK, :]).then_inc(v_dve.sem, 1)
                        dve.wait_ge(score_ps.sem, score_ps.at(t, b + 1))
                        dve.tensor_tensor(masked[:, b % 2, :, :], score_b[:, 0:U * KEYS].rearrange("p (u k) -> p u k", k=KEYS),
                                          window[:, min(b, 1), :, :], ALU.add).then_inc(masked_ready.sem, 1)
                        dve.wait_ge(masked_ready.sem, masked_ready.at(t, b + 1))
                        dve.tensor_reduce(low[:, :], masked[:, b % 2, :, :], AX.X, ALU.max, negate=True).then_inc(low_ready.sem, 1)
                        if nxt is not None and b == 0:
                            norm_stats(dve, g, ln, nxt)
                        if nxt is not None and b == 1:
                            norm_apply(dve, g, ln, nxt)
                        dve.wait_ge(exped.sem, exped.at(t, b + 1))
                        ch.did(dve.tensor_reduce(total[:, :], ex[:, :, :], AX.X, ALU.add))
                        ch.settle()
                        ch.did(dve.reciprocal(total[:, :], total[:, :]))
                        ch.settle()
                        if b >= 1:
                            dve.wait_ge(mix_ps.sem, mix_ps.at(t, 2 * b))
                        place = prob[:, :].rearrange("p (r c) -> p r c", r=4)[:, :, 0:2 * BK].rearrange("p r (u k) -> p r u k", u=2)[:, :, :, 0:KEYS]
                        dve.tensor_tensor(place, ex[:, :, :].rearrange("p (r u) k -> p r u k", u=2),
                                          total[:, :].rearrange("p (r u) -> p r u", u=2).unsqueeze(3).broadcast_to([P, 4, 2, KEYS]),
                                          ALU.mult).then_inc(prob_ready.sem, 1)
                    if nxt is not None:
                        queries_in(nxt)
                    dve.wait_ge(s["out_ps"].sem, s["out_ps"].at(t, 1))
                    x = x_tiles(g, t, N)
                    ch.did(dve.tensor_tensor(x, out_ps.rearrange("p (k d) -> p k d", d=P), x, ALU.add))
                    ch.settle()
                    ch.end()

                dve.memset(q[:, :, :, :, :].rearrange("p a b c d -> p (a b c d)"), 0.0).then_inc(s["cleared"].sem, 1)
                dve.memset(prob[:, :], 0.0).then_inc(s["cleared"].sem, 1)
                dve.memset(xT[:, :, :], 0.0).then_inc(s["cleared"].sem, 1)
                dve.wait_ge(s["cleared"].sem, 3)
                norm_vector(dve, g, ln, 0)
                queries_in(0)
                each_turn(dve, NB, turn)

            @block.gpsimd
            def _(pool):
                def turn(t, nxt):
                    for b in range(B):
                        pool.wait_ge(low_ready.sem, low_ready.at(t, b + 1))
                        if b >= 1:
                            pool.wait_ge(exped.sem, exped.at(t, b))
                        pool.tensor_tensor(moved[:, :, :], masked[:, b % 2, :, :], low[:, :].unsqueeze(2).broadcast_to([P, U, KEYS]),
                                           ALU.add).then_inc(moved_ready.sem, 1)
                        if nxt is not None and b == 0:
                            norm_pool(pool, ln, nxt)

                norm_pool_setup(pool, ln)
                norm_pool(pool, ln, 0)
                each_turn(pool, NB, turn)

            @block.scalar
            def _(act):
                def x_in(t):
                    act.wait_ge(s["xT_ps"].sem, s["xT_ps"].at(t, 1))
                    act.copy(xT[:, 2:ROWS - 1, 1:WIN], turned[:, 1:1 + 16 * 15].rearrange("p (r k) -> p r k", k=16))
                    act.copy(xT[:, ROWS - 1, 1:WIN - 1], turned[:, 241:S])
                    act.copy(xT[:, :, 0], turned[:, 0:1].broadcast_to([P, ROWS])).then_inc(s["xT_ready"].sem, 1)

                def queries_in(t, ws):
                    for w in ws:
                        act.wait_ge(q_ps.sem, q_ps.at(t, w + 1))
                        act.copy(*query_block(2 * w, 0))
                        act.copy(*query_block(2 * w, 1)).then_inc(q_act.sem, 1)

                def keys_in(t):
                    for gp in range(G):
                        act.wait_ge(k_ps.sem, k_ps.at(t, gp + 1))
                        act.copy(k[:, gp, :], v_b[gp % 2][:, 0:ROWS * WIN]).then_inc(k_ready.sem, 1)

                def first_in(t):
                    act.wait_ge(s["first_ps"].sem, s["first_ps"].at(t, 1))
                    act.copy(oT[:, :, 0], turned[:, 0:G]).then_inc(s["first_ready"].sem, 1)

                def values_in(t, b):
                    act.wait_ge(v_ps.sem, v_ps.at(t, b + 1))
                    if b >= 2:
                        act.wait_ge(pv_ps.sem, pv_ps.at(t, b - 1))
                    act.copy(v[:, b % 2, 512:1024], v_b[1][0:BK, :]).then_inc(v_act.sem, 1)

                def turn(t, nxt):
                    values_in(t, 0)
                    for b in range(B):
                        act.wait_ge(moved_ready.sem, moved_ready.at(t, b + 1))
                        if b >= 1:
                            act.wait_ge(prob_ready.sem, prob_ready.at(t, b))
                        act.activation(ex[:, :, :], moved[:, :, :], ACT.Exp).then_inc(exped.sem, 1)
                        if b + 1 < B:
                            values_in(t, b + 1)
                        if nxt is not None and b == 2:
                            x_in(nxt)
                        if nxt is not None and b == 3:
                            queries_in(nxt, (0, 1))
                        for half in range(2):
                            act.wait_ge(mix_ps.sem, mix_ps.at(t, 2 * b + half + 1))
                            if b >= 1 and half == 0:
                                act.wait_ge(pv_ps.sem, pv_ps.at(t, b))
                            act.copy(mixed[:, :, 4 * half:4 * half + 4, :].rearrange("p g u i -> p u g i"),
                                     mix_b[half][0:BK, :].rearrange("p (u g i) -> p u g i", u=4, i=8)).then_inc(mixed_ready.sem, 1)
                        if nxt is not None and b == 3:
                            queries_in(nxt, (2, 3))
                        act.wait_ge(pv_ps.sem, pv_ps.at(t, b + 1))
                        act.copy(oT[:, :, 1 + 64 * b:65 + 64 * b], pv_b[b % 2][:, :].rearrange("p (g i) -> p g i", g=G)).then_inc(oT_ready.sem, 1)
                    if nxt is not None:
                        keys_in(nxt)
                        first_in(nxt)

                act.wait_ge(s["cleared"].sem, 3)
                x_in(0)
                queries_in(0, range(G // 2))
                keys_in(0)
                first_in(0)
                each_turn(act, NB, turn)

            @block.tensor
            def _(pe):
                wq, wk, wv = (g["wqkv1"][:, a * H * D:(a + 1) * H * D] for a in range(3))

                def queries(t, ws):
                    for w in ws:
                        if w >= 2:
                            pe.wait_ge(q_dve.sem, q_dve.at(t, w - 1))
                        for m in range(2):
                            gp = 2 * w + m
                            last = pe.matmul(v_b[w % 2][:, m * S:(m + 1) * S], wq[:, gp * P:(gp + 1) * P], xT[:, 2:ROWS, 1:WIN], start=True, stop=True)
                        last.then_inc(q_ps.sem, 1)

                def keys(t):
                    for gp in range(G):
                        if gp < 2:
                            pe.wait_ge(q_dve.sem, q_dve.at(t, G // 2 - 1 + gp))
                        else:
                            pe.wait_ge(k_ready.sem, k_ready.at(t, gp - 1))
                        pe.matmul(v_b[gp % 2][:, 0:ROWS * WIN], wk[:, gp * P:(gp + 1) * P], xT[:, :, :].rearrange("p r k -> p (r k)"),
                                  start=True, stop=True).then_inc(k_ps.sem, 1)

                def first_token(t):
                    for gp in range(G):
                        last = pe.matmul(turned[:, gp:gp + 1], wv[:, gp * P:(gp + 1) * P], xT[:, 0, 0:1], start=True, stop=True)
                    last.then_inc(s["first_ps"].sem, 1)

                def values_and_scores(t, b):
                    if b == 0:
                        pe.wait_ge(k_ready.sem, k_ready.at(t, G))
                    else:
                        pe.wait_ge(v_act.sem, v_act.at(t, b))
                        pe.wait_ge(v_dve.sem, v_dve.at(t, b))
                    for half in range(2):
                        last = pe.matmul(v_b[half][0:BK, :], xT[:, 4 * b:4 * b + 6, :].rearrange("p r k -> p (r k)"),
                                         wv[:, 512 * half:512 * half + 512], start=True, stop=True)
                    last.then_inc(v_ps.sem, 1)
                    if b >= 1:
                        pe.wait_ge(masked_ready.sem, masked_ready.at(t, b))
                    for u in range(U):
                        row = 4 * b + u // 2
                        for gp in range(G):
                            four = gp // 2
                            last = pe.matmul(score_b[32 * four:32 * four + 32, u * KEYS:(u + 1) * KEYS],
                                             q[:, gp, U * b + u, :, :].rearrange("p h i -> p (h i)"), k[:, gp, WIN * row:WIN * row + KEYS],
                                             start=(gp % 2 == 0), stop=(gp % 2 == 1))
                    last.then_inc(score_ps.sem, 1)

                def mixing(t, b):
                    pe.wait_ge(prob_ready.sem, prob_ready.at(t, b + 1))
                    for half in range(2):
                        if b >= 1:
                            pe.wait_ge(mixed_ready.sem, mixed_ready.at(t, 2 * b - 1 + half))
                        for u in range(4 * half, 4 * half + 4):
                            last = pe.matmul(mix_b[half][0:BK, (u % 4) * P:(u % 4 + 1) * P], prob[:, u * BK:(u + 1) * BK],
                                             g["mix"][:, :, :].rearrange("p g i -> p (g i)"), start=True, stop=True)
                        last.then_inc(mix_ps.sem, 1)

                def weigh_values(t, b):
                    pe.wait_ge(mixed_ready.sem, mixed_ready.at(t, 2 * b + 2))
                    pe.wait_ge(v_act.sem, v_act.at(t, b + 1))
                    pe.wait_ge(v_dve.sem, v_dve.at(t, b + 1))
                    if b >= 2:
                        pe.wait_ge(oT_ready.sem, oT_ready.at(t, b - 1))
                    for h in range(H):
                        last = pe.matmul(pv_b[b % 2][D * (h % 2):D * (h % 2) + D, (h // 2) * 64:(h // 2) * 64 + 64], v[:, b % 2, h * D:(h + 1) * D],
                                         mixed[:, h, :, :].rearrange("p u i -> p (u i)"), start=True, stop=True)
                    last.then_inc(pv_ps.sem, 1)

                def turn(t, nxt):
                    for b in range(B):
                        if b + 1 < B:
                            values_and_scores(t, b + 1)
                        if nxt is not None and b == 2:
                            turn_tokens(pe, g, ln, turned, s["xT_ps"], nxt)
                        if nxt is not None and b == 3:
                            pe.wait_ge(s["xT_ready"].sem, s["xT_ready"].at(nxt, 1))
                            pe.wait_ge(v_act.sem, v_act.at(t, B))
                            pe.wait_ge(v_dve.sem, v_dve.at(t, B))
                            queries(nxt, (0, 1))
                        mixing(t, b)
                        if nxt is not None and b == 3:
                            queries(nxt, (2, 3))
                        weigh_values(t, b)
                    if nxt is not None:
                        keys(nxt)
                    pe.wait_ge(oT_ready.sem, oT_ready.at(t, B))
                    pe.wait_ge(s["first_ready"].sem, s["first_ready"].at(t, 1))
                    for n in range(N):
                        dst = out_ps[:, n * P:(n + 1) * P]
                        for gp in range(G):
                            pe.matmul(dst, oT[:, gp, n * P:(n + 1) * P], g["wout1"][:, gp, :], start=(gp == 0), stop=False)
                        last = add_bias(pe, g, dst, B_O1, True)
                    last.then_inc(s["out_ps"].sem, 1)
                    if nxt is not None:
                        first_token(nxt)
                        values_and_scores(nxt, 0)

                pe.wait_ge(s["cleared"].sem, 3)
                turn_tokens(pe, g, ln, turned, s["xT_ps"], 0)
                pe.wait_ge(s["xT_ready"].sem, s["xT_ready"].at(0, 1))
                queries(0, range(G // 2))
                keys(0)
                first_token(0)
                values_and_scores(0, 0)
                each_turn(pe, NB, turn)


_INS = ['L0_attn_x', 'L0_attn_Wq', 'L0_attn_bq', 'L0_attn_Wk', 'L0_attn_bk', 'L0_attn_Wv', 'L0_attn_bv', 'L0_attn_Wo',
        'L0_attn_bo', 'L0_attn_Er', 'L0_ffn_weights', 'L0_ffn_scale', 'L0_ffn_bias', 'L1_attn_w_qkv', 'L1_attn_w_out',
        'L1_attn_b_out', 'L1_attn_w_th', 'L1_ffn_gate_w', 'L1_ffn_expert_w', 'L2_attn_W_qkv', 'L2_ffn_Wr', 'L2_ffn_Wg',
        'L2_ffn_Wu', 'L2_ffn_Wd', 'L2_ffn_Sg', 'L2_ffn_Su', 'L2_ffn_Sd', 'L3_attn_w_qkv', 'L3_attn_b_qkv',
        'L3_attn_w_out', 'L3_attn_b_out', 'L3_ffn_w_gate', 'L3_ffn_w_up', 'L3_ffn_w_down']


def kernel(**inputs):
    import numpy as _np
    import concourse.bacc as _bacc
    from concourse import mybir as _mybir
    from concourse.bass_utils import run_bass_kernel_spmd as _run

    nc = _bacc.Bacc("TRN2", target_bir_lowering=False, num_devices=1)
    arrays, aps = {}, {}
    for name in _INS + ["const"]:
        a = CONST if name == "const" else _np.ascontiguousarray(inputs[name])
        arrays[f"in_{name}_dram"] = a
        aps[name] = nc.dram_tensor(f"in_{name}_dram", a.shape, _mybir.dt.from_np(a.dtype), kind="ExternalInput").ap()
    shape = tuple(inputs["L0_attn_x"].shape)
    out = nc.dram_tensor("out_0_dram", shape, F32, kind="ExternalOutput").ap()
    network(nc, aps, out)
    r = _run(nc, [arrays], core_ids=[0])
    return r.results[0]["out_0_dram"]
```
